# Optimizing a Trainium2 kernel written in Bass

```python
import numpy as np
import jax
import jax.numpy as jnp

def _softmax(x, axis=-1):
    return jax.nn.softmax(x, axis=axis)

def _gelu(x):
    return jax.nn.gelu(x, approximate=True)

def _silu(x):
    return jax.nn.silu(x)

def _sigmoid(x):
    return jax.nn.sigmoid(x)

def _layernorm(x, axis=-1, eps=1e-05):
    m = jnp.mean(x, axis=axis, keepdims=True)
    v = jnp.var(x, axis=axis, keepdims=True)
    return (x - m) / jnp.sqrt(v + eps)

def _scatter_add(tgt, idx, src, axis=0):
    return tgt.at[idx].add(src)

def _segment_sum(src, seg, n):
    return jax.ops.segment_sum(src, seg, n)
kernel_name = 'mk_xattn_ffn_d4_seqx_r8_cfc148'

def setup_inputs(seed: int=0):
    np.random.seed(seed)
    _w = jnp.asarray

    def _rec_inputs():
        import jax
        import jax.numpy as jnp
        _rk = jax.random.key(seed)
        x = 7.22e-05 + 1 * jax.random.normal(jax.random.fold_in(_rk, 1), (8, 128, 512), jnp.float32)
        _lenS = 128 - jax.random.randint(jax.random.fold_in(_rk, 7), (8,), 0, max(1, 128 // 4) + 1, jnp.int32)
        _lenS2 = 128 - jax.random.randint(jax.random.fold_in(_rk, 8), (8,), 0, max(1, 128 // 4) + 1, jnp.int32)
        _ctx_4096P = jax.random.normal(jax.random.fold_in(_rk, 11), (8, 16, 512), jnp.float32)
        _ctx_4096c = jax.random.dirichlet(jax.random.fold_in(_rk, 511), 0.3 * jnp.ones((16,), jnp.float32), (8, 128))
        _ctx_4096t = jnp.einsum('bsk,bkd->bsd', _ctx_4096c, _ctx_4096P)
        _ctx_4096t = _ctx_4096t * jax.lax.rsqrt(jnp.mean(jnp.square(_ctx_4096t)) + 1e-12) * 0.953939
        ctx_4096 = 4.13588e-05 + 0.999923 * (_ctx_4096t + 0.3 * jax.random.normal(jax.random.fold_in(_rk, 611), (8, 128, 512), jnp.float32))
        _validS = jnp.arange(128)[None, :] < _lenS[:, None]
        _validS2 = jnp.arange(128)[None, :] < _lenS2[:, None]
        _causal = jnp.tril(jnp.ones((128, 128), dtype=bool))
        mask_BxSxS2_bk0 = jnp.logical_not(jnp.broadcast_to(_validS2[:, None, :], (8, 128, 128)))
        mask_BxSxS2_ff0 = jnp.where(jnp.ones((8, 128, 128), dtype=bool), 0.0, -1000000000.0).astype(jnp.float32)
        return (x, ctx_4096, mask_BxSxS2_bk0, mask_BxSxS2_ff0)
    x, ctx_4096, mask_BxSxS2_bk0, mask_BxSxS2_ff0 = _rec_inputs()

    def _L0_xattn_setup():
        import jax, jax.numpy as jnp
        import numpy as np
        B, LQ, LK, D, H, DH = (2, 128, 128, 512, 32, 128)
        EPS = 1e-05

        def _rmsnorm(x, weight):
            var = jnp.mean(jnp.square(x), axis=-1, keepdims=True)
            return x * jax.lax.rsqrt(var + EPS) * weight
        key = jax.random.key(seed)
        ks = jax.random.split(key, 8)
        scale = 0.02
        return {'hidden_states': jax.random.normal(ks[0], (B, LQ, D), jnp.float32), 'key_value_states': jax.random.normal(ks[1], (B, LK, D), jnp.float32), 'attention_mask': jax.random.randint(ks[2], (B, LQ, LK), 0, 2) > 0, 'position_bias': jax.random.normal(ks[3], (H, LQ, LK), jnp.float32), 'ln_weight': jnp.ones((D,), jnp.float32), 'w_q': jax.random.normal(ks[4], (H * DH, D), jnp.float32) * scale, 'w_k': jax.random.normal(ks[5], (H * DH, D), jnp.float32) * scale, 'w_v': jax.random.normal(ks[6], (H * DH, D), jnp.float32) * scale, 'w_out': jax.random.normal(ks[7], (D, H * DH), jnp.float32) * scale}
    _L0_xattn_all = _L0_xattn_setup()
    _L0_xattn_in = {k: v for k, v in _L0_xattn_all.items() if k in ('position_bias', 'ln_weight', 'w_q', 'w_k', 'w_v', 'w_out')}
    del _L0_xattn_all

    def _L0_ffn_setup():
        import jax, jax.numpy as jnp
        import numpy as np
        import math
        B, S, IN, OUT = (4, 256, 512, 512)
        E, R, K = (8, 64, 128)
        SCALE = 64.0 / 64.0
        MULTIPLIER = 1.0
        key = jax.random.key(seed)
        ks = jax.random.split(key, 6)
        return {'x': jax.random.normal(ks[0], (B, S, IN), jnp.float32), 'W_org': jax.random.normal(ks[1], (OUT, IN), jnp.float32) * 0.02, 'lora_down': jax.random.normal(ks[2], (E, IN, R), jnp.float32) * 0.02, 'lora_up': jax.random.normal(ks[3], (E, R, OUT), jnp.float32) * 0.02, 'lora_keys': jax.random.normal(ks[4], (E, K), jnp.float32), 'Wq': jax.random.normal(ks[5], (K, IN), jnp.float32) * 0.02}
    _L0_ffn_all = _L0_ffn_setup()
    _L0_ffn_in = {k: v for k, v in _L0_ffn_all.items() if k in ('W_org', 'lora_down', 'lora_up', 'lora_keys', 'Wq')}
    del _L0_ffn_all

    def _L1_xattn_setup():
        import jax, jax.numpy as jnp
        import numpy as np
        EMBED = 512
        HEADS = 32
        GROUP = 4
        KV_HEADS = HEADS // GROUP
        HEAD_DIM = EMBED // HEADS
        B, S = (2, 256)
        key = jax.random.key(seed)
        ks = jax.random.split(key, 7)
        scale = 0.02
        return {'queries': jax.random.normal(ks[0], (B, S, EMBED), dtype=jnp.float32), 'keys': jax.random.normal(ks[1], (B, S, EMBED), dtype=jnp.float32), 'values': jax.random.normal(ks[2], (B, S, EMBED), dtype=jnp.float32), 'Wq': jax.random.normal(ks[3], (EMBED, EMBED), dtype=jnp.float32) * scale, 'Wk': jax.random.normal(ks[4], (EMBED, KV_HEADS * HEAD_DIM), dtype=jnp.float32) * scale, 'Wv': jax.random.normal(ks[5], (EMBED, KV_HEADS * HEAD_DIM), dtype=jnp.float32) * scale, 'Wo': jax.random.normal(ks[6], (EMBED, EMBED), dtype=jnp.float32) * scale}
    _L1_xattn_all = _L1_xattn_setup()
    _L1_xattn_in = {k: v for k, v in _L1_xattn_all.items() if k in ('Wq', 'Wk', 'Wv', 'Wo')}
    del _L1_xattn_all

    def _L1_ffn_setup():
        import jax, jax.numpy as jnp
        import numpy as np
        HID, BOT, RDIM, NSLOT, K, VB = (512, 64, 48, 128, 8, 32)
        TAU_LOW, TAU_HIGH, EARLY_EXIT = (0.5, 2.0, 0.05)

        def _uncertainty(h, Wu1, bu1, Wu2, bu2):
            var = jnp.var(h, axis=-1)
            log_var = jnp.log1p(var)
            norm_var = log_var / (jnp.mean(log_var) + 1e-06)
            learned = (jax.nn.gelu(h @ Wu1.T + bu1) @ Wu2.T + bu2)[..., 0]
            return jnp.clip(norm_var * 0.5 + jax.nn.sigmoid(learned) * 2.5, 0.0, 5.0)
        key = jax.random.key(seed)
        ks = jax.random.split(key, 12)
        B, S = (2, 256)
        return {'hidden_states': jax.random.normal(ks[0], (B, S, HID), dtype=jnp.float32), 'Wq': jax.random.normal(ks[1], (BOT, HID), dtype=jnp.float32) / np.sqrt(HID), 'Wr': jax.random.normal(ks[2], (RDIM, BOT), dtype=jnp.float32) / np.sqrt(BOT), 'aux_keys': jax.random.normal(ks[3], (NSLOT, BOT), dtype=jnp.float32) * 0.01, 'aux_values': jax.random.normal(ks[4], (NSLOT, HID), dtype=jnp.float32) * 0.02, 'Wvd': jax.random.normal(ks[5], (VB, HID), dtype=jnp.float32) * 0.1 / np.sqrt(HID), 'Wvu': jax.random.normal(ks[6], (HID, VB), dtype=jnp.float32) * 0.1 / np.sqrt(VB), 'Wu1': jax.random.normal(ks[7], (HID // 4, HID), dtype=jnp.float32) / np.sqrt(HID), 'bu1': jnp.zeros((HID // 4,), dtype=jnp.float32), 'Wu2': jax.random.normal(ks[8], (1, HID // 4), dtype=jnp.float32) * 0.01, 'bu2': jnp.zeros((1,), dtype=jnp.float32), 'gate_w1': jnp.float32(0.5), 'gate_bias': jnp.float32(-1.0), 'log_rel': jnp.zeros((NSLOT,), dtype=jnp.float32)}
    _L1_ffn_all = _L1_ffn_setup()
    _L1_ffn_in = {k: v for k, v in _L1_ffn_all.items() if k in ('Wq', 'Wr', 'aux_keys', 'aux_values', 'Wvd', 'Wvu', 'Wu1', 'bu1', 'Wu2', 'bu2', 'gate_w1', 'gate_bias', 'log_rel')}
    del _L1_ffn_all

    def _L2_xattn_setup():
        import jax, jax.numpy as jnp
        import numpy as np
        import math
        EPS = 1e-05
        LAMBDA = 0.6

        def _crucial_k(C):
            f = math.floor(LAMBDA * C)
            return f + f % 2

        def _conv1d(y, w):
            return jax.lax.conv_general_dilated(y, w, window_strides=(1,), padding=((3, 3),), dimension_numbers=('NCH', 'OIH', 'NCH'))

        def _norm_active(z, gamma, beta):
            mu = jnp.mean(z, axis=(0, 2), keepdims=True)
            var = jnp.mean((z - mu) ** 2, axis=(0, 2), keepdims=True)
            zn = (z - mu) * jax.lax.rsqrt(var + EPS)
            zn = zn * gamma.reshape(1, -1, 1) + beta.reshape(1, -1, 1)
            return jax.nn.sigmoid(jax.nn.relu(zn))
        key = jax.random.key(seed)
        k1, k2, k3 = jax.random.split(key, 3)
        B, C, L = (32, 32, 512)
        x = jax.random.normal(k1, (B, C, L), dtype=jnp.float32)
        channel_map = jax.random.normal(k2, (B, C, L), dtype=jnp.float32)
        fan_in = 2 * 7
        bound = 1.0 / math.sqrt(fan_in)
        conv_w = jax.random.uniform(k3, (1, 2, 7), jnp.float32, -bound, bound)
        bn_gamma = jnp.ones((1,), jnp.float32)
        bn_beta = jnp.zeros((1,), jnp.float32)
        return {'x': x, 'channel_map': channel_map, 'conv_w': conv_w, 'bn_gamma': bn_gamma, 'bn_beta': bn_beta}
    _L2_xattn_all = _L2_xattn_setup()
    _L2_xattn_in = {k: v for k, v in _L2_xattn_all.items() if k in ('conv_w', 'bn_gamma', 'bn_beta')}
    del _L2_xattn_all

    def _L2_ffn_setup():
        import jax, jax.numpy as jnp
        import numpy as np
        B, S, D, O, E, R = (2, 512, 512, 512, 8, 16)
        TOP_K = 2
        SCALING = 32.0 / 16.0
        key = jax.random.key(seed)
        k = jax.random.split(key, 6)
        x = jax.random.normal(k[0], (B, S, D), dtype=jnp.float32)
        W_base = jax.random.normal(k[1], (O, D), dtype=jnp.float32) * 0.02
        b_base = jax.random.normal(k[2], (O,), dtype=jnp.float32) * 0.02
        W_router = jax.random.normal(k[3], (E, D), dtype=jnp.float32) * 0.01
        lora_A = jax.random.normal(k[4], (E, R, D), dtype=jnp.float32) * (1.0 / np.sqrt(D))
        lora_B = jax.random.normal(k[5], (E, O, R), dtype=jnp.float32) * 0.02
        return {'x': x, 'W_base': W_base, 'b_base': b_base, 'W_router': W_router, 'lora_A': lora_A, 'lora_B': lora_B}
    _L2_ffn_all = _L2_ffn_setup()
    _L2_ffn_in = {k: v for k, v in _L2_ffn_all.items() if k in ('W_base', 'b_base', 'W_router', 'lora_A', 'lora_B')}
    del _L2_ffn_all

    def _L3_xattn_setup():
        import jax, jax.numpy as jnp
        import numpy as np
        BS, SEQ, D_MODEL = (4, 128, 512)
        N_Q_HEADS, N_KV_HEADS, D_K, D_V = (32, 8, 128, 128)
        ROPE_BASE = 10000.0

        def _rotate_half(x):
            x1, x2 = jnp.split(x, 2, axis=-1)
            return jnp.concatenate([-x2, x1], axis=-1)

        def _apply_rope(x, pos0):
            d = x.shape[-1]
            seq = x.shape[2]
            inv_freq = 1.0 / ROPE_BASE ** (jnp.arange(0, d, 2, dtype=jnp.float32) / d)
            pos = (pos0 + jnp.arange(seq)).astype(jnp.float32)
            ang = pos[:, None] * inv_freq[None, :]
            cos = jnp.concatenate([jnp.cos(ang), jnp.cos(ang)], axis=-1)
            sin = jnp.concatenate([jnp.sin(ang), jnp.sin(ang)], axis=-1)
            return x * cos[None, None] + _rotate_half(x) * sin[None, None]
        key = jax.random.key(seed)
        ks = jax.random.split(key, 8)
        w_scale = 0.02
        return {'query': jax.random.normal(ks[0], (BS, SEQ, D_MODEL), dtype=jnp.float32), 'key': jax.random.normal(ks[1], (BS, SEQ, D_MODEL), dtype=jnp.float32), 'value': jax.random.normal(ks[2], (BS, SEQ, D_MODEL), dtype=jnp.float32), 'mask': jnp.zeros((BS, SEQ, SEQ), dtype=jnp.float32), 'wq': jax.random.normal(ks[3], (D_MODEL, N_Q_HEADS * D_K), dtype=jnp.float32) * w_scale, 'wk': jax.random.normal(ks[4], (D_MODEL, N_KV_HEADS * D_K), dtype=jnp.float32) * w_scale, 'wv': jax.random.normal(ks[5], (D_MODEL, N_KV_HEADS * D_V), dtype=jnp.float32) * w_scale, 'wo': jax.random.normal(ks[6], (N_Q_HEADS * D_V, D_MODEL), dtype=jnp.float32) * w_scale, 'curr_seq_pos': 0}
    _L3_xattn_all = _L3_xattn_setup()
    _L3_xattn_in = {k: v for k, v in _L3_xattn_all.items() if k in ('wq', 'wk', 'wv', 'wo')}
    del _L3_xattn_all

    def _L3_ffn_setup():
        import jax, jax.numpy as jnp
        import numpy as np
        R = 16
        LORA_ALPHA = 16
        SCALING = LORA_ALPHA / R
        key = jax.random.key(seed)
        kx, kr, ka = jax.random.split(key, 3)
        B, S, D, DO, E = (4, 256, 512, 512, 8)
        x = jax.random.normal(kx, (B, S, D), dtype=jnp.float32)
        bound_r = 1.0 / np.sqrt(D)
        route_w = jax.random.uniform(kr, (E, D), jnp.float32, -bound_r, bound_r)
        bound_a = 1.0 / np.sqrt(D)
        A = jax.random.uniform(ka, (E, R, D), jnp.float32, -bound_a, bound_a)
        kb = jax.random.fold_in(key, 7)
        Bw = jax.random.normal(kb, (E, DO, R), dtype=jnp.float32) * 0.02
        return {'x': x, 'route_w': route_w, 'A': A, 'Bw': Bw}
    _L3_ffn_all = _L3_ffn_setup()
    _L3_ffn_in = {k: v for k, v in _L3_ffn_all.items() if k in ('route_w', 'A', 'Bw')}
    del _L3_ffn_all
    return {'x': x, 'ctx_4096': ctx_4096, 'mask_BxSxS2_bk0': mask_BxSxS2_bk0, 'mask_BxSxS2_ff0': mask_BxSxS2_ff0, 'L0_xattn_position_bias': _L0_xattn_in['position_bias'], 'L0_xattn_ln_weight': _L0_xattn_in['ln_weight'], 'L0_xattn_w_q': _L0_xattn_in['w_q'], 'L0_xattn_w_k': _L0_xattn_in['w_k'], 'L0_xattn_w_v': _L0_xattn_in['w_v'], 'L0_xattn_w_out': _L0_xattn_in['w_out'], 'L0_ffn_W_org': _L0_ffn_in['W_org'], 'L0_ffn_lora_down': _L0_ffn_in['lora_down'], 'L0_ffn_lora_up': _L0_ffn_in['lora_up'], 'L0_ffn_lora_keys': _L0_ffn_in['lora_keys'], 'L0_ffn_Wq': _L0_ffn_in['Wq'], 'L1_xattn_Wq': _L1_xattn_in['Wq'], 'L1_xattn_Wk': _L1_xattn_in['Wk'], 'L1_xattn_Wv': _L1_xattn_in['Wv'], 'L1_xattn_Wo': _L1_xattn_in['Wo'], 'L1_ffn_Wq': _L1_ffn_in['Wq'], 'L1_ffn_Wr': _L1_ffn_in['Wr'], 'L1_ffn_aux_keys': _L1_ffn_in['aux_keys'], 'L1_ffn_aux_values': _L1_ffn_in['aux_values'], 'L1_ffn_Wvd': _L1_ffn_in['Wvd'], 'L1_ffn_Wvu': _L1_ffn_in['Wvu'], 'L1_ffn_Wu1': _L1_ffn_in['Wu1'], 'L1_ffn_bu1': _L1_ffn_in['bu1'], 'L1_ffn_Wu2': _L1_ffn_in['Wu2'], 'L1_ffn_bu2': _L1_ffn_in['bu2'], 'L1_ffn_gate_w1': _L1_ffn_in['gate_w1'], 'L1_ffn_gate_bias': _L1_ffn_in['gate_bias'], 'L1_ffn_log_rel': _L1_ffn_in['log_rel'], 'L2_xattn_conv_w': _L2_xattn_in['conv_w'], 'L2_xattn_bn_gamma': _L2_xattn_in['bn_gamma'], 'L2_xattn_bn_beta': _L2_xattn_in['bn_beta'], 'L2_ffn_W_base': _L2_ffn_in['W_base'], 'L2_ffn_b_base': _L2_ffn_in['b_base'], 'L2_ffn_W_router': _L2_ffn_in['W_router'], 'L2_ffn_lora_A': _L2_ffn_in['lora_A'], 'L2_ffn_lora_B': _L2_ffn_in['lora_B'], 'L3_xattn_wq': _L3_xattn_in['wq'], 'L3_xattn_wk': _L3_xattn_in['wk'], 'L3_xattn_wv': _L3_xattn_in['wv'], 'L3_xattn_wo': _L3_xattn_in['wo'], 'L3_ffn_route_w': _L3_ffn_in['route_w'], 'L3_ffn_A': _L3_ffn_in['A'], 'L3_ffn_Bw': _L3_ffn_in['Bw']}

def reference(x, ctx_4096, mask_BxSxS2_bk0, mask_BxSxS2_ff0, L0_xattn_position_bias, L0_xattn_ln_weight, L0_xattn_w_q, L0_xattn_w_k, L0_xattn_w_v, L0_xattn_w_out, L0_ffn_W_org, L0_ffn_lora_down, L0_ffn_lora_up, L0_ffn_lora_keys, L0_ffn_Wq, L1_xattn_Wq, L1_xattn_Wk, L1_xattn_Wv, L1_xattn_Wo, L1_ffn_Wq, L1_ffn_Wr, L1_ffn_aux_keys, L1_ffn_aux_values, L1_ffn_Wvd, L1_ffn_Wvu, L1_ffn_Wu1, L1_ffn_bu1, L1_ffn_Wu2, L1_ffn_bu2, L1_ffn_gate_w1, L1_ffn_gate_bias, L1_ffn_log_rel, L2_xattn_conv_w, L2_xattn_bn_gamma, L2_xattn_bn_beta, L2_ffn_W_base, L2_ffn_b_base, L2_ffn_W_router, L2_ffn_lora_A, L2_ffn_lora_B, L3_xattn_wq, L3_xattn_wk, L3_xattn_wv, L3_xattn_wo, L3_ffn_route_w, L3_ffn_A, L3_ffn_Bw):
    import jax
    import jax.numpy as jnp

    def _L0_xattn_ref(hidden_states, key_value_states, attention_mask, position_bias, ln_weight, w_q, w_k, w_v, w_out):
        import jax, jax.numpy as jnp
        import numpy as np
        B, LQ, LK, D, H, DH = (2, 128, 128, 512, 32, 128)
        EPS = 1e-05

        def _rmsnorm(x, weight):
            var = jnp.mean(jnp.square(x), axis=-1, keepdims=True)
            return x * jax.lax.rsqrt(var + EPS) * weight
        x = _rmsnorm(hidden_states, ln_weight)
        b, lq, _ = x.shape
        lk = key_value_states.shape[1]
        h_q = (x @ w_q.T).reshape(b, lq, H, DH)
        h_k = (key_value_states @ w_k.T).reshape(b, lk, H, DH)
        h_v = (key_value_states @ w_v.T).reshape(b, lk, H, DH)
        score = jnp.einsum('bqhd,bkhd->bhqk', h_q, h_k)
        score = score + position_bias[None]
        m = attention_mask[:, None]
        score = jnp.where(m, score, -jnp.inf)
        score = jax.nn.softmax(score, axis=-1)
        score = jnp.where(m, score, 0.0)
        attn = jnp.einsum('bhqk,bkhd->bqhd', score, h_v).reshape(b, lq, H * DH)
        out = attn @ w_out.T
        return hidden_states + out

    def _L0_ffn_ref(x, W_org, lora_down, lora_up, lora_keys, Wq):
        import jax, jax.numpy as jnp
        import numpy as np
        import math
        B, S, IN, OUT = (4, 256, 512, 512)
        E, R, K = (8, 64, 128)
        SCALE = 64.0 / 64.0
        MULTIPLIER = 1.0
        base = jnp.einsum('bsi,oi->bso', x, W_org)
        q = jnp.einsum('bi,ki->bk', x.mean(axis=1), Wq)
        scores = jnp.einsum('bk,ek->be', q, lora_keys) / math.sqrt(K)
        coeffs = jax.nn.softmax(scores, axis=-1)
        h = jnp.einsum('bsi,eir->bser', x, lora_down)
        delta = jnp.einsum('be,bser,ero->bso', coeffs, h, lora_up)
        return base + delta * (SCALE * MULTIPLIER)

    def _L1_xattn_ref(queries, keys, values, Wq, Wk, Wv, Wo):
        import jax, jax.numpy as jnp
        import numpy as np
        EMBED = 512
        HEADS = 32
        GROUP = 4
        KV_HEADS = HEADS // GROUP
        HEAD_DIM = EMBED // HEADS
        B, S = (2, 256)
        b, s, _ = queries.shape
        q = (queries @ Wq).reshape(b, s, KV_HEADS, GROUP, HEAD_DIM)
        k = (keys @ Wk).reshape(b, s, KV_HEADS, HEAD_DIM)
        v = (values @ Wv).reshape(b, s, KV_HEADS, HEAD_DIM)
        scale = 1.0 / jnp.sqrt(jnp.asarray(HEAD_DIM, dtype=q.dtype))
        scores = jnp.einsum('bqhgd,bkhd->bhgqk', q, k) * scale
        attn = jax.nn.softmax(scores, axis=-1)
        out = jnp.einsum('bhgqk,bkhd->bqhgd', attn, v)
        out = out.reshape(b, s, EMBED)
        return out @ Wo

    def _L1_ffn_ref(hidden_states, Wq, Wr, aux_keys, aux_values, Wvd, Wvu, Wu1, bu1, Wu2, bu2, gate_w1, gate_bias, log_rel):
        import jax, jax.numpy as jnp
        import numpy as np
        HID, BOT, RDIM, NSLOT, K, VB = (512, 64, 48, 128, 8, 32)
        TAU_LOW, TAU_HIGH, EARLY_EXIT = (0.5, 2.0, 0.05)

        def _uncertainty(h, Wu1, bu1, Wu2, bu2):
            var = jnp.var(h, axis=-1)
            log_var = jnp.log1p(var)
            norm_var = log_var / (jnp.mean(log_var) + 1e-06)
            learned = (jax.nn.gelu(h @ Wu1.T + bu1) @ Wu2.T + bu2)[..., 0]
            return jnp.clip(norm_var * 0.5 + jax.nn.sigmoid(learned) * 2.5, 0.0, 5.0)
        query = hidden_states @ Wq.T
        rq = query @ Wr.T
        rk = aux_keys @ Wr.T
        router_scores = jnp.einsum('bsr,nr->bsn', rq, rk) / np.sqrt(RDIM) + log_rel
        top_scores, top_idx = jax.lax.top_k(router_scores, K)
        sel_keys = aux_keys[top_idx]
        attn = jnp.einsum('bsd,bskd->bsk', query, sel_keys) / np.sqrt(BOT) + log_rel[top_idx]
        w = jax.nn.softmax(attn, axis=-1)
        sel_vals = aux_values[top_idx]
        aux_out = jnp.einsum('bsk,bskh->bsh', w, sel_vals)
        aux_out = aux_out @ Wvd.T @ Wvu.T
        u = _uncertainty(hidden_states, Wu1, bu1, Wu2, bu2)
        u_norm = jnp.clip((u - TAU_LOW) / (TAU_HIGH - TAU_LOW), 0.0, 1.0)
        gate = jax.nn.sigmoid(gate_w1 * u_norm + gate_bias)
        gate = jnp.where(gate < EARLY_EXIT, 0.0, gate)
        return hidden_states + gate[..., None] * aux_out

    def _L2_xattn_ref(x, channel_map, conv_w, bn_gamma, bn_beta):
        import jax, jax.numpy as jnp
        import numpy as np
        import math
        EPS = 1e-05
        LAMBDA = 0.6

        def _crucial_k(C):
            f = math.floor(LAMBDA * C)
            return f + f % 2

        def _conv1d(y, w):
            return jax.lax.conv_general_dilated(y, w, window_strides=(1,), padding=((3, 3),), dimension_numbers=('NCH', 'OIH', 'NCH'))

        def _norm_active(z, gamma, beta):
            mu = jnp.mean(z, axis=(0, 2), keepdims=True)
            var = jnp.mean((z - mu) ** 2, axis=(0, 2), keepdims=True)
            zn = (z - mu) * jax.lax.rsqrt(var + EPS)
            zn = zn * gamma.reshape(1, -1, 1) + beta.reshape(1, -1, 1)
            return jax.nn.sigmoid(jax.nn.relu(zn))
        B, C, L = x.shape
        k = _crucial_k(C)
        cm = jnp.moveaxis(channel_map, 1, 2)
        _, topk_idx = jax.lax.top_k(cm, k)
        b_idx = jnp.arange(B)[:, None, None]
        l_idx = jnp.arange(L)[None, :, None]
        mask = jnp.zeros((B, L, C), x.dtype).at[b_idx, l_idx, topk_idx].set(1.0)
        crucial_channels = jnp.moveaxis(mask, 2, 1)
        subcrucial_channels = 1.0 - crucial_channels
        crucial_features = crucial_channels * x
        subcrucial_features = subcrucial_channels * x
        c_max = jnp.max(crucial_features, axis=1, keepdims=True)
        c_avg = jnp.mean(crucial_features, axis=1, keepdims=True) * (C / k)
        s_max = jnp.max(subcrucial_features, axis=1, keepdims=True)
        s_avg = jnp.mean(subcrucial_features, axis=1, keepdims=True) * (C / (C - k))
        crucial_x = jnp.concatenate([c_max, c_avg], axis=1)
        subcrucial_x = jnp.concatenate([s_max, s_avg], axis=1)
        A_S1 = _norm_active(_conv1d(crucial_x, conv_w), bn_gamma, bn_beta)
        A_S2 = _norm_active(_conv1d(subcrucial_x, conv_w), bn_gamma, bn_beta)
        return crucial_features * A_S1 + subcrucial_features * A_S2

    def _L2_ffn_ref(x, W_base, b_base, W_router, lora_A, lora_B):
        import jax, jax.numpy as jnp
        import numpy as np
        B, S, D, O, E, R = (2, 512, 512, 512, 8, 16)
        TOP_K = 2
        SCALING = 32.0 / 16.0
        d = x.shape[-1]
        n_experts = W_router.shape[0]
        xf = x.reshape(-1, d)
        logits = xf @ W_router.T
        probs = jax.nn.softmax(logits, axis=-1)
        topk_p, topk_i = jax.lax.top_k(probs, TOP_K)
        topk_p = topk_p / jnp.sum(topk_p, axis=-1, keepdims=True)
        w = jnp.sum(jax.nn.one_hot(topk_i, n_experts, dtype=xf.dtype) * topk_p[..., None], axis=1)
        h = jnp.einsum('td,erd->ter', xf, lora_A)
        lora_out = jnp.einsum('ter,eor,te->to', h, lora_B, w) * SCALING
        base = x @ W_base.T + b_base
        return base + lora_out.reshape(x.shape[:-1] + (W_base.shape[0],))

    def _L3_xattn_ref(query, key, value, mask, wq, wk, wv, wo, curr_seq_pos):
        import jax, jax.numpy as jnp
        import numpy as np
        BS, SEQ, D_MODEL = (4, 128, 512)
        N_Q_HEADS, N_KV_HEADS, D_K, D_V = (32, 8, 128, 128)
        ROPE_BASE = 10000.0

        def _rotate_half(x):
            x1, x2 = jnp.split(x, 2, axis=-1)
            return jnp.concatenate([-x2, x1], axis=-1)

        def _apply_rope(x, pos0):
            d = x.shape[-1]
            seq = x.shape[2]
            inv_freq = 1.0 / ROPE_BASE ** (jnp.arange(0, d, 2, dtype=jnp.float32) / d)
            pos = (pos0 + jnp.arange(seq)).astype(jnp.float32)
            ang = pos[:, None] * inv_freq[None, :]
            cos = jnp.concatenate([jnp.cos(ang), jnp.cos(ang)], axis=-1)
            sin = jnp.concatenate([jnp.sin(ang), jnp.sin(ang)], axis=-1)
            return x * cos[None, None] + _rotate_half(x) * sin[None, None]
        bs, sq, _ = query.shape
        n_groups = N_Q_HEADS // N_KV_HEADS
        q = (query @ wq).reshape(bs, sq, N_Q_HEADS, D_K).transpose((0, 2, 1, 3))
        sk = key.shape[1]
        k = (key @ wk).reshape(bs, sk, N_KV_HEADS, 1, D_K)
        k = jnp.repeat(k, n_groups, axis=3).reshape(bs, sk, N_Q_HEADS, D_K).transpose((0, 2, 1, 3))
        v = (value @ wv).reshape(bs, sk, N_KV_HEADS, 1, D_V)
        v = jnp.repeat(v, n_groups, axis=3).reshape(bs, sk, N_Q_HEADS, D_V).transpose((0, 2, 1, 3))
        scale = jnp.sqrt(jnp.float32(D_K))
        q = _apply_rope(q, curr_seq_pos)
        k = _apply_rope(k, curr_seq_pos)
        raw = jnp.einsum('bhqd,bhkd->bhqk', q, k) / scale
        masked = raw + mask[:bs, None, curr_seq_pos:curr_seq_pos + sq, :sk]
        attn = jax.nn.softmax(masked, axis=-1)
        out = jnp.einsum('bhqk,bhkd->bhqd', attn, v)
        out = out.transpose((0, 2, 1, 3)).reshape(bs, sq, N_Q_HEADS * D_V)
        return out @ wo

    def _L3_ffn_ref(x, route_w, A, Bw):
        import jax, jax.numpy as jnp
        import numpy as np
        R = 16
        LORA_ALPHA = 16
        SCALING = LORA_ALPHA / R
        logits = jnp.einsum('bsd,ed->bse', x, route_w)
        topk_v, topk_idx = jax.lax.top_k(logits, 1)
        E = logits.shape[-1]
        route_weight = jax.nn.one_hot(topk_idx[..., 0], E, dtype=logits.dtype) * topk_v
        h = jnp.einsum('bsd,erd->bser', x, A)
        wh = route_weight[..., None] * h
        out = jnp.einsum('bser,eor->bso', wh, Bw) * SCALING
        return out
    x = x + _L0_xattn_ref(_layernorm(x, axis=-1), ctx_4096, mask_BxSxS2_bk0, L0_xattn_position_bias, L0_xattn_ln_weight, L0_xattn_w_q, L0_xattn_w_k, L0_xattn_w_v, L0_xattn_w_out)
    x = x + _L0_ffn_ref(_layernorm(x, axis=-1), L0_ffn_W_org, L0_ffn_lora_down, L0_ffn_lora_up, L0_ffn_lora_keys, L0_ffn_Wq)
    x = x + _L1_xattn_ref(_layernorm(x, axis=-1), ctx_4096, ctx_4096, L1_xattn_Wq, L1_xattn_Wk, L1_xattn_Wv, L1_xattn_Wo)
    x = x + _L1_ffn_ref(_layernorm(x, axis=-1), L1_ffn_Wq, L1_ffn_Wr, L1_ffn_aux_keys, L1_ffn_aux_values, L1_ffn_Wvd, L1_ffn_Wvu, L1_ffn_Wu1, L1_ffn_bu1, L1_ffn_Wu2, L1_ffn_bu2, L1_ffn_gate_w1, L1_ffn_gate_bias, L1_ffn_log_rel)
    x = x + _L2_xattn_ref(_layernorm(x, axis=-1), ctx_4096, L2_xattn_conv_w, L2_xattn_bn_gamma, L2_xattn_bn_beta)
    x = x + _L2_ffn_ref(_layernorm(x, axis=-1), L2_ffn_W_base, L2_ffn_b_base, L2_ffn_W_router, L2_ffn_lora_A, L2_ffn_lora_B)
    x = x + _L3_xattn_ref(_layernorm(x, axis=-1), ctx_4096, ctx_4096, mask_BxSxS2_ff0, L3_xattn_wq, L3_xattn_wk, L3_xattn_wv, L3_xattn_wo, 0)
    x = x + _L3_ffn_ref(_layernorm(x, axis=-1), L3_ffn_route_w, L3_ffn_A, L3_ffn_Bw)
    return x

_drawn_inputs = setup_inputs


def setup_inputs(seed=0):
    import zlib

    import numpy as np

    out = dict(_drawn_inputs(seed))
    spreads = {'L0_xattn_ln_weight': (1.0, 0.2), 'L1_ffn_bu1': (0.0, 2.0), 'L1_ffn_log_rel': (0.0, 2.0)}
    factors = {'L0_ffn_lora_down': 4.697,
     'L0_ffn_lora_up': 4.704,
     'L0_ffn_lora_keys': 8.0,
     'L0_ffn_Wq': 8.0,
     'L1_xattn_Wq': 8.0,
     'L1_xattn_Wk': 8.0,
     'L1_ffn_Wq': 8.0,
     'L1_ffn_Wr': 27.506,
     'L1_ffn_aux_keys': 8.0,
     'L1_ffn_aux_values': 56.73,
     'L1_ffn_Wvd': 8.0,
     'L1_ffn_Wvu': 38.094,
     'L1_ffn_Wu1': 64.0,
     'L1_ffn_Wu2': 64.0,
     'L2_ffn_b_base': 8.0,
     'L3_xattn_wq': 8.0,
     'L3_xattn_wk': 8.0,
     'L3_ffn_route_w': 4.394,
     'L3_ffn_A': 3.49,
     'L3_ffn_Bw': 3.481}
    for name, (base, spread) in spreads.items():
        noise = np.random.default_rng([zlib.crc32(name.encode()), seed]).standard_normal(out[name].shape)
        drawn = base * np.exp(spread * noise) if base else spread * noise
        out[name] = jnp.asarray(drawn.astype(out[name].dtype))
    for name, factor in factors.items():
        out[name] = (out[name] * factor).astype(out[name].dtype)
    return out
```

```python
import numpy as np
import concourse.bass as bass
from concourse import mybir
from contextlib import ExitStack

F32 = mybir.dt.float32
F32R = mybir.dt.float32r
U8 = mybir.dt.uint8
ALU = mybir.AluOpType
ACT = mybir.ActivationFunctionType
AX = mybir.AxisListType

P = 128
B = 8
D = 512
DC = D // P
T = B * P
BH = B // 2
HALF = BH * P
EPS = 1e-5
MASKED = -1e30
FLOOR = -1e29


def wait(eng, sem, value):
    if not (isinstance(value, int) and value <= 0):
        eng.wait_ge(sem, value)


def product(pe, out, lhs, rhs, start, stop):
    if len(lhs) == 1:
        return pe.matmul(out, lhs[0], rhs[0], start=start, stop=stop)
    pe.matmul(out, lhs[0], rhs[0], start=start, stop=False)
    pe.matmul(out, lhs[0], rhs[1], start=False, stop=False)
    return pe.matmul(out, lhs[1], rhs[0], start=False, stop=stop)


def as_f32(ap):
    return ap.bitcast(F32)


class Core:

    def __init__(self, nc, ctx):
        self.nc, self.ctx = nc, ctx
        self.held = []
        self.x = self.sb(ctx, "x", [P, B, D])
        self.ident = self.sb(ctx, "ident", [P, P])
        self.neg_half = self.sb(ctx, "neg_half", [P, B])
        self.stats = self.sb(ctx, "stats", [P, B, 6])
        self.mv = self.sb(ctx, "mv", [P, B, 2])
        self.var_eps = self.sb(ctx, "var_eps", [P, B])
        self.rstd = self.sb(ctx, "rstd", [P, B])
        self.bank = [ctx.enter_context(nc.psum_tensor(f"bank{n}", [P, 512], F32)) for n in range(8)]
        self.x_loaded = self.sem("x_loaded")
        self.const_ready = self.sem("const_ready")
        self.stats_done = self.sem("stats_done")
        self.mv_done = self.sem("mv_done")
        self.var_done = self.sem("var_done")
        self.rstd_done = self.sem("rstd_done")
        self.xn_done = self.sem("xn_done")
        self.xt_full = self.sem("xt_full")
        self.xt_copied = self.sem("xt_copied")
        self.norms = 0
        self.held = []

    def sb(self, ctx, name, shape, dt=F32):
        return ctx.enter_context(self.nc.sbuf_tensor(name, shape, dt))

    def pair(self, ctx, name, shape):
        return (self.sb(ctx, name + "_hi", shape, F32R), self.sb(ctx, name + "_lo", shape, F32R))

    def sem(self, name):
        handle = self.nc.alloc_semaphore(name=name)
        self.held.append(handle)
        return handle

    def free_semaphores(self):
        self.nc.all_engine_barrier()
        self.nc.clear_and_free_semaphores(self.held)
        self.nc.all_engine_barrier()
        self.held = []


def norm_stage(core, xn, xt, loads):
    nc, n = core.nc, core.norms
    core.norms += 1
    with nc.Block() as block:

        @block.sync
        def _(sp):
            loads(sp)

        @block.vector
        def _(dve):
            for b in range(B):
                dve.bn_stats(core.stats[:, b, :], core.x[:, b, :]).then_inc(core.stats_done, 1)
            dve.wait_ge(core.stats_done, B * (n + 1))
            for b in range(B):
                dve.bn_aggr(core.mv[:, b, :], core.stats[:, b, :]).then_inc(core.mv_done, 1)
            dve.wait_ge(core.mv_done, B * (n + 1))
            dve.tensor_scalar_add(core.var_eps[:, :], core.mv[:, :, 1], EPS).then_inc(core.var_done, 1)
            dve.wait_ge(core.rstd_done, n + 1)
            for b in range(B):
                dve.tensor_scalar(xn[:, b, :], core.x[:, b, :], core.mv[:, b, 0:1], core.rstd[:, b:b + 1],
                                  ALU.subtract, ALU.mult).then_inc(core.xn_done, 1)
            for b in range(1, B, 2):
                dve.wait_ge(core.xt_full, B * n + b + 1)
                dve.tensor_copy(xt[:, :, b * P:(b + 1) * P], core.bank[b][:, :].rearrange("p (c t) -> p c t", c=DC)
                                ).then_inc(core.xt_copied, 1)

        @block.gpsimd
        def _(pool):
            pool.wait_ge(core.var_done, n + 1)
            pool.tensor_tensor(core.rstd[:, :], core.var_eps[:, :], core.neg_half[:, :], ALU.pow
                               ).then_inc(core.rstd_done, 1)

        @block.tensor
        def _(pe):
            for b in range(B):
                pe.wait_ge(core.xn_done, B * n + b + 1)
                for c in range(DC):
                    last = pe.transpose(core.bank[b][:, c * P:(c + 1) * P], xn[:, b, c * P:(c + 1) * P],
                                        core.ident[:, :])
                last.then_inc(core.xt_full, 1)

        @block.scalar
        def _(act):
            for b in range(0, B, 2):
                act.wait_ge(core.xt_full, B * n + b + 1)
                act.activation(xt[:, :, b * P:(b + 1) * P], core.bank[b][:, :].rearrange("p (c t) -> p c t", c=DC),
                               ACT.Copy).then_inc(core.xt_copied, 1)


L0_HEADS = 32
L0_PAIRS = L0_HEADS // 2


def l0_attention(core, dram):
    nc, x, bank = core.nc, core.x, core.bank
    with ExitStack() as ctx:
        sb = lambda name, shape, dt=F32: core.sb(ctx, "l0x_" + name, shape, dt)
        pair = lambda name, shape: core.pair(ctx, "l0x_" + name, shape)
        sem = lambda name: core.sem("l0x_" + name)

        qin = pair("qin", [P, DC, T])
        cin = pair("cin", [P, DC, T])
        w_qk = [pair("w_qk0", [P, 2, DC, P]), pair("w_qk1", [P, 2, DC, P])]
        w_v = pair("w_v", [P, DC, 2 * P])
        w_o = pair("w_o", [P, 2, D])

        with ExitStack() as ctx1:
            h = core.sb(ctx1, "l0x_h", [P, B, D])
            xr = core.sb(ctx1, "l0x_xr", [P, B, D])
            ctx_raw = core.sb(ctx1, "l0x_ctx_raw", [P, DC, T])
            lnw = core.sb(ctx1, "l0x_lnw", [P, DC])
            ms = core.sb(ctx1, "l0x_ms", [P, B])
            r2 = core.sb(ctx1, "l0x_r2", [P, B])
            ctx_loaded, lnw_loaded = sem("ctx_loaded"), sem("lnw_loaded")
            h_done, added = sem("h_done"), sem("added")
            ms1, ms2, r2_done = sem("ms1"), sem("ms2"), sem("r2_done")
            xt_hi, ctx_hi, ctx_lo = sem("xt_hi"), sem("ctx_hi"), sem("ctx_lo")
            cst = sem("cst")
            with nc.Block() as block:

                @block.sync
                def _(sp):
                    for b in range(B):
                        sp.dma_start(x[:, b, :], dram["x"][b, :, :]).then_inc(core.x_loaded, 16)
                    sp.dma_start(lnw[:, :], dram["L0_xattn_ln_weight"]).then_inc(lnw_loaded, 16)
                    sp.dma_start(ctx_raw[:, :, :], dram["ctx_t"]).then_inc(ctx_loaded, 16)

                @block.gpsimd
                def _(pool):
                    pool.memset(core.neg_half[:, :], -0.5).then_inc(core.const_ready, 1)
                    pool.memset(core.ident[:, :], 0.0).then_inc(cst, 1)
                    pool.wait_ge(cst, 1)
                    pool.affine_select(out=core.ident[:, :], in_=core.ident[:, :], compare_op=ALU.not_equal, fill=1.0,
                                       base=0, pattern=[[-1, P]], channel_multiplier=1).then_inc(core.const_ready, 1)
                    pool.wait_ge(core.const_ready, 2)
                    pool.wait_ge(core.var_done, 1)
                    pool.tensor_tensor(core.rstd[:, :], core.var_eps[:, :], core.neg_half[:, :], ALU.pow
                                       ).then_inc(core.rstd_done, 1)
                    pool.wait_ge(ms2, 1)
                    pool.tensor_tensor(r2[:, :], ms[:, :], core.neg_half[:, :], ALU.pow).then_inc(r2_done, 1)
                    for b in range(B):
                        pool.wait_ge(h_done, b + 1)
                        pool.tensor_tensor(x[:, b, :], x[:, b, :], h[:, b, :], ALU.add).then_inc(added, 1)
                    for c in range(DC):
                        pool.wait_ge(ctx_hi, c + 1)
                        pool.tensor_tensor(cin[1][:, c, :], ctx_raw[:, c, :], as_f32(cin[0][:, c, :]), ALU.subtract
                                           ).then_inc(ctx_lo, 1)

                @block.vector
                def _(dve):
                    for b in range(B):
                        dve.wait_ge(core.x_loaded, 16 * B)
                        dve.bn_stats(core.stats[:, b, :], x[:, b, :]).then_inc(core.stats_done, 1)
                    dve.wait_ge(core.stats_done, B)
                    for b in range(B):
                        dve.bn_aggr(core.mv[:, b, :], core.stats[:, b, :]).then_inc(core.mv_done, 1)
                    dve.wait_ge(core.mv_done, B)
                    dve.tensor_scalar_add(core.var_eps[:, :], core.mv[:, :, 1], EPS).then_inc(core.var_done, 1)
                    dve.wait_ge(core.rstd_done, 1)
                    dve.tensor_tensor(ms[:, :], core.mv[:, :, 1], core.rstd[:, :], ALU.mult).then_inc(ms1, 1)
                    for b in range(B):
                        dve.tensor_scalar(h[:, b, :], x[:, b, :], core.mv[:, b, 0:1], core.rstd[:, b:b + 1],
                                          ALU.subtract, ALU.mult).then_inc(h_done, 1)
                    dve.wait_ge(ms1, 1)
                    dve.tensor_tensor(ms[:, :], ms[:, :], core.rstd[:, :], ALU.mult).then_inc(ms1, 1)
                    dve.wait_ge(ms1, 2)
                    dve.tensor_scalar_add(ms[:, :], ms[:, :], EPS).then_inc(ms2, 1)
                    dve.wait_ge(r2_done, 1)
                    dve.wait_ge(h_done, B)
                    for b in range(B):
                        dve.tensor_scalar(xr[:, b, :], h[:, b, :], r2[:, b:b + 1], None, ALU.mult
                                          ).then_inc(core.xn_done, 1)
                    dve.wait_ge(lnw_loaded, 16)
                    for b in range(B):
                        dve.wait_ge(xt_hi, b + 1)
                        for c in range(DC):
                            last = dve.scalar_tensor_tensor(
                                qin[1][:, c, b * P:(b + 1) * P], bank[b][:, c * P:(c + 1) * P], lnw[:, c:c + 1],
                                as_f32(qin[0][:, c, b * P:(b + 1) * P]), ALU.mult, ALU.subtract)
                        last.then_inc(core.xt_copied, 1)

                @block.tensor
                def _(pe):
                    pe.wait_ge(core.const_ready, 2)
                    for b in range(B):
                        pe.wait_ge(core.xn_done, b + 1)
                        for c in range(DC):
                            last = pe.transpose(bank[b][:, c * P:(c + 1) * P], xr[:, b, c * P:(c + 1) * P],
                                                core.ident[:, :])
                        last.then_inc(core.xt_full, 1)

                @block.scalar
                def _(act):
                    act.wait_ge(lnw_loaded, 16)
                    for b in range(B):
                        act.wait_ge(core.xt_full, b + 1)
                        for c in range(DC):
                            last = act.activation(qin[0][:, c, b * P:(b + 1) * P], bank[b][:, c * P:(c + 1) * P],
                                                  ACT.Copy, scale=lnw[:, c:c + 1])
                        last.then_inc(xt_hi, 1)
                    act.wait_ge(ctx_loaded, 16)
                    for c in range(DC):
                        act.activation(cin[0][:, c, :], ctx_raw[:, c, :], ACT.Copy).then_inc(ctx_hi, 1)
            core.norms += 1

        raw_qk = [sb("raw_qk0", [P, 2, DC, P]), sb("raw_qk1", [P, 2, DC, P])]
        raw_v, raw_o = sb("raw_v", [P, DC, 2 * P]), sb("raw_o", [P, 2, D])
        q, k = pair("q", [P, T]), pair("k", [P, T])
        v = pair("v", [P, B, 2 * P])
        probs = sb("probs", [P, B, P])
        probs_t = pair("probs_t", [P, B, P])
        heads = pair("heads", [P, 2, T])
        bias = sb("bias", [P, 2, P])
        comb = sb("comb", [P, B, P])
        mask_u8 = sb("mask_u8", [P, B, P], U8)
        neg = sb("neg", [P, B, P])
        top, row_sum, inv_sum = sb("top", [P, B]), sb("row_sum", [P, B]), sb("inv_sum", [P, B])

        mask_loaded, neg_ready = sem("mask_loaded"), sem("neg_ready")
        bias_loaded = [sem("bias_loaded0"), sem("bias_loaded1")]
        comb_ready = sem("comb_ready")
        qk_loaded, qk_hi, qk_ready = ([sem(f"{s}{j}") for j in range(2)] for s in ("qk_loaded", "qk_hi", "qk_ready"))
        v_loaded, v_hi, v_ready = sem("v_loaded"), sem("v_hi"), sem("v_ready")
        o_loaded, o_hi, o_ready = sem("o_loaded"), sem("o_hi"), sem("o_ready")
        ring_full, ring_hi, ring_drained = sem("ring_full"), sem("ring_hi"), sem("ring_drained")
        scores_full, scores_read, top_raw, top_ready = (sem("scores_full"), sem("scores_read"), sem("top_raw"),
                                                        sem("top_ready"))
        exp_done, sum_ok, inv_done, probs_ready = sem("exp_done"), sem("sum_ok"), sem("inv_done"), sem("probs_ready")
        t_full, t_hi, t_drained = sem("t_full"), sem("t_hi"), sem("t_drained")
        h_full, h_hi, h_drained = sem("h_full"), sem("h_hi"), sem("h_drained")

        N = L0_PAIRS
        PER = 20

        def ring_at(i, what):
            if isinstance(i, int) and i == 0 and what == "qk0":
                return 0
            return PER * i - 8 + {"qk0": 0, "out": 4, "qk1": 12, "v": 16}[what]

        OUT_LAST = PER * N - 8

        def turns(body, eng):
            body(0, True, False)
            with eng.Fori(1, N - 1) as i:
                body(i, False, False)
            body(N - 1, False, True)

        with nc.Block() as block:

            @block.sync
            def _(sp):
                sp.dma_start(mask_u8[:, :, :], dram["mask_b_q"]).then_inc(mask_loaded, 16)

                def turn(i, first, last):
                    for j in range(2):
                        wait(sp, qk_ready[j], i)
                        sp.dma_start(raw_qk[j][:, :, :, :], dram["L0_qk"][i, j, :, :, :, :]).then_inc(qk_loaded[j], 16)
                        wait(sp, comb_ready, 2 * i + j - 1)
                        sp.dma_start(bias[:, j, :], dram["L0_xattn_position_bias"][2 * i + j, :, :]
                                     ).then_inc(bias_loaded[j], 16)
                        if j == 0:
                            wait(sp, v_ready, i)
                            sp.dma_start(raw_v[:, :, :], dram["L0_v"][i, :, :, :]).then_inc(v_loaded, 16)
                    wait(sp, o_ready, i)
                    sp.dma_start(raw_o[:, :, :], dram["L0_o"][i, :, :, :]).then_inc(o_loaded, 16)

                turns(turn, sp)

            @block.gpsimd
            def _(pool):
                def split_low(i, raw, w, hi, ready):
                    pool.wait_ge(hi, i + 1)
                    pool.tensor_tensor(w[1][:, :], raw, as_f32(w[0][:, :]), ALU.subtract).then_inc(ready, 1)

                flat = lambda t: t[:, :, :].rearrange("p a b -> p (a b)")
                flat4 = lambda t: t[:, :, :, :].rearrange("p a b c -> p (a b c)")
                fl = lambda w: (flat(w[0]), flat(w[1]))
                fl4 = lambda w: (flat4(w[0]), flat4(w[1]))

                def combine(i, j):
                    pool.wait_ge(bias_loaded[j], 16 * (i + 1))
                    wait(pool, scores_read, 2 * (2 * i + j))
                    pool.tensor_tensor(comb[:, :, :], neg[:, :, :], bias[:, j:j + 1, :].to_broadcast([P, B, P]),
                                       ALU.add).then_inc(comb_ready, 1)

                pool.wait_ge(mask_loaded, 16)
                pool.tensor_copy(comb[:, :, :], mask_u8[:, :, :]).then_inc(neg_ready, 1)
                pool.wait_ge(neg_ready, 1)
                pool.tensor_scalar(neg[:, :, :], comb[:, :, :], 1.0, -MASKED, ALU.subtract, ALU.mult
                                   ).then_inc(neg_ready, 1)
                pool.wait_ge(neg_ready, 2)
                split_low(0, flat4(raw_qk[0]), fl4(w_qk[0]), qk_hi[0], qk_ready[0])
                split_low(0, flat4(raw_qk[1]), fl4(w_qk[1]), qk_hi[1], qk_ready[1])

                def turn(i, first, last):
                    combine(i, 0)
                    split_low(i, flat(raw_v), fl(w_v), v_hi, v_ready)
                    if not last:
                        split_low(i + 1, flat4(raw_qk[0]), fl4(w_qk[0]), qk_hi[0], qk_ready[0])
                    split_low(i, flat(raw_o), fl(w_o), o_hi, o_ready)
                    combine(i, 1)
                    if not last:
                        split_low(i + 1, flat4(raw_qk[1]), fl4(w_qk[1]), qk_hi[1], qk_ready[1])

                turns(turn, pool)

            @block.tensor
            def _(pe):
                def project_qk(i, j):
                    pe.wait_ge(qk_ready[j], i + 1)
                    if not (isinstance(i, int) and i == 0 and j == 0):
                        pe.wait_ge(scores_full, 2 * (2 * i + j))
                    w = w_qk[j]
                    for n in range(4):
                        wait(pe, ring_drained, ring_at(i, "qk%d" % j) + n - 3)
                        src = (qin, cin)[n // 2]
                        for c in range(DC):
                            part = slice((n % 2) * HALF, (n % 2 + 1) * HALF)
                            mm = product(pe, bank[n][:, :], [w[s][:, n // 2, c, :] for s in range(2)],
                                         [src[s][:, c, part] for s in range(2)], c == 0, c == DC - 1)
                        mm.then_inc(ring_full, 1)

                def project_v(i):
                    pe.wait_ge(v_ready, i + 1)
                    for m in range(4):
                        wait(pe, ring_drained, ring_at(i, "v") + m - 3)
                        for b in (2 * m, 2 * m + 1):
                            for c in range(DC):
                                mm = product(pe, bank[m][:, (b % 2) * 2 * P:(b % 2 + 1) * 2 * P],
                                             [cin[s][:, c, b * P:(b + 1) * P] for s in range(2)],
                                             [w_v[s][:, c, :] for s in range(2)], c == 0, c == DC - 1)
                        mm.then_inc(ring_full, 1)

                def scores(i, j):
                    h = 2 * i + j
                    pe.wait_ge(ring_drained, ring_at(i, "qk%d" % j) + 4)
                    wait(pe, scores_read, 2 * h)
                    for half in range(2):
                        for y in range(BH):
                            t = slice((half * BH + y) * P, (half * BH + y + 1) * P)
                            mm = product(pe, bank[4 + half][:, y * P:(y + 1) * P], [q[s][:, t] for s in range(2)],
                                         [k[s][:, t] for s in range(2)], True, True)
                        mm.then_inc(scores_full, 1)

                def transpose_probs(h):
                    pe.wait_ge(probs_ready, h + 1)
                    wait(pe, h_drained, 2 * h)
                    for half in range(2):
                        for y in range(BH):
                            mm = pe.transpose(bank[6 + half][:, y * P:(y + 1) * P], probs[:, half * BH + y, :],
                                              core.ident[:, :])
                        mm.then_inc(t_full, 1)

                def weigh_values(h, j):
                    for half in range(2):
                        pe.wait_ge(t_drained, 2 * h + half + 1)
                        if half == 0:
                            pe.wait_ge(ring_drained, v_until(h, j))
                        for y in range(BH):
                            b = half * BH + y
                            mm = product(pe, bank[6 + half][:, y * P:(y + 1) * P],
                                         [v[s][:, b, j * P:(j + 1) * P] for s in range(2)],
                                         [probs_t[s][:, b, :] for s in range(2)], True, True)
                        mm.then_inc(h_full, 1)

                v_end = [None]

                def v_until(h, j):
                    return v_end[0]

                def project_out(i, at):
                    pe.wait_ge(o_ready, i + 1)
                    pe.wait_ge(h_drained, 4 * i + 4)
                    for b in range(B):
                        wait(pe, ring_drained, at + b - 3)
                        for j in range(2):
                            mm = product(pe, bank[b % 4][:, :], [heads[s][:, j, b * P:(b + 1) * P] for s in range(2)],
                                         [w_o[s][:, j, :] for s in range(2)], j == 0, j == 1)
                        mm.then_inc(ring_full, 1)

                def turn(i, first, last):
                    project_qk(i, 0)
                    if not first:
                        transpose_probs(2 * i - 1)
                        v_end[0] = ring_at(i - 1, "v") + 4
                        weigh_values(2 * i - 1, 1)
                        project_out(i - 1, ring_at(i, "out"))
                    scores(i, 0)
                    project_qk(i, 1)
                    transpose_probs(2 * i)
                    project_v(i)
                    v_end[0] = ring_at(i, "v") + 4
                    weigh_values(2 * i, 0)
                    scores(i, 1)

                turns(turn, pe)
                transpose_probs(2 * N - 1)
                v_end[0] = ring_at(N - 1, "v") + 4
                weigh_values(2 * N - 1, 1)
                project_out(N - 1, OUT_LAST)

            @block.scalar
            def _(act):
                def exps(h):
                    act.wait_ge(top_ready, h + 1)
                    wait(act, inv_done, h)
                    for b in range(B):
                        act.activation(probs[:, b, :], probs[:, b, :], ACT.Exp, bias=top[:, b:b + 1],
                                       accum_out=row_sum[:, b:b + 1]).then_inc(exp_done, 1)

                def split_high(i, raw, w, loaded, hi, free):
                    act.wait_ge(loaded, 16 * (i + 1))
                    wait(act, ring_full, free)
                    act.activation(w, raw, ACT.Copy).then_inc(hi, 1)

                def high(full, at, dst, src, done):
                    act.wait_ge(full, at + 1)
                    act.activation(dst, src, ACT.Copy).then_inc(done, 1)

                def qk_high(i, j):
                    at = ring_at(i, "qk%d" % j)
                    for n in range(4):
                        high(ring_full, at + n, (q, k)[n // 2][0][:, (n % 2) * HALF:(n % 2 + 1) * HALF],
                             bank[n][:, :], ring_hi)

                def v_high(i):
                    at = ring_at(i, "v")
                    for m in range(4):
                        if m == 0 and not (isinstance(i, int) and i == 0):
                            act.wait_ge(h_full, 4 * i)
                        high(ring_full, at + m, v[0][:, 2 * m:2 * m + 2, :],
                             bank[m][:, :].rearrange("p (b n) -> p b n", b=2), ring_hi)

                def probs_high(h):
                    for half in range(2):
                        high(t_full, 2 * h + half, probs_t[0][:, half * BH:(half + 1) * BH, :],
                             bank[6 + half][:, :].rearrange("p (b n) -> p b n", b=BH), t_hi)

                def heads_high(h, j):
                    for half in range(2):
                        high(h_full, 2 * h + half, heads[0][:, j, half * HALF:(half + 1) * HALF],
                             bank[6 + half][:, :], h_hi)

                split_high(0, raw_qk[0][:, :, :, :], w_qk[0][0][:, :, :, :], qk_loaded[0], qk_hi[0], 0)
                split_high(0, raw_qk[1][:, :, :, :], w_qk[1][0][:, :, :, :], qk_loaded[1], qk_hi[1], 0)

                def turn(i, first, last):
                    if not first:
                        exps(2 * i - 1)
                    split_high(i, raw_v[:, :, :], w_v[0][:, :, :], v_loaded, v_hi, ring_at(i, "qk0") if not first else 0)
                    qk_high(i, 0)
                    if not first:
                        probs_high(2 * i - 1)
                        heads_high(2 * i - 1, 1)
                    if not last:
                        split_high(i + 1, raw_qk[0][:, :, :, :], w_qk[0][0][:, :, :, :], qk_loaded[0], qk_hi[0],
                                   ring_at(i, "qk0") + 4)
                    split_high(i, raw_o[:, :, :], w_o[0][:, :, :], o_loaded, o_hi,
                               ring_at(i, "out") + 8 if not first else 0)
                    exps(2 * i)
                    qk_high(i, 1)
                    probs_high(2 * i)
                    v_high(i)
                    if not first:
                        wait(act, ring_full, ring_at(i, "out") + 8)
                    heads_high(2 * i, 0)
                    if not last:
                        split_high(i + 1, raw_qk[1][:, :, :, :], w_qk[1][0][:, :, :, :], qk_loaded[1], qk_hi[1],
                                   ring_at(i, "qk1") + 4)

                turns(turn, act)
                exps(2 * N - 1)
                probs_high(2 * N - 1)
                heads_high(2 * N - 1, 1)

            @block.vector
            def _(dve):
                def add_bias(h):
                    dve.wait_ge(comb_ready, h + 1)
                    for half in range(2):
                        part = slice(half * BH, (half + 1) * BH)
                        dve.wait_ge(scores_full, 2 * h + half + 1)
                        wait(dve, t_full, 2 * h)
                        dve.tensor_tensor(probs[:, part, :], bank[4 + half][:, :].rearrange("p (b n) -> p b n", b=BH),
                                          comb[:, part, :], ALU.add).then_inc(scores_read, 1)
                    dve.wait_ge(scores_read, 2 * h + 2)
                    wait(dve, exp_done, B * h)
                    dve.tensor_reduce(top[:, :], probs[:, :, :], AX.X, ALU.max).then_inc(top_raw, 1)
                    dve.wait_ge(top_raw, h + 1)
                    dve.tensor_scalar(top[:, :], top[:, :], FLOOR, -1.0, ALU.max, ALU.mult).then_inc(top_ready, 1)

                def normalise(h):
                    dve.wait_ge(exp_done, B * (h + 1))
                    dve.tensor_scalar_max(inv_sum[:, :], row_sum[:, :], 1e-30).then_inc(sum_ok, 1)
                    dve.wait_ge(sum_ok, h + 1)
                    dve.reciprocal(inv_sum[:, :], inv_sum[:, :]).then_inc(inv_done, 1)
                    dve.wait_ge(inv_done, h + 1)
                    dve.tensor_tensor(probs[:, :, :], probs[:, :, :],
                                      inv_sum[:, :].rearrange("p (b o) -> p b o", o=1).to_broadcast([P, B, P]),
                                      ALU.mult).then_inc(probs_ready, 1)

                def low(hi, at, dst, src, dst_hi, done):
                    dve.wait_ge(hi, at + 1)
                    dve.tensor_tensor(dst, src, as_f32(dst_hi), ALU.subtract).then_inc(done, 1)

                def qk_low(i, j, n0):
                    at = (12 * i) + 4 * j
                    for n in (n0, n0 + 1):
                        part = slice((n % 2) * HALF, (n % 2 + 1) * HALF)
                        t = (q, k)[n // 2]
                        low(ring_hi, at + n, t[1][:, part], bank[n][:, :], t[0][:, part], ring_drained)

                def v_low(i):
                    for m in range(4):
                        low(ring_hi, 12 * i + 8 + m, v[1][:, 2 * m:2 * m + 2, :],
                            bank[m][:, :].rearrange("p (b n) -> p b n", b=2), v[0][:, 2 * m:2 * m + 2, :], ring_drained)

                def probs_low(h):
                    for half in range(2):
                        part = slice(half * BH, (half + 1) * BH)
                        low(t_hi, 2 * h + half, probs_t[1][:, part, :],
                            bank[6 + half][:, :].rearrange("p (b n) -> p b n", b=BH), probs_t[0][:, part, :], t_drained)

                def heads_low(h, j):
                    for half in range(2):
                        part = slice(half * HALF, (half + 1) * HALF)
                        low(h_hi, 2 * h + half, heads[1][:, j, part], bank[6 + half][:, :], heads[0][:, j, part],
                            h_drained)

                def add_out(at):
                    for b in range(B):
                        dve.wait_ge(ring_full, at + b + 1)
                        dve.tensor_tensor(x[:, b, :], x[:, b, :], bank[b % 4][:, :], ALU.add).then_inc(ring_drained, 1)

                def turn(i, first, last):
                    if not first:
                        add_bias(2 * i - 1)
                    qk_low(i, 0, 0)
                    if not first:
                        normalise(2 * i - 1)
                    qk_low(i, 0, 2)
                    if not first:
                        probs_low(2 * i - 1)
                        heads_low(2 * i - 1, 1)
                        add_out(ring_at(i, "out"))
                    add_bias(2 * i)
                    qk_low(i, 1, 0)
                    normalise(2 * i)
                    qk_low(i, 1, 2)
                    probs_low(2 * i)
                    v_low(i)
                    heads_low(2 * i, 0)

                turns(turn, dve)
                add_bias(2 * N - 1)
                normalise(2 * N - 1)
                probs_low(2 * N - 1)
                heads_low(2 * N - 1, 1)
                add_out(OUT_LAST)


def l0_ffn(core, dram):
    nc, x, bank = core.nc, core.x, core.bank
    E, R, EC = 8, 64, 4
    with ExitStack() as ctx:
        sb = lambda name, shape, dt=F32: core.sb(ctx, "l0f_" + name, shape, dt)
        sem = lambda name: core.sem("l0f_" + name)
        xn, xt = sb("xn", [P, B, D]), sb("xt", [P, DC, T])
        w_q, keys = sb("w_q", [P, DC, P]), sb("keys", [P, E])
        w_down, w_org, w_up = sb("w_down", [P, DC, E * R]), sb("w_org", [P, DC, D]), sb("w_up", [P, EC, D])
        h = sb("h", [P, EC, T])
        y_sum, query = sb("y_sum", [P, DC, B]), sb("query", [P, B])
        top, total, inv = sb("top", [B, 1]), sb("total", [B, 1]), sb("inv", [B, 1])
        exps, coef = sb("exps", [B, E]), sb("coef", [B, E, R])
        coef_t = sb("coef_t", [P, EC, B])
        q_loaded, down_loaded, out_loaded = sem("q_loaded"), sem("down_loaded"), sem("out_loaded")

        def loads(sp):
            sp.dma_start(w_q[:, :, :], dram["L0f_wq"]).then_inc(q_loaded, 16)
            sp.dma_start(keys[:, :], dram["L0f_keys"]).then_inc(q_loaded, 16)
            sp.dma_start(w_down[:, :, :], dram["L0f_down"]).then_inc(down_loaded, 16)
            sp.dma_start(w_org[:, :, :], dram["L0f_org"]).then_inc(out_loaded, 16)
            sp.dma_start(w_up[:, :, :], dram["L0f_up"]).then_inc(out_loaded, 16)

        norm_stage(core, xn, xt, loads)

        sum_done, query_full, query_done = sem("sum_done"), sem("query_full"), sem("query_done")
        scores_full, top_done, exp_done, inv_done = sem("scores_full"), sem("top_done"), sem("exp_done"), sem("inv_done")
        raw_done = sem("raw_done")
        coef_done, coef_full, coef_t_done = sem("coef_done"), sem("coef_full"), sem("coef_t_done")
        ring_full, ring_drained = sem("ring_full"), sem("ring_drained")
        scale = 1.0 / float(np.sqrt(P))
        with nc.Block() as block:

            @block.tensor
            def _(pe):
                def low_rank(n):
                    j, half = n // 2, n % 2
                    wait(pe, ring_drained, n - 3)
                    for c in range(DC):
                        mm = product(pe, bank[4 + n % 4][:, :], [w_down[:, c, j * P:(j + 1) * P]],
                                     [xt[:, c, half * HALF:(half + 1) * HALF]], c == 0, c == DC - 1)
                    mm.then_inc(ring_full, 1)

                pe.wait_ge(down_loaded, 16)
                low_rank(0)
                pe.wait_ge(q_loaded, 32)
                pe.wait_ge(sum_done, 1)
                for c in range(DC):
                    mm = product(pe, bank[0][:, 0:B], [w_q[:, c, :]], [y_sum[:, c, :]], c == 0, c == DC - 1)
                mm.then_inc(query_full, 1)
                low_rank(1)
                pe.wait_ge(query_done, 1)
                product(pe, bank[1][0:B, 0:E], [query[:, :]], [keys[:, :]], True, True).then_inc(scores_full, 1)
                low_rank(2)
                low_rank(3)
                pe.wait_ge(coef_done, 1)
                for j in range(EC):
                    mm = product(pe, bank[2][:, j * B:(j + 1) * B],
                                 [coef[:, 2 * j:2 * j + 2, :].rearrange("b e r -> b (e r)")],
                                 [core.ident[0:B, 0:B]], True, True)
                mm.then_inc(coef_full, 1)
                for n in range(4, 8):
                    low_rank(n)
                pe.wait_ge(out_loaded, 32)
                for b in range(B):
                    part = slice(b * P, (b + 1) * P)
                    wait(pe, ring_drained, 8 + b - 3)
                    if b == 0:
                        pe.wait_ge(ring_drained, 8)
                    for c in range(DC):
                        product(pe, bank[4 + b % 4][:, :], [xt[:, c, part]], [w_org[:, c, :]], c == 0, False)
                    for j in range(EC):
                        mm = product(pe, bank[4 + b % 4][:, :], [h[:, j, part]], [w_up[:, j, :]], False, j == EC - 1)
                    mm.then_inc(ring_full, 1)

            @block.scalar
            def _(act):
                act.wait_ge(query_full, 1)
                act.activation(query[:, :], bank[0][:, 0:B], ACT.Copy, scale=1.0 / P).then_inc(query_done, 1)
                act.wait_ge(top_done, 1)
                act.activation(exps[:, :], bank[1][0:B, 0:E], ACT.Exp, bias=top[:, :], scale=scale,
                               accum_out=total[:, :]).then_inc(exp_done, 1)

            @block.vector
            def _(dve):
                dve.tensor_reduce(y_sum[:, :, :], xt[:, :, :].rearrange("p c (b t) -> p c b t", b=B), AX.X, ALU.add
                                  ).then_inc(sum_done, 1)
                dve.wait_ge(scores_full, 1)
                dve.tensor_reduce(top[:, :], bank[1][0:B, 0:E], AX.X, ALU.max).then_inc(raw_done, 1)
                dve.wait_ge(raw_done, 1)
                dve.tensor_scalar(top[:, :], top[:, :], -scale, None, ALU.mult).then_inc(top_done, 1)
                dve.wait_ge(exp_done, 1)
                dve.reciprocal(inv[:, :], total[:, :]).then_inc(inv_done, 1)
                dve.wait_ge(inv_done, 1)
                dve.tensor_scalar(coef[:, :, :], exps[:, :].rearrange("b (e o) -> b e o", o=1).to_broadcast([B, E, R]),
                                  inv[:, 0:1], None, ALU.mult).then_inc(coef_done, 1)
                dve.wait_ge(coef_full, 1)
                dve.tensor_copy(coef_t[:, :, :], bank[2][:, 0:EC * B].rearrange("p (j b) -> p j b", j=EC)
                                ).then_inc(coef_t_done, 1)
                dve.wait_ge(coef_t_done, 1)
                for n in range(8):
                    j, half = n // 2, n % 2
                    dve.wait_ge(ring_full, n + 1)
                    dve.tensor_tensor(h[:, j, half * HALF:(half + 1) * HALF].rearrange("p (b t) -> p b t", b=BH),
                                      bank[4 + n % 4][:, :].rearrange("p (b t) -> p b t", b=BH),
                                      coef_t[:, j, half * BH:(half + 1) * BH].rearrange("p (b o) -> p b o", o=1)
                                      .to_broadcast([P, BH, P]), ALU.mult).then_inc(ring_drained, 1)
                for b in range(B):
                    dve.wait_ge(ring_full, 8 + b + 1)
                    dve.tensor_tensor(x[:, b, :], x[:, b, :], bank[4 + b % 4][:, :], ALU.add).then_inc(ring_drained, 1)


def l1_attention(core, dram):
    nc, x, bank = core.nc, core.x, core.bank
    KV, G, HD = 8, 4, 16
    SCALE = 1.0 / float(np.sqrt(HD))
    with ExitStack() as ctx:
        sb = lambda name, shape, dt=F32: core.sb(ctx, "l1x_" + name, shape, dt)
        sem = lambda name: core.sem("l1x_" + name)
        xn, xt, ct = sb("xn", [P, B, D]), sb("xt", [P, DC, T]), sb("ct", [P, DC, T])
        w_q, w_kv, w_o = sb("w_q", [P, DC, D]), sb("w_kv", [P, DC, 2 * P]), sb("w_o", [P, G, D])
        same = sb("same", [P, KV])
        q = sb("q", [P, G, P])
        kt, vt = sb("kt", [P, P]), sb("vt", [P, P])
        kd = sb("kd", [P, KV, P])
        v1 = sb("v1", [P, KV, HD + 1])
        top = [sb(f"top{n}", [P, KV]) for n in range(2)]
        probs = [sb(f"probs{n}", [P, KV, P]) for n in range(2)]
        probs_t = [sb(f"probs_t{n}", [P, KV, P]) for n in range(2)]
        inv = sb("inv", [P, KV])
        a, at = sb("a", [P, G, KV, HD]), sb("at", [P, G, P])
        loaded, made, same_ready, ones_ready = sem("loaded"), sem("made"), sem("same_ready"), sem("ones_ready")

        def loads(sp):
            sp.dma_start(w_q[:, :, :], dram["L1x_wq"]).then_inc(loaded, 16)
            sp.dma_start(ct[:, :, :], dram["ctx_t"]).then_inc(loaded, 16)
            sp.dma_start(w_kv[:, :, :], dram["L1x_wkv"]).then_inc(loaded, 16)
            sp.dma_start(w_o[:, :, :], dram["L1x_wo"]).then_inc(loaded, 16)

        norm_stage(core, xn, xt, loads)

        q_full, q_done, kv_full, kt_done, vt_done = (sem("q_full"), sem("q_done"), sem("kv_full"), sem("kt_done"),
                                                     sem("vt_done"))
        kd_done, v_full, v_done = sem("kd_done"), sem("v_full"), sem("v_done")
        s_full, top_done, shifted, exp_done = sem("s_full"), sem("top_done"), sem("shifted"), sem("exp_done")
        t_full, t_done, a_full, inv_done, a_done = (sem("t_full"), sem("t_done"), sem("a_full"), sem("inv_done"),
                                                    sem("a_done"))
        at_full, at_done, o_full, o_done = sem("at_full"), sem("at_done"), sem("o_full"), sem("o_done")
        with nc.Block() as block:

            @block.gpsimd
            def _(pool):
                pool.memset(v1[:, :, :], 1.0).then_inc(ones_ready, 1)
                pool.memset(same[:, :], 1.0).then_inc(made, 1)
                pool.wait_ge(made, 1)
                pool.affine_select(out=same[:, :], in_=same[:, :], compare_op=ALU.is_ge, fill=0.0, base=0,
                                   pattern=[[-HD, KV]], channel_multiplier=1).then_inc(made, 1)
                pool.wait_ge(made, 2)
                pool.affine_select(out=same[:, :], in_=same[:, :], compare_op=ALU.is_ge, fill=0.0, base=HD - 1,
                                   pattern=[[HD, KV]], channel_multiplier=-1).then_inc(same_ready, 1)
                pool.wait_ge(same_ready, 1)

                def turn(b):
                    pool.wait_ge(kt_done, b + 1)
                    wait(pool, s_full, G * b)
                    pool.tensor_tensor(kd[:, :, :], kt[:, :].rearrange("p (o k) -> p o k", o=1).to_broadcast([P, KV, P]),
                                       same[:, :].rearrange("p (n o) -> p n o", o=1).to_broadcast([P, KV, P]),
                                       ALU.mult).then_inc(kd_done, 1)

                turn(0)
                with pool.Fori(1, B) as b:
                    turn(b)

            @block.tensor
            def _(pe):
                pe.wait_ge(loaded, 64)

                def turn(b, first):
                    tokens = bass.ds(b * P, P)
                    wait(pe, o_done, b)
                    for n, w in enumerate((slice(0, P), slice(P, 2 * P))):
                        for c in range(DC):
                            mm = product(pe, bank[7][:, n * P:(n + 1) * P], [w_kv[:, c, w]], [ct[:, c, tokens]],
                                         c == 0, c == DC - 1)
                    mm.then_inc(kv_full, 1)
                    wait(pe, a_done, G * b)
                    for g in range(G):
                        for c in range(DC):
                            mm = product(pe, bank[6][:, g * P:(g + 1) * P], [w_q[:, c, g * P:(g + 1) * P]],
                                         [xt[:, c, tokens]], c == 0, c == DC - 1)
                    mm.then_inc(q_full, 1)
                    pe.wait_ge(vt_done, b + 1)
                    pe.transpose(bank[7][:, 0:P], vt[:, :], core.ident[:, :]).then_inc(v_full, 1)
                    pe.wait_ge(kd_done, b + 1)
                    pe.wait_ge(q_done, b + 1)
                    for g in range(G + 1):
                        if g < G:
                            if g >= 2:
                                pe.wait_ge(shifted, G * b + g - 1)
                            for n in range(2):
                                mm = product(pe, bank[2 * (g % 2) + n][:, :], [q[:, g, :]],
                                             [kd[:, n * BH:(n + 1) * BH, :].rearrange("p n k -> p (n k)")], True, True)
                            mm.then_inc(s_full, 1)
                        if g >= 1:
                            s = g - 1
                            pe.wait_ge(exp_done, G * b + s + 1)
                            if first and s == 0:
                                pass
                            else:
                                pe.wait_ge(t_done, 2 * (G * b + s))
                            for m in range(KV):
                                mm = pe.transpose(bank[4 + m // 4][:, (m % 4) * P:(m % 4 + 1) * P],
                                                  probs[s % 2][:, m, :], core.ident[:, :])
                                if m % 4 == 3:
                                    mm.then_inc(t_full, 1)
                            if s == 0:
                                pe.wait_ge(v_done, b + 1)
                            else:
                                pe.wait_ge(a_done, G * b + s)
                            for m in range(KV):
                                if m % 4 == 0:
                                    pe.wait_ge(t_done, 2 * (G * b + s) + m // 4 + 1)
                                mm = product(pe, bank[6][:, m * (HD + 1):(m + 1) * (HD + 1)], [probs_t[s % 2][:, m, :]],
                                             [v1[:, m, :]], True, True)
                            mm.then_inc(a_full, 1)
                    pe.wait_ge(a_done, G * b + G)
                    for g in range(G):
                        mm = pe.transpose(bank[4][:, g * P:(g + 1) * P], a[:, g, :, :].rearrange("p n d -> p (n d)"),
                                          core.ident[:, :])
                    mm.then_inc(at_full, 1)
                    pe.wait_ge(at_done, b + 1)
                    for g in range(G):
                        mm = product(pe, bank[7][:, :], [at[:, g, :]], [w_o[:, g, :]], g == 0, g == G - 1)
                    mm.then_inc(o_full, 1)

                turn(0, True)
                with pe.Fori(1, B) as b:
                    turn(b, False)

            @block.scalar
            def _(act):
                def turn(b):
                    act.wait_ge(kv_full, b + 1)
                    act.activation(kt[:, :], bank[7][:, 0:P], ACT.Copy).then_inc(kt_done, 1)
                    act.activation(vt[:, :], bank[7][:, P:2 * P], ACT.Copy).then_inc(vt_done, 1)
                    act.wait_ge(q_full, b + 1)
                    act.activation(q[:, :, :], bank[6][:, :].rearrange("p (g t) -> p g t", g=G), ACT.Copy
                                   ).then_inc(q_done, 1)
                    for g in range(G):
                        act.wait_ge(shifted, G * b + g + 1)
                        act.activation(probs[g % 2][:, :, :], probs[g % 2][:, :, :], ACT.Exp, scale=SCALE
                                       ).then_inc(exp_done, 1)
                        for n in range(2):
                            act.wait_ge(t_full, 2 * (G * b + g) + n + 1)
                            act.activation(probs_t[g % 2][:, n * BH:(n + 1) * BH, :],
                                           bank[4 + n][:, :].rearrange("p (m k) -> p m k", m=BH), ACT.Copy
                                           ).then_inc(t_done, 1)
                    act.wait_ge(at_full, b + 1)
                    act.activation(at[:, :, :], bank[4][:, :].rearrange("p (g t) -> p g t", g=G), ACT.Copy
                                   ).then_inc(at_done, 1)

                turn(0)
                with act.Fori(1, B) as b:
                    turn(b)

            @block.vector
            def _(dve):
                wide = lambda t: t[:, :].rearrange("p (n o) -> p n o", o=1)

                def result(b, g):
                    bk = bank[6][:, 0:KV * (HD + 1)].rearrange("p (n d) -> p n d", d=HD + 1)
                    dve.wait_ge(a_full, G * b + g + 1)
                    dve.reciprocal(inv[:, :], bk[:, :, HD]).then_inc(inv_done, 1)
                    dve.wait_ge(inv_done, G * b + g + 1)
                    dve.tensor_tensor(a[:, g, :, :], bk[:, :, 0:HD], wide(inv).to_broadcast([P, KV, HD]), ALU.mult
                                      ).then_inc(a_done, 1)

                def turn(b, first):
                    dve.wait_ge(v_full, b + 1)
                    dve.tensor_copy(v1[:, :, 0:HD], bank[7][:, 0:P].rearrange("p (n d) -> p n d", n=KV)
                                    ).then_inc(v_done, 1)
                    for g in range(G):
                        s = bank[2 * (g % 2):2 * (g % 2) + 2]
                        dve.wait_ge(s_full, G * b + g + 1)
                        if not first:
                            dve.wait_ge(shifted, G * b)
                        for n in range(2):
                            dve.tensor_reduce(top[g % 2][:, n * BH:(n + 1) * BH],
                                              s[n][:, :].rearrange("p (m k) -> p m k", m=BH), AX.X, ALU.max
                                              ).then_inc(top_done, 1)
                        if g >= 2 or not first:
                            dve.wait_ge(t_full, 2 * (G * b + g - 1))
                        for n in range(2):
                            dve.wait_ge(top_done, 2 * (G * b + g) + n + 1)
                            mm = dve.tensor_tensor(
                                probs[g % 2][:, n * BH:(n + 1) * BH, :], s[n][:, :].rearrange("p (m k) -> p m k", m=BH),
                                wide(top[g % 2])[:, n * BH:(n + 1) * BH, :].to_broadcast([P, BH, P]), ALU.subtract)
                        mm.then_inc(shifted, 1)
                        if g >= 1:
                            result(b, g - 1)
                    result(b, G - 1)
                    dve.wait_ge(o_full, b + 1)
                    xb = x[:, bass.ds(b, 1), :].rearrange("p o d -> p (o d)")
                    dve.tensor_tensor(xb, xb, bank[7][:, :], ALU.add).then_inc(o_done, 1)

                dve.wait_ge(ones_ready, 1)
                turn(0, True)
                with dve.Fori(1, B) as b:
                    turn(b, False)


def l1_ffn(core, dram):
    nc, x, bank = core.nc, core.x, core.bank
    BOT, RD, SLOTS, TOPK, VB = 64, 48, P, 8, 32
    TAU_LOW, TAU_HIGH, EARLY_EXIT = 0.5, 2.0, 0.05
    TAKEN = -3e38
    GELU = float(np.sqrt(2.0 / np.pi))
    with ExitStack() as ctx:
        sb = lambda name, shape, dt=F32: core.sb(ctx, "l1f_" + name, shape, dt)
        sem = lambda name: core.sem("l1f_" + name)
        xn, xt = sb("xn", [P, B, D]), sb("xt", [P, DC, T])
        w_q, w_r, keys = sb("w_q", [P, DC, BOT]), sb("w_r", [BOT, RD]), sb("keys", [BOT, SLOTS])
        values, w_vd, w_vu = sb("values", [P, DC, SLOTS]), sb("w_vd", [P, DC, VB]), sb("w_vu", [VB, D])
        w_u1, w_u2 = sb("w_u1", [P, DC, P]), sb("w_u2", [P, 1])
        consts = sb("consts", [P, 4])
        log_rel = sb("log_rel", [P, 1, SLOTS])
        ones = sb("ones", [P, P])
        rk, vd, table = sb("rk", [RD, SLOTS]), sb("vd", [VB, SLOTS]), sb("table", [SLOTS, D])
        q, rq = sb("q", [BOT, T]), sb("rq", [RD, T])
        z, th = sb("z", [P, T]), sb("th", [P, T])
        route, rest, attn = sb("route", [P, B, SLOTS]), sb("rest", [P, B, SLOTS]), sb("attn", [P, B, SLOTS])
        top8, top, total = sb("top8", [P, B, TOPK]), sb("top", [P, B]), sb("total", [P, B])
        attn_t = sb("attn_t", [SLOTS, T])
        lv, lsum, u, gate = sb("lv", [P, B]), sb("lsum", [P, 1]), sb("u", [P, B]), sb("gate", [P, B])
        loaded, ones_done = sem("loaded"), sem("ones_done")
        names = (("L1f_wq", w_q), ("L1f_wr", w_r), ("L1f_keys", keys), ("L1f_values", values), ("L1f_wvd", w_vd),
                 ("L1f_wvu", w_vu), ("L1f_wu1", w_u1), ("L1f_wu2", w_u2), ("L1f_consts", consts), ("L1f_log_rel", log_rel))

        def loads(sp):
            for name, t in names:
                sp.dma_start(t[tuple(slice(None) for _ in t.shape)], dram[name]).then_inc(loaded, 16)

        norm_stage(core, xn, xt, loads)

        small_full, small_done, table_full, table_done = (sem("small_full"), sem("small_done"), sem("table_full"),
                                                          sem("table_done"))
        q_full, q_done, rq_full, rq_done = sem("q_full"), sem("q_done"), sem("rq_full"), sem("rq_done")
        z_full, z_done, gelu_step, th_done, gelu_done = (sem("z_full"), sem("z_done"), sem("gelu_step"), sem("th_done"),
                                                         sem("gelu_done"))
        route_full, attn_full, route_done, top8_done, rest_done = (sem("route_full"), sem("attn_full"),
                                                                   sem("route_done"), sem("top8_done"), sem("rest_done"))
        attn_step, top_done, exp_done = sem("attn_step"), sem("top_done"), sem("exp_done")
        t_full, t_done, aux_full, aux_read = sem("t_full"), sem("t_done"), sem("aux_full"), sem("aux_read")
        learned_full, var_done, lv_done, lsum_done, mean_full = (sem("learned_full"), sem("var_done"), sem("lv_done"),
                                                                 sem("lsum_done"), sem("mean_full"))
        gate_step, tanh_in, tanh_out = sem("gate_step"), sem("tanh_in"), sem("tanh_out")
        y_added = sem("y_added")
        with nc.Block() as block:

            @block.gpsimd
            def _(pool):
                pool.memset(ones[:, :], 1.0).then_inc(ones_done, 1)
                for b in range(B):
                    pool.tensor_tensor(x[:, b, :], x[:, b, :], xn[:, b, :], ALU.add).then_inc(y_added, 1)

            @block.tensor
            def _(pe):
                pe.wait_ge(loaded, 16 * len(names))
                for half in range(2):
                    part = slice(half * HALF, (half + 1) * HALF)
                    for c in range(DC):
                        mm = product(pe, bank[half][0:BOT, :], [w_q[:, c, :]], [xt[:, c, part]], c == 0, c == DC - 1)
                    mm.then_inc(q_full, 1)
                for half in range(2):
                    part = slice(half * HALF, (half + 1) * HALF)
                    for c in range(DC):
                        mm = product(pe, bank[2 + half][:, :], [w_u1[:, c, :]], [xt[:, c, part]], c == 0, c == DC - 1)
                    mm.then_inc(z_full, 1)
                product(pe, bank[4][0:RD, 0:SLOTS], [w_r[:, :]], [keys[:, :]], True, True).then_inc(small_full, 1)
                for c in range(DC):
                    mm = product(pe, bank[5][0:VB, 0:SLOTS], [w_vd[:, c, :]], [values[:, c, :]], c == 0, c == DC - 1)
                mm.then_inc(small_full, 1)
                pe.wait_ge(q_done, 2)
                for half in range(2):
                    part = slice(half * HALF, (half + 1) * HALF)
                    product(pe, bank[6 + half][0:RD, :], [w_r[:, :]], [q[:, part]], True, True).then_inc(rq_full, 1)
                pe.wait_ge(small_done, 2)
                product(pe, bank[4][:, :], [vd[:, :]], [w_vu[:, :]], True, True).then_inc(table_full, 1)
                pe.wait_ge(rq_done, 2)
                for b in range(B):
                    mm = product(pe, bank[b // BH][:, (b % BH) * P:(b % BH + 1) * P], [rq[:, b * P:(b + 1) * P]],
                                 [rk[:, :]], True, True)
                    mm.then_inc(route_full, 1)
                for b in range(B):
                    mm = product(pe, bank[6 + b // BH][:, (b % BH) * P:(b % BH + 1) * P], [q[:, b * P:(b + 1) * P]],
                                 [keys[:, :]], True, True)
                    mm.then_inc(attn_full, 1)
                pe.wait_ge(ones_done, 1)
                pe.wait_ge(lsum_done, 1)
                product(pe, bank[5][:, 0:1], [ones[:, :]], [lsum[:, :]], True, True).then_inc(mean_full, 1)
                pe.wait_ge(gelu_done, 1)
                pe.wait_ge(z_done, 2)
                for b in range(B):
                    mm = product(pe, bank[2][:, b:b + 1], [z[:, b * P:(b + 1) * P]], [w_u2[:, :]], True, True)
                mm.then_inc(learned_full, 1)
                pe.wait_ge(route_done, 2)
                for b in range(B):
                    pe.wait_ge(exp_done, b + 1)
                    mm = pe.transpose(bank[b // BH][:, (b % BH) * P:(b % BH + 1) * P], attn[:, b, :], core.ident[:, :])
                    if b % BH == BH - 1:
                        mm.then_inc(t_full, 1)
                pe.wait_ge(table_done, 1)
                ring = (3, 4, 6, 7)
                for b in range(B):
                    if b % BH == 0:
                        pe.wait_ge(t_done, b // BH + 1)
                    wait(pe, aux_read, b - 3)
                    product(pe, bank[ring[b % 4]][:, :], [attn_t[:, b * P:(b + 1) * P]], [table[:, :]], True, True
                            ).then_inc(aux_full, 1)

            @block.scalar
            def _(act):
                act.wait_ge(var_done, 1)
                act.activation(lv[:, :], lv[:, :], ACT.Ln, bias=1.0).then_inc(lv_done, 1)
                act.wait_ge(loaded, 16 * len(names))
                for half in range(2):
                    part = slice(half * HALF, (half + 1) * HALF)
                    act.wait_ge(q_full, half + 1)
                    act.activation(q[:, part], bank[half][0:BOT, :], ACT.Copy).then_inc(q_done, 1)
                for half in range(2):
                    part = slice(half * HALF, (half + 1) * HALF)
                    act.wait_ge(z_full, half + 1)
                    act.activation(z[:, part], bank[2 + half][:, :], ACT.Identity, bias=consts[:, 0:1]
                                   ).then_inc(z_done, 1)
                act.wait_ge(small_full, 2)
                act.activation(rk[:, :], bank[4][0:RD, 0:SLOTS], ACT.Copy).then_inc(small_done, 1)
                act.activation(vd[:, :], bank[5][0:VB, 0:SLOTS], ACT.Copy).then_inc(small_done, 1)
                for half in range(2):
                    part = slice(half * HALF, (half + 1) * HALF)
                    act.wait_ge(rq_full, half + 1)
                    act.activation(rq[:, part], bank[6 + half][0:RD, :], ACT.Copy).then_inc(rq_done, 1)
                act.wait_ge(table_full, 1)
                act.activation(table[:, :], bank[4][:, :], ACT.Copy).then_inc(table_done, 1)
                act.wait_ge(gelu_step, 3)
                act.activation(th[:, :], th[:, :], ACT.Tanh, scale=GELU).then_inc(th_done, 1)
                act.wait_ge(tanh_in, 1)
                act.activation(u[:, :], u[:, :], ACT.Tanh, scale=0.5).then_inc(tanh_out, 1)
                for b in range(B):
                    act.wait_ge(top_done, 1)
                    act.activation(attn[:, b, :], attn[:, b, :], ACT.Exp, bias=top[:, b:b + 1],
                                   accum_out=total[:, b:b + 1]).then_inc(exp_done, 1)
                act.wait_ge(tanh_in, 2)
                act.activation(gate[:, :], gate[:, :], ACT.Tanh, scale=0.5).then_inc(tanh_out, 1)
                for half in range(2):
                    act.wait_ge(t_full, half + 1)
                    act.activation(attn_t[:, half * HALF:(half + 1) * HALF], bank[half][:, :], ACT.Copy
                                   ).then_inc(t_done, 1)

            @block.vector
            def _(dve):
                steps = [0]

                def then(instruction):
                    steps[0] += 1
                    instruction.then_inc(gate_step, 1)
                    dve.wait_ge(gate_step, steps[0])

                then(dve.tensor_tensor(lv[:, :], core.mv[:, :, 1], core.rstd[:, :], ALU.mult))
                dve.tensor_tensor(lv[:, :], lv[:, :], core.rstd[:, :], ALU.mult).then_inc(var_done, 1)
                dve.wait_ge(z_done, 2)
                dve.tensor_tensor(th[:, :], z[:, :], z[:, :], ALU.mult).then_inc(gelu_step, 1)
                dve.wait_ge(gelu_step, 1)
                dve.tensor_scalar(th[:, :], th[:, :], 0.044715, 1.0, ALU.mult, ALU.add).then_inc(gelu_step, 1)
                dve.wait_ge(gelu_step, 2)
                dve.tensor_tensor(th[:, :], th[:, :], z[:, :], ALU.mult).then_inc(gelu_step, 1)
                dve.wait_ge(lv_done, 1)
                dve.tensor_reduce(lsum[:, :], lv[:, :], AX.X, ALU.add).then_inc(lsum_done, 1)
                for half in range(2):
                    dve.wait_ge(route_full, BH * (half + 1))
                    dve.scalar_tensor_tensor(route[:, half * BH:(half + 1) * BH, :],
                                             bank[half][:, :].rearrange("p (b n) -> p b n", b=BH),
                                             1.0 / float(np.sqrt(RD)), log_rel[:, :, :].to_broadcast([P, BH, SLOTS]),
                                             ALU.mult, ALU.add).then_inc(route_done, 1)
                dve.wait_ge(route_done, 2)
                for b in range(B):
                    dve.max(top8[:, b, :], route[:, b, :]).then_inc(top8_done, 1)
                dve.wait_ge(th_done, 1)
                dve.scalar_tensor_tensor(z[:, :], th[:, :], 1.0, z[:, :], ALU.add, ALU.mult).then_inc(gelu_done, 1)
                dve.wait_ge(top8_done, B)
                for b in range(B):
                    dve.match_replace(rest[:, b, :], top8[:, b, :], route[:, b, :], TAKEN).then_inc(rest_done, 1)
                for half in range(2):
                    dve.wait_ge(attn_full, BH * (half + 1))
                    dve.scalar_tensor_tensor(attn[:, half * BH:(half + 1) * BH, :],
                                             bank[6 + half][:, :].rearrange("p (b n) -> p b n", b=BH),
                                             1.0 / float(np.sqrt(BOT)), log_rel[:, :, :].to_broadcast([P, BH, SLOTS]),
                                             ALU.mult, ALU.add).then_inc(attn_step, 1)
                dve.wait_ge(rest_done, B)
                dve.tensor_tensor(rest[:, :, :], rest[:, :, :], route[:, :, :], ALU.is_equal).then_inc(attn_step, 1)
                dve.wait_ge(attn_step, 3)
                dve.scalar_tensor_tensor(attn[:, :, :], rest[:, :, :], MASKED, attn[:, :, :], ALU.mult, ALU.add
                                         ).then_inc(attn_step, 1)
                dve.wait_ge(attn_step, 4)
                dve.tensor_reduce(top[:, :], attn[:, :, :], AX.X, ALU.max).then_inc(attn_step, 1)
                dve.wait_ge(attn_step, 5)
                dve.tensor_scalar(top[:, :], top[:, :], -1.0, None, ALU.mult).then_inc(top_done, 1)
                dve.wait_ge(learned_full, 1)
                dve.tensor_scalar(u[:, :], bank[2][:, 0:B], 0.5, consts[:, 1:2], ALU.mult, ALU.add
                                  ).then_inc(tanh_in, 1)
                dve.wait_ge(mean_full, 1)
                then(dve.tensor_scalar(lsum[:, :], bank[5][:, 0:1], 1.0 / T, 1e-6, ALU.mult, ALU.add))
                then(dve.reciprocal(lsum[:, :], lsum[:, :]))
                then(dve.tensor_scalar(lv[:, :], lv[:, :], lsum[:, 0:1], 0.5, ALU.mult, ALU.mult))
                dve.wait_ge(tanh_out, 1)
                then(dve.tensor_scalar(u[:, :], u[:, :], 1.25, 1.25, ALU.mult, ALU.add))
                then(dve.tensor_tensor(u[:, :], u[:, :], lv[:, :], ALU.add))
                then(dve.tensor_scalar(u[:, :], u[:, :], 0.0, 5.0, ALU.max, ALU.min))
                then(dve.tensor_scalar(u[:, :], u[:, :], -TAU_LOW, 1.0 / (TAU_HIGH - TAU_LOW), ALU.add, ALU.mult))
                then(dve.tensor_scalar(u[:, :], u[:, :], 0.0, 1.0, ALU.max, ALU.min))
                dve.tensor_scalar(gate[:, :], u[:, :], consts[:, 2:3], consts[:, 3:4], ALU.mult, ALU.add
                                  ).then_inc(tanh_in, 1)
                dve.wait_ge(tanh_out, 2)
                then(dve.tensor_scalar(gate[:, :], gate[:, :], 0.5, 0.5, ALU.mult, ALU.add))
                then(dve.scalar_tensor_tensor(gate[:, :], gate[:, :], EARLY_EXIT, gate[:, :], ALU.is_ge, ALU.mult))
                dve.wait_ge(exp_done, B)
                then(dve.reciprocal(total[:, :], total[:, :]))
                then(dve.tensor_tensor(gate[:, :], gate[:, :], total[:, :], ALU.mult))
                dve.wait_ge(y_added, B)
                for b in range(B):
                    dve.wait_ge(aux_full, b + 1)
                    dve.scalar_tensor_tensor(x[:, b, :], bank[(3, 4, 6, 7)[b % 4]][:, :], gate[:, b:b + 1],
                                             x[:, b, :], ALU.mult, ALU.add).then_inc(aux_read, 1)


def l2_attention(core, dram):
    nc, x, bank = core.nc, core.x, core.bank
    CRUCIAL = 76
    OTHERS = P - CRUCIAL
    ROUNDS, REST = OTHERS // 8, OTHERS % 8
    TILES = DC * B
    TAKEN = -3e38
    TAPS, PAD = 7, 3
    KINDS = 4
    SETS = 2
    with ExitStack() as ctx:
        sb = lambda name, shape, dt=F32: core.sb(ctx, "l2x_" + name, shape, dt)
        sem = lambda name: core.sem("l2x_" + name)
        xn, xt = sb("xn", [P, B, D]), sb("xt", [P, DC, T])
        work = sb("work", [P, DC, T])
        top8 = sb("top8", [P, TILES, 8])
        fc, fo = sb("fc", [P, DC, T]), sb("fo", [P, DC, T])
        stat = sb("stat", [P, DC, KINDS, B])
        padded, acc = sb("padded", [KINDS * B, D + 2 * PAD]), sb("acc", [KINDS * B, D])
        taps, affine = sb("taps", [KINDS * B, TAPS]), sb("affine", [SETS * B, 2])
        pick, mean = sb("pick", [KINDS * B, SETS * B]), sb("mean", [SETS * B, SETS, B])
        z, zstat, zmv = sb("z", [SETS * B, D]), sb("zstat", [SETS * B, 6]), sb("zmv", [SETS * B, 2])
        mu, dev, rs = sb("mu", [SETS * B, 1]), sb("dev", [SETS * B, 1]), sb("rs", [SETS * B, 1])
        amap = sb("amap", [P, DC, SETS, B])
        loaded, small_loaded, made, const_done = sem("loaded"), sem("small_loaded"), sem("made"), sem("const_done")

        def loads(sp):
            sp.dma_start(work[:, :, :], dram["ctx_t_rev"]).then_inc(loaded, 16)
            sp.dma_start(taps[:, :], dram["L2x_taps"]).then_inc(small_loaded, 16)
            sp.dma_start(affine[:, :], dram["L2x_affine"]).then_inc(small_loaded, 16)

        norm_stage(core, xn, xt, loads)

        step, masked = sem("step"), sem("masked")
        stat_full, stat_done, z_full, z_done = sem("stat_full"), sem("stat_done"), sem("z_full"), sem("z_done")
        mean_in, mean_full, var_in, var_full, rs_in, rs_done = (sem("mean_in"), sem("mean_full"), sem("var_in"),
                                                                sem("var_full"), sem("rs_in"), sem("rs_done"))
        tanh_in, tanh_out, map_in, map_full, map_done = (sem("tanh_in"), sem("tanh_out"), sem("map_in"),
                                                         sem("map_full"), sem("map_done"))
        others_done, out_ready, back_full, added = (sem("others_done"), sem("out_ready"), sem("back_full"),
                                                    sem("added"))
        tiles = lambda t: t[:, :, :].rearrange("p c (b n) -> p (c b) n", b=B)
        with nc.Block() as block:

            @block.gpsimd
            def _(pool):
                pool.memset(mean[:, :, :], 1.0 / B).then_inc(made, 1)
                pool.memset(padded[:, :], 0.0).then_inc(const_done, 1)
                pool.wait_ge(made, 1)
                pool.affine_select(out=mean[:, :, :], in_=mean[:, :, :], compare_op=ALU.is_ge, fill=0.0, base=0,
                                   pattern=[[-B, SETS], [0, B]], channel_multiplier=1).then_inc(made, 1)
                pool.wait_ge(made, 2)
                pool.affine_select(out=mean[:, :, :], in_=mean[:, :, :], compare_op=ALU.is_ge, fill=0.0, base=B - 1,
                                   pattern=[[B, SETS], [0, B]], channel_multiplier=-1).then_inc(const_done, 1)
                pool.wait_ge(rs_in, 1)
                pool.tensor_tensor(rs[:, :], rs[:, :], core.neg_half[0:SETS * B, 0:1], ALU.pow).then_inc(rs_done, 1)

            @block.tensor
            def _(pe):
                pe.wait_ge(stat_done, 1)
                for c in range(DC):
                    mm = pe.transpose(bank[0][0:KINDS * B, c * P:(c + 1) * P],
                                      stat[:, c, :, :].rearrange("p k b -> p (k b)"), core.ident[:, :])
                mm.then_inc(stat_full, 1)
                pe.wait_ge(z_done, 1)
                product(pe, bank[1][0:SETS * B, :], [pick[:, :]], [acc[:, :]], True, True).then_inc(z_full, 1)
                pe.wait_ge(const_done, 2)
                group = mean[:, :, :].rearrange("p s b -> p (s b)")
                pe.wait_ge(mean_in, 1)
                product(pe, bank[2][0:SETS * B, 0:1], [group], [zmv[:, 0:1]], True, True).then_inc(mean_full, 1)
                pe.wait_ge(var_in, 1)
                product(pe, bank[3][0:SETS * B, 0:1], [group], [dev[:, :]], True, True).then_inc(var_full, 1)
                pe.wait_ge(map_in, 1)
                for c in range(DC):
                    mm = pe.transpose(bank[0][:, c * SETS * B:(c + 1) * SETS * B], z[:, c * P:(c + 1) * P],
                                      core.ident[0:SETS * B, 0:SETS * B])
                mm.then_inc(map_full, 1)
                for b in range(B):
                    pe.wait_ge(out_ready, DC)
                    for c in range(DC):
                        mm = pe.transpose(bank[b][:, c * P:(c + 1) * P], fc[:, c, b * P:(b + 1) * P], core.ident[:, :])
                    mm.then_inc(back_full, 1)

            @block.scalar
            def _(act):
                act.wait_ge(tanh_in, 1)
                act.activation(z[:, :], z[:, :], ACT.Tanh, scale=0.5).then_inc(tanh_out, 1)

            @block.vector
            def _(dve):
                steps = [0]

                def mark(instruction):
                    steps[0] += 1
                    instruction.then_inc(step, 1)

                def settle():
                    dve.wait_ge(step, steps[0])

                wt = tiles(work)
                dve.wait_ge(loaded, 16)
                mark(dve.tensor_scalar(work[:, :, :], work[:, :, :], -1.0, None, ALU.mult))
                settle()
                for r in range(ROUNDS + 1):
                    for n in range(TILES):
                        mark(dve.max(top8[:, n, :], wt[:, n, :]))
                    settle()
                    if r == ROUNDS:
                        mark(dve.memset(top8[:, :, REST:8], TAKEN))
                        settle()
                    for n in range(TILES):
                        mark(dve.match_replace(wt[:, n, :], top8[:, n, :], wt[:, n, :], TAKEN))
                    settle()
                mark(dve.tensor_scalar(tiles(fc), wt[:, :, ::-1], TAKEN, None, ALU.not_equal))
                settle()
                mark(dve.tensor_tensor(fc[:, :, :], fc[:, :, :], xt[:, :, :], ALU.mult))
                settle()
                mark(dve.tensor_tensor(fo[:, :, :], xt[:, :, :], fc[:, :, :], ALU.subtract))
                settle()
                for k, (t, op) in enumerate(((fc, ALU.max), (fo, ALU.max), (fc, ALU.add), (fo, ALU.add))):
                    for c in range(DC):
                        mark(dve.tensor_reduce(stat[:, c, k, :], t[:, c, :].rearrange("p (b n) -> p b n", b=B), AX.X, op))
                settle()
                mark(dve.tensor_scalar(stat[:, :, 2, :], stat[:, :, 2, :], 1.0 / CRUCIAL, None, ALU.mult))
                dve.tensor_scalar(stat[:, :, 3, :], stat[:, :, 3, :], 1.0 / OTHERS, None, ALU.mult).then_inc(stat_done, 1)
                dve.wait_ge(small_loaded, 32)
                dve.wait_ge(const_done, 2)
                dve.wait_ge(stat_full, 1)
                mark(dve.tensor_copy(padded[:, PAD:PAD + D], bank[0][0:KINDS * B, :]))
                settle()
                mark(dve.tensor_scalar(acc[:, :], padded[:, 0:D], taps[:, 0:1], None, ALU.mult))
                for t in range(1, TAPS):
                    settle()
                    mark(dve.scalar_tensor_tensor(acc[:, :], padded[:, t:t + D], taps[:, t:t + 1], acc[:, :], ALU.mult,
                                                  ALU.add))
                settle()
                dve.tensor_tensor(pick[:, :], core.ident[0:KINDS * B, 0:SETS * B],
                                  core.ident[0:KINDS * B, SETS * B:KINDS * B], ALU.add).then_inc(z_done, 1)
                dve.wait_ge(z_full, 1)
                mark(dve.tensor_copy(z[:, :], bank[1][0:SETS * B, :]))
                settle()
                mark(dve.bn_stats(zstat[:, :], z[:, :]))
                settle()
                dve.bn_aggr(zmv[:, :], zstat[:, :]).then_inc(mean_in, 1)
                dve.wait_ge(mean_in, 1)
                dve.wait_ge(mean_full, 1)
                mark(dve.tensor_copy(mu[:, :], bank[2][0:SETS * B, 0:1]))
                settle()
                mark(dve.tensor_tensor(dev[:, :], zmv[:, 0:1], mu[:, :], ALU.subtract))
                settle()
                mark(dve.tensor_tensor(dev[:, :], dev[:, :], dev[:, :], ALU.mult))
                settle()
                dve.tensor_tensor(dev[:, :], dev[:, :], zmv[:, 1:2], ALU.add).then_inc(var_in, 1)
                dve.wait_ge(var_full, 1)
                dve.tensor_scalar_add(rs[:, :], bank[3][0:SETS * B, 0:1], EPS).then_inc(rs_in, 1)
                dve.wait_ge(rs_done, 1)
                mark(dve.tensor_scalar(z[:, :], z[:, :], mu[:, 0:1], rs[:, 0:1], ALU.subtract, ALU.mult))
                settle()
                mark(dve.tensor_scalar(z[:, :], z[:, :], affine[:, 0:1], affine[:, 1:2], ALU.mult, ALU.add))
                settle()
                dve.tensor_scalar(z[:, :], z[:, :], 0.0, None, ALU.max).then_inc(tanh_in, 1)
                dve.wait_ge(tanh_out, 1)
                dve.tensor_scalar(z[:, :], z[:, :], 0.5, 0.5, ALU.mult, ALU.add).then_inc(map_in, 1)
                dve.wait_ge(map_full, 1)
                mark(dve.tensor_copy(amap[:, :, :, :],
                                     bank[0][:, 0:DC * SETS * B].rearrange("p (c s b) -> p c s b", c=DC, s=SETS)))
                settle()
                for c in range(DC):
                    for s, t in enumerate((fc, fo)):
                        v = t[:, c, :].rearrange("p (b n) -> p b n", b=B)
                        mark(dve.tensor_tensor(v, v, amap[:, c, s, :].rearrange("p (b o) -> p b o", o=1)
                                               .to_broadcast([P, B, P]), ALU.mult))
                    settle()
                    dve.tensor_tensor(fc[:, c, :], fc[:, c, :], fo[:, c, :], ALU.add).then_inc(out_ready, 1)
                for b in range(B):
                    dve.wait_ge(back_full, b + 1)
                    dve.tensor_tensor(x[:, b, :], x[:, b, :], bank[b][:, :], ALU.add).then_inc(added, 1)


def routed_ffn(core, dram, name, top_k, softmax, base, scaling):
    nc, x, bank = core.nc, core.x, core.bank
    E, R = 8, 16
    with ExitStack() as ctx:
        sb = lambda n, shape, dt=F32: core.sb(ctx, name + "_" + n, shape, dt)
        sem = lambda n: core.sem(name + "_" + n)
        xn, xt = sb("xn", [P, B, D]), sb("xt", [P, DC, T])
        w_a, w_b = sb("w_a", [P, DC, P + E]), sb("w_b", [P, D])
        p, wide, wide2 = sb("p", [P, B, E]), sb("wide", [P, B, E, E]), sb("wide2", [P, B, E, E])
        before = sb("before", [P, 1, E, E])
        red, rank, weight = sb("red", [P, B]), sb("rank", [P, B, E]), sb("weight", [P, B, E])
        h, ht = sb("h", [P, B, E, R]), sb("ht", [P, T])
        loaded, base_loaded, made, before_done = sem("loaded"), sem("base_loaded"), sem("made"), sem("before_done")
        if base:
            w_base, bias = sb("w_base", [P, DC, D]), sb("bias", [P, D])

        def loads(sp):
            sp.dma_start(w_a[:, :, :], dram[name + "_a"]).then_inc(loaded, 16)
            sp.dma_start(w_b[:, :], dram[name + "_b"]).then_inc(loaded, 16)
            if base:
                sp.dma_start(w_base[:, :, :], dram[name + "_base"]).then_inc(base_loaded, 16)
                sp.dma_start(bias[:, :], dram[name + "_bias"]).then_inc(base_loaded, 16)

        norm_stage(core, xn, xt, loads)

        a_full, a_read, step, exp_in, exp_out = sem("a_full"), sem("a_read"), sem("step"), sem("exp_in"), sem("exp_out")
        h_done, t_full, t_done, o_full, o_read, biased = (sem("h_done"), sem("t_full"), sem("t_done"), sem("o_full"),
                                                          sem("o_read"), sem("biased"))
        low = lambda b: bank[b // 2][:, (b % 2) * (P + E):(b % 2) * (P + E) + P]
        logits = lambda n: bank[n][:, 0:2 * (P + E)].rearrange("p (b m) -> p b m", b=2)[:, :, P:P + E]
        with nc.Block() as block:

            @block.gpsimd
            def _(pool):
                pool.memset(before[:, :, :, :], 1.0).then_inc(made, 1)
                pool.wait_ge(made, 1)
                pool.affine_select(out=before[:, 0, :, :], in_=before[:, 0, :, :], compare_op=ALU.is_gt, fill=0.0,
                                   base=0, pattern=[[1, E], [-1, E]], channel_multiplier=0).then_inc(before_done, 1)
                if base:
                    pool.wait_ge(base_loaded, 32)
                    for b in range(B):
                        pool.tensor_tensor(x[:, b, :], x[:, b, :], bias[:, :], ALU.add).then_inc(biased, 1)

            @block.tensor
            def _(pe):
                pe.wait_ge(loaded, 32)
                for b in range(B):
                    for c in range(DC):
                        mm = product(pe, bank[b // 2][:, (b % 2) * (P + E):(b % 2 + 1) * (P + E)],
                                     [xt[:, c, b * P:(b + 1) * P]], [w_a[:, c, :]], c == 0, c == DC - 1)
                    if b % 2:
                        mm.then_inc(a_full, 1)

                def base_product(b):
                    wait(pe, o_read, b - 3)
                    for c in range(DC):
                        product(pe, bank[4 + b % 4][:, :], [xt[:, c, b * P:(b + 1) * P]], [w_base[:, c, :]], c == 0,
                                False)

                if base:
                    pe.wait_ge(base_loaded, 32)
                    for b in range(4):
                        base_product(b)
                for half in range(2):
                    pe.wait_ge(h_done, half + 1)
                    for y in range(BH):
                        b = half * BH + y
                        mm = pe.transpose(bank[half][:, y * P:(y + 1) * P], h[:, b, :, :].rearrange("p e r -> p (e r)"),
                                          core.ident[:, :])
                    mm.then_inc(t_full, 1)
                for b in range(B):
                    pe.wait_ge(t_done, b // BH + 1)
                    if b >= 4 and base:
                        base_product(b)
                    elif b >= 4:
                        pe.wait_ge(o_read, b - 3)
                    product(pe, bank[4 + b % 4][:, :], [ht[:, b * P:(b + 1) * P]], [w_b[:, :]], not base, True
                            ).then_inc(o_full, 1)

            @block.scalar
            def _(act):
                if softmax:
                    act.wait_ge(exp_in, 1)
                    act.activation(p[:, :, :], p[:, :, :], ACT.Exp).then_inc(exp_out, 1)
                for half in range(2):
                    act.wait_ge(t_full, half + 1)
                    act.activation(ht[:, half * HALF:(half + 1) * HALF], bank[half][:, :], ACT.Copy).then_inc(t_done, 1)

            @block.vector
            def _(dve):
                steps = [0]

                def then(instruction):
                    steps[0] += 1
                    instruction.then_inc(step, 1)
                    dve.wait_ge(step, steps[0])

                over_e = lambda t: t[:, :].rearrange("p (b o) -> p b o", o=1).to_broadcast([P, B, E])
                for n in range(4):
                    dve.wait_ge(a_full, n + 1)
                    dve.tensor_copy(p[:, 2 * n:2 * n + 2, :], logits(n)).then_inc(a_read, 1)
                dve.wait_ge(a_read, 4)
                if softmax:
                    then(dve.tensor_reduce(red[:, :], p[:, :, :], AX.X, ALU.max))
                    dve.tensor_tensor(p[:, :, :], p[:, :, :], over_e(red), ALU.subtract).then_inc(exp_in, 1)
                    dve.wait_ge(exp_out, 1)
                    then(dve.tensor_reduce(red[:, :], p[:, :, :], AX.X, ALU.add))
                    then(dve.reciprocal(red[:, :], red[:, :]))
                    then(dve.tensor_tensor(p[:, :, :], p[:, :, :], over_e(red), ALU.mult))
                other = p[:, :, :].rearrange("p b (o e) -> p b o e", o=1).to_broadcast([P, B, E, E])
                own = p[:, :, :].rearrange("p b (e o) -> p b e o", o=1).to_broadcast([P, B, E, E])
                dve.tensor_tensor(wide[:, :, :, :], other, own, ALU.is_gt).then_inc(step, 1)
                dve.tensor_tensor(wide2[:, :, :, :], other, own, ALU.is_equal).then_inc(step, 1)
                steps[0] += 2
                dve.wait_ge(step, steps[0])
                dve.wait_ge(before_done, 1)
                then(dve.tensor_tensor(wide2[:, :, :, :], wide2[:, :, :, :], before[:, :, :, :].to_broadcast([P, B, E, E]),
                                       ALU.mult))
                then(dve.tensor_tensor(wide[:, :, :, :], wide[:, :, :, :], wide2[:, :, :, :], ALU.add))
                then(dve.tensor_reduce(rank[:, :, :], wide[:, :, :, :], AX.X, ALU.add))
                then(dve.scalar_tensor_tensor(weight[:, :, :], rank[:, :, :], float(top_k), p[:, :, :], ALU.is_lt,
                                              ALU.mult))
                if softmax:
                    then(dve.tensor_reduce(red[:, :], weight[:, :, :], AX.X, ALU.add))
                    then(dve.reciprocal(red[:, :], red[:, :]))
                    then(dve.scalar_tensor_tensor(weight[:, :, :], weight[:, :, :], scaling, over_e(red), ALU.mult,
                                                  ALU.mult))
                for b in range(B):
                    mm = dve.tensor_tensor(h[:, b, :, :], low(b).rearrange("p (e r) -> p e r", e=E),
                                           weight[:, b, :].rearrange("p (e o) -> p e o", o=1).to_broadcast([P, E, R]),
                                           ALU.mult)
                    if b == B - 1:
                        mm.then_inc(h_done, 2)
                if base:
                    dve.wait_ge(biased, B)
                for b in range(B):
                    dve.wait_ge(o_full, b + 1)
                    dve.tensor_tensor(x[:, b, :], x[:, b, :], bank[4 + b % 4][:, :], ALU.add).then_inc(o_read, 1)


def l2_ffn(core, dram):
    routed_ffn(core, dram, "l2f", 2, True, True, 2.0)


def l3_ffn(core, dram):
    routed_ffn(core, dram, "l3f", 1, False, False, 1.0)


def l3_attention(core, dram):
    nc, x, bank = core.nc, core.x, core.bank
    GROUPS, G = 8, 4
    HP = P // 2
    SCALE = 1.0 / float(np.sqrt(P))
    with ExitStack() as ctx:
        sb = lambda name, shape, dt=F32: core.sb(ctx, "l3x_" + name, shape, dt)
        pair = lambda name, shape: core.pair(ctx, "l3x_" + name, shape)
        sem = lambda name: core.sem("l3x_" + name)
        qin, cin = pair("qin", [P, DC, T]), pair("cin", [P, DC, T])

        with ExitStack() as ctx1:
            xn, xt = core.sb(ctx1, "l3x_xn", [P, B, D]), core.sb(ctx1, "l3x_xt", [P, DC, T])
            ctx_raw = core.sb(ctx1, "l3x_ctx_raw", [P, DC, T])
            ctx_loaded, in_hi, ctx_lo, in_lo = sem("ctx_loaded"), sem("in_hi"), sem("ctx_lo"), sem("in_lo")

            def loads(sp):
                sp.dma_start(ctx_raw[:, :, :], dram["ctx_t"]).then_inc(ctx_loaded, 16)

            norm_stage(core, xn, xt, loads)
            with nc.Block() as block:

                @block.scalar
                def _(act):
                    for c in range(DC):
                        act.activation(qin[0][:, c, :], xt[:, c, :], ACT.Copy).then_inc(in_hi, 1)
                    act.wait_ge(ctx_loaded, 16)
                    for c in range(DC):
                        act.activation(cin[0][:, c, :], ctx_raw[:, c, :], ACT.Copy).then_inc(in_hi, 1)

                @block.vector
                def _(dve):
                    for c in range(DC):
                        dve.wait_ge(in_hi, c + 1)
                        dve.tensor_tensor(qin[1][:, c, :], xt[:, c, :], as_f32(qin[0][:, c, :]), ALU.subtract
                                          ).then_inc(in_lo, 1)
                    for c in range(DC):
                        dve.wait_ge(in_hi, DC + c + 1)
                        dve.tensor_tensor(cin[1][:, c, :], ctx_raw[:, c, :], as_f32(cin[0][:, c, :]), ALU.subtract
                                          ).then_inc(ctx_lo, 1)

        raw_kv, raw_q, raw_o = sb("raw_kv", [P, 2, DC, P]), sb("raw_q", [P, 2, DC, P]), sb("raw_o", [P, 2, D])
        w_kv = pair("w_kv", [P, 2, DC, P])
        w_q = [pair("w_q0", [P, 2, DC, P]), pair("w_q1", [P, 2, DC, P])]
        w_o = pair("w_o", [P, 2, D])
        q = [pair("q0", [P, T]), pair("q1", [P, T])]
        k, v = pair("k", [P, T]), pair("v", [P, B, P])
        rope = sb("rope", [P, 2, P])
        turned = [sb("turned0", [P, HALF]), sb("turned1", [P, HALF])]
        cross = [sb("cross0", [P, HALF]), sb("cross1", [P, HALF])]
        probs = [sb("probs0", [P, B, P]), sb("probs1", [P, B, P])]
        probs_t = pair("probs_t", [P, B, P])
        heads = pair("heads", [P, 2, T])
        mask = sb("mask", [P, B, P])
        top, row_sum, inv_sum = sb("top", [P, B]), sb("row_sum", [P, B]), sb("inv_sum", [P, B])

        mask_loaded, rope_loaded = sem("mask_loaded"), sem("rope_loaded")
        kv_loaded, kv_hi, kv_ready = sem("kv_loaded"), sem("kv_hi"), sem("kv_ready")
        q_loaded, q_hi, q_ready = sem("q_loaded"), sem("q_hi"), sem("q_ready")
        o_loaded, o_hi, o_ready = sem("o_loaded"), sem("o_hi"), sem("o_ready")
        ring_full, ring_drained, v_hi = sem("ring_full"), sem("ring_drained"), sem("v_hi")
        rope_sum, rope_hi, rope_low = sem("rope_sum"), sem("rope_hi"), sem("rope_low")
        scores_full, scores_read, top_raw, top_ready = (sem("scores_full"), sem("scores_read"), sem("top_raw"),
                                                        sem("top_ready"))
        exp_done, inv_done, probs_ready = sem("exp_done"), sem("inv_done"), sem("probs_ready")
        t_full, t_hi, t_drained = sem("t_full"), sem("t_hi"), sem("t_drained")
        h_full, h_hi, h_drained = sem("h_full"), sem("h_hi"), sem("h_drained")

        N = GROUPS
        PER = 28
        OFFSET = {"q1": 0, "v": 2, "out23": 4, "q2": 12, "q3": 14, "out01": 16, "k": 24, "q0": 26}

        def ring_at(g, what):
            first = isinstance(g, int) and g == 0 and what in ("q1", "v")
            return 4 + PER * g - 8 + OFFSET[what] + (8 if first else 0)

        OUT_LAST = ring_at(N - 1, "k")

        def rope_at(g, what):
            return 4 + 10 * g + {"q1": 0, "q2": 2, "q3": 4, "k": 6, "q0": 8}[what]

        def turns(body, eng):
            body(0, True, False)
            with eng.Fori(1, N - 1) as g:
                body(g, False, False)
            body(N - 1, False, True)

        with nc.Block() as block:

            @block.sync
            def _(sp):
                sp.dma_start(raw_kv[:, :, :, :], dram["L3_kv"][0, :, :, :, :]).then_inc(kv_loaded, 16)

                def load_q(n, g, s):
                    wait(sp, q_ready, n)
                    for j in range(2):
                        sp.dma_start(raw_q[:, j, :, :], dram["L3_q"][4 * g + 2 * s + j, :, :, :]).then_inc(q_loaded, 16)

                def load_o(u):
                    wait(sp, o_ready, u)
                    sp.dma_start(raw_o[:, :, :], dram["L3_o"][u, :, :, :]).then_inc(o_loaded, 16)

                load_q(0, 0, 0)
                sp.dma_start(rope[:, :, :], dram["L3_rope"]).then_inc(rope_loaded, 16)
                sp.dma_start(mask[:, :, :], dram["L3_mask"]).then_inc(mask_loaded, 16)
                load_q(1, 0, 1)

                def turn(g, first, last):
                    load_o(2 * g)
                    if not last:
                        sp.wait_ge(kv_ready, g + 1)
                        sp.dma_start(raw_kv[:, :, :, :], dram["L3_kv"][g + 1, :, :, :, :]).then_inc(kv_loaded, 16)
                        load_q(2 * g + 2, g + 1, 0)
                    load_o(2 * g + 1)
                    if not last:
                        load_q(2 * g + 3, g + 1, 1)

                turns(turn, sp)

            @block.gpsimd
            def _(pool):
                flat = lambda t: t[:, :, :].rearrange("p a b -> p (a b)")
                flat4 = lambda t: t[:, :, :, :].rearrange("p a b c -> p (a b c)")

                def split_low(n, raw, w, hi, ready):
                    f = flat4 if len(raw.shape) == 4 else flat
                    pool.wait_ge(hi, n + 1)
                    pool.tensor_tensor(f(w[1]), f(raw), as_f32(f(w[0])), ALU.subtract).then_inc(ready, 1)

                def rotate(ring, at, dst):
                    for n in range(2):
                        pool.wait_ge(ring_drained, ring + n + 1)
                        pool.tensor_tensor(turned[n][:, :], turned[n][:, :], cross[n][:, :], ALU.add
                                           ).then_inc(rope_sum, 1)
                    for n in range(2):
                        part = slice(n * HALF, (n + 1) * HALF)
                        pool.wait_ge(rope_hi, at + n + 1)
                        pool.tensor_tensor(dst[1][:, part], turned[n][:, :], as_f32(dst[0][:, part]), ALU.subtract
                                           ).then_inc(rope_low, 1)

                split_low(0, raw_kv, w_kv, kv_hi, kv_ready)
                split_low(0, raw_q, w_q[0], q_hi, q_ready)
                rotate(0, 0, k)
                rotate(2, 2, q[0])
                split_low(1, raw_q, w_q[1], q_hi, q_ready)

                def turn(g, first, last):
                    rotate(ring_at(g, "q1"), rope_at(g, "q1"), q[1])
                    if not last:
                        split_low(g + 1, raw_kv, w_kv, kv_hi, kv_ready)
                    rotate(ring_at(g, "q2"), rope_at(g, "q2"), q[0])
                    if not last:
                        split_low(2 * g + 2, raw_q, w_q[0], q_hi, q_ready)
                    split_low(2 * g, raw_o, w_o, o_hi, o_ready)
                    rotate(ring_at(g, "q3"), rope_at(g, "q3"), q[1])
                    if not last:
                        rotate(ring_at(g, "k"), rope_at(g, "k"), k)
                        rotate(ring_at(g, "q0"), rope_at(g, "q0"), q[0])
                        split_low(2 * g + 3, raw_q, w_q[1], q_hi, q_ready)
                    split_low(2 * g + 1, raw_o, w_o, o_hi, o_ready)

                turns(turn, pool)

            @block.tensor
            def _(pe):
                def project(at, bk, w, n_w, src):
                    for n in range(2):
                        wait(pe, ring_drained, at + n - 3)
                        part = slice(n * HALF, (n + 1) * HALF)
                        for c in range(DC):
                            mm = product(pe, bank[bk + n][:, :], [w[s][:, n_w, c, :] for s in range(2)],
                                         [src[s][:, c, part] for s in range(2)], c == 0, c == DC - 1)
                        mm.then_inc(ring_full, 1)

                def project_v(g):
                    at = ring_at(g, "v")
                    for n in range(2):
                        wait(pe, ring_drained, at + n - 3)
                        for y in range(BH):
                            b = n * BH + y
                            for c in range(DC):
                                mm = product(pe, bank[2 + n][:, y * P:(y + 1) * P],
                                             [cin[s][:, c, b * P:(b + 1) * P] for s in range(2)],
                                             [w_kv[s][:, 1, c, :] for s in range(2)], c == 0, c == DC - 1)
                        mm.then_inc(ring_full, 1)

                def scores(h, j, rotated):
                    pe.wait_ge(rope_low, rotated)
                    wait(pe, scores_read, 2 * h)
                    for half in range(2):
                        for y in range(BH):
                            t = slice((half * BH + y) * P, (half * BH + y + 1) * P)
                            mm = product(pe, bank[4 + half][:, y * P:(y + 1) * P],
                                         [q[j % 2][s][:, t] for s in range(2)], [k[s][:, t] for s in range(2)], True,
                                         True)
                        mm.then_inc(scores_full, 1)

                def transpose_probs(h, j):
                    pe.wait_ge(probs_ready, h + 1)
                    wait(pe, h_drained, 2 * h)
                    for half in range(2):
                        for y in range(BH):
                            mm = pe.transpose(bank[6 + half][:, y * P:(y + 1) * P], probs[j % 2][:, half * BH + y, :],
                                              core.ident[:, :])
                        mm.then_inc(t_full, 1)

                def weigh_values(h):
                    for half in range(2):
                        pe.wait_ge(t_drained, 2 * h + half + 1)
                        for y in range(BH):
                            b = half * BH + y
                            mm = product(pe, bank[6 + half][:, y * P:(y + 1) * P], [v[s][:, b, :] for s in range(2)],
                                         [probs_t[s][:, b, :] for s in range(2)], True, True)
                        mm.then_inc(h_full, 1)

                def project_out(u, at):
                    pe.wait_ge(o_ready, u + 1)
                    pe.wait_ge(h_drained, 4 * u + 4)
                    for b in range(B):
                        wait(pe, ring_drained, at + b - 3)
                        for j in range(2):
                            mm = product(pe, bank[b % 4][:, :], [heads[s][:, j, b * P:(b + 1) * P] for s in range(2)],
                                         [w_o[s][:, j, :] for s in range(2)], j == 0, j == 1)
                        mm.then_inc(ring_full, 1)

                pe.wait_ge(kv_ready, 1)
                project(0, 0, w_kv, 0, cin)
                pe.wait_ge(q_ready, 1)
                project(2, 2, w_q[0], 0, qin)

                def turn(g, first, last):
                    scores(G * g, 0, rope_at(g, "q1"))
                    project(ring_at(g, "q1"), 0, w_q[0], 1, qin)
                    if not first:
                        transpose_probs(G * g - 1, 3)
                        weigh_values(G * g - 1)
                    project_v(g)
                    if not first:
                        project_out(2 * g - 1, ring_at(g, "out23"))
                    scores(G * g + 1, 1, rope_at(g, "q1") + 2)
                    pe.wait_ge(q_ready, 2 * g + 2)
                    project(ring_at(g, "q2"), 0, w_q[1], 0, qin)
                    transpose_probs(G * g, 0)
                    pe.wait_ge(ring_drained, ring_at(g, "v") + 2)
                    weigh_values(G * g)
                    scores(G * g + 2, 2, rope_at(g, "q2") + 2)
                    project(ring_at(g, "q3"), 2, w_q[1], 1, qin)
                    transpose_probs(G * g + 1, 1)
                    weigh_values(G * g + 1)
                    project_out(2 * g, ring_at(g, "out01"))
                    scores(G * g + 3, 3, rope_at(g, "q3") + 2)
                    if not last:
                        pe.wait_ge(kv_ready, g + 2)
                        project(ring_at(g, "k"), 0, w_kv, 0, cin)
                        pe.wait_ge(q_ready, 2 * g + 3)
                        project(ring_at(g, "q0"), 2, w_q[0], 0, qin)
                    transpose_probs(G * g + 2, 2)
                    weigh_values(G * g + 2)

                turns(turn, pe)
                transpose_probs(G * N - 1, 3)
                weigh_values(G * N - 1)
                project_out(2 * N - 1, OUT_LAST)

            @block.scalar
            def _(act):
                def exps(h, j):
                    act.wait_ge(top_ready, h + 1)
                    wait(act, inv_done, h)
                    for b in range(B):
                        act.activation(probs[j % 2][:, b, :], probs[j % 2][:, b, :], ACT.Exp, bias=top[:, b:b + 1],
                                       accum_out=row_sum[:, b:b + 1]).then_inc(exp_done, 1)

                def split_high(n, raw, w, loaded, per, hi, free):
                    act.wait_ge(loaded, per * (n + 1))
                    wait(act, ring_full, free)
                    sl = tuple(slice(None) for _ in raw.shape)
                    act.activation(w[0][sl], raw[sl], ACT.Copy).then_inc(hi, 1)

                def rotated_high(at, dst, free):
                    wait(act, scores_full, free)
                    for n in range(2):
                        act.wait_ge(rope_sum, at + n + 1)
                        act.activation(dst[0][:, n * HALF:(n + 1) * HALF], turned[n][:, :], ACT.Copy
                                       ).then_inc(rope_hi, 1)

                def probs_high(h):
                    for half in range(2):
                        act.wait_ge(t_full, 2 * h + half + 1)
                        act.activation(probs_t[0][:, half * BH:(half + 1) * BH, :],
                                       bank[6 + half][:, :].rearrange("p (b n) -> p b n", b=BH), ACT.Copy
                                       ).then_inc(t_hi, 1)

                def heads_high(h, j):
                    for half in range(2):
                        act.wait_ge(h_full, 2 * h + half + 1)
                        act.activation(heads[0][:, j % 2, half * HALF:(half + 1) * HALF], bank[6 + half][:, :], ACT.Copy
                                       ).then_inc(h_hi, 1)

                def values_high(g):
                    wait(act, h_full, 2 * G * g)
                    for n in range(2):
                        act.wait_ge(ring_full, ring_at(g, "v") + n + 1)
                        act.activation(v[0][:, n * BH:(n + 1) * BH, :],
                                       bank[2 + n][:, :].rearrange("p (b n) -> p b n", b=BH), ACT.Copy).then_inc(v_hi, 1)

                split_high(0, raw_kv, w_kv, kv_loaded, 16, kv_hi, 0)
                split_high(0, raw_q, w_q[0], q_loaded, 32, q_hi, 0)
                rotated_high(0, k, 0)
                rotated_high(2, q[0], 0)
                split_high(1, raw_q, w_q[1], q_loaded, 32, q_hi, 0)

                def turn(g, first, last):
                    h = G * g
                    exps(h, 0)
                    rotated_high(rope_at(g, "q1"), q[1], 2 * h)
                    if not first:
                        probs_high(h - 1)
                        heads_high(h - 1, 3)
                    values_high(g)
                    if not last:
                        split_high(g + 1, raw_kv, w_kv, kv_loaded, 16, kv_hi, ring_at(g, "v") + 2)
                    exps(h + 1, 1)
                    rotated_high(rope_at(g, "q2"), q[0], 2 * h + 2)
                    probs_high(h)
                    if not last:
                        split_high(2 * g + 2, raw_q, w_q[0], q_loaded, 32, q_hi, ring_at(g, "q1") + 2)
                    split_high(2 * g, raw_o, w_o, o_loaded, 16, o_hi, 0 if first else ring_at(g, "out23") + 8)
                    heads_high(h, 0)
                    exps(h + 2, 2)
                    rotated_high(rope_at(g, "q3"), q[1], 2 * h + 4)
                    probs_high(h + 1)
                    heads_high(h + 1, 1)
                    exps(h + 3, 3)
                    if not last:
                        rotated_high(rope_at(g, "k"), k, 2 * h + 8)
                        rotated_high(rope_at(g, "q0"), q[0], 2 * h + 6)
                        split_high(2 * g + 3, raw_q, w_q[1], q_loaded, 32, q_hi, ring_at(g, "q3") + 2)
                    split_high(2 * g + 1, raw_o, w_o, o_loaded, 16, o_hi, ring_at(g, "out01") + 8)
                    probs_high(h + 2)
                    heads_high(h + 2, 2)

                turns(turn, act)
                probs_high(G * N - 1)
                heads_high(G * N - 1, 3)

            @block.vector
            def _(dve):
                def mask_scores(h, j):
                    if isinstance(h, int) and h == 0:
                        dve.wait_ge(mask_loaded, 16)
                    wait(dve, t_full, 2 * (h - 1))
                    for half in range(2):
                        part = slice(half * BH, (half + 1) * BH)
                        dve.wait_ge(scores_full, 2 * h + half + 1)
                        dve.scalar_tensor_tensor(probs[j % 2][:, part, :],
                                                 bank[4 + half][:, :].rearrange("p (b n) -> p b n", b=BH), SCALE,
                                                 mask[:, part, :], ALU.mult, ALU.add).then_inc(scores_read, 1)
                    dve.wait_ge(scores_read, 2 * h + 2)
                    wait(dve, exp_done, B * h)
                    dve.tensor_reduce(top[:, :], probs[j % 2][:, :, :], AX.X, ALU.max).then_inc(top_raw, 1)
                    dve.wait_ge(top_raw, h + 1)
                    dve.tensor_scalar(top[:, :], top[:, :], -1.0, None, ALU.mult).then_inc(top_ready, 1)

                def normalise(h, j):
                    dve.wait_ge(exp_done, B * (h + 1))
                    dve.reciprocal(inv_sum[:, :], row_sum[:, :]).then_inc(inv_done, 1)
                    dve.wait_ge(inv_done, h + 1)
                    dve.tensor_tensor(probs[j % 2][:, :, :], probs[j % 2][:, :, :],
                                      inv_sum[:, :].rearrange("p (b o) -> p b o", o=1).to_broadcast([P, B, P]),
                                      ALU.mult).then_inc(probs_ready, 1)

                def rotate(ring, at, bk):
                    table = lambda part, n: rope[part, n:n + 1, :].to_broadcast([part.stop - part.start, BH, P])
                    low, high, whole = slice(0, HP), slice(HP, P), slice(0, P)
                    for n in range(2):
                        src = bank[bk + n][:, :].rearrange("p (b t) -> p b t", b=BH)
                        cosine = turned[n][:, :].rearrange("p (b t) -> p b t", b=BH)
                        sine = cross[n][:, :].rearrange("p (b t) -> p b t", b=BH)
                        dve.wait_ge(ring_full, ring + n + 1)
                        wait(dve, rope_low, at + n - 1)
                        dve.tensor_tensor(cosine, src, table(whole, 0), ALU.mult)
                        dve.tensor_tensor(sine[high, :, :], src[low, :, :], table(low, 1), ALU.mult)
                        dve.tensor_tensor(sine[low, :, :], src[high, :, :], table(high, 1), ALU.mult
                                          ).then_inc(ring_drained, 1)

                def low(hi, at, dst, src, dst_hi, done):
                    dve.wait_ge(hi, at + 1)
                    dve.tensor_tensor(dst, src, as_f32(dst_hi), ALU.subtract).then_inc(done, 1)

                def probs_low(h):
                    for half in range(2):
                        part = slice(half * BH, (half + 1) * BH)
                        low(t_hi, 2 * h + half, probs_t[1][:, part, :],
                            bank[6 + half][:, :].rearrange("p (b n) -> p b n", b=BH), probs_t[0][:, part, :], t_drained)

                def heads_low(h, j):
                    for half in range(2):
                        part = slice(half * HALF, (half + 1) * HALF)
                        low(h_hi, 2 * h + half, heads[1][:, j % 2, part], bank[6 + half][:, :], heads[0][:, j % 2, part],
                            h_drained)

                def values_low(g):
                    for n in range(2):
                        part = slice(n * BH, (n + 1) * BH)
                        low(v_hi, 2 * g + n, v[1][:, part, :], bank[2 + n][:, :].rearrange("p (b n) -> p b n", b=BH),
                            v[0][:, part, :], ring_drained)

                def add_out(at):
                    for b in range(B):
                        dve.wait_ge(ring_full, at + b + 1)
                        dve.tensor_tensor(x[:, b, :], x[:, b, :], bank[b % 4][:, :], ALU.add).then_inc(ring_drained, 1)

                dve.wait_ge(rope_loaded, 16)
                rotate(0, 0, 0)
                rotate(2, 2, 2)

                def turn(g, first, last):
                    h = G * g
                    mask_scores(h, 0)
                    rotate(ring_at(g, "q1"), rope_at(g, "q1"), 0)
                    normalise(h, 0)
                    if not first:
                        probs_low(h - 1)
                        heads_low(h - 1, 3)
                    values_low(g)
                    if not first:
                        add_out(ring_at(g, "out23"))
                    mask_scores(h + 1, 1)
                    rotate(ring_at(g, "q2"), rope_at(g, "q2"), 0)
                    normalise(h + 1, 1)
                    probs_low(h)
                    heads_low(h, 0)
                    mask_scores(h + 2, 2)
                    rotate(ring_at(g, "q3"), rope_at(g, "q3"), 2)
                    normalise(h + 2, 2)
                    probs_low(h + 1)
                    heads_low(h + 1, 1)
                    add_out(ring_at(g, "out01"))
                    mask_scores(h + 3, 3)
                    if not last:
                        rotate(ring_at(g, "k"), rope_at(g, "k"), 0)
                        rotate(ring_at(g, "q0"), rope_at(g, "q0"), 2)
                    normalise(h + 3, 3)
                    probs_low(h + 2)
                    heads_low(h + 2, 2)

                turns(turn, dve)
                probs_low(G * N - 1)
                heads_low(G * N - 1, 3)
                add_out(OUT_LAST)


def build(nc, dram, out):
    ctx = ExitStack()
    with ctx:
        core = Core(nc, ctx)
        for layer in [l0_attention, l0_ffn, l1_attention, l1_ffn, l2_attention, l2_ffn, l3_attention, l3_ffn]:
            layer(core, dram)
            if layer is l1_ffn:
                core.free_semaphores()
        stored = core.sem("stored")
        with nc.Block() as block:

            @block.sync
            def _(sp):
                for b in range(B):
                    sp.dma_start(out[b, :, :], core.x[:, b, :]).then_inc(stored, 16)
                sp.wait_ge(stored, 16 * B)


def laid_out(inputs):
    a = {name: np.asarray(value) for name, value in inputs.items()}
    chunks = lambda w: w.reshape(DC, P, -1).transpose(1, 0, 2)
    got = {"x": a["x"]}
    got["ctx_t"] = chunks(a["ctx_4096"].reshape(T, D).T)
    got["mask_b_q"] = a["mask_BxSxS2_bk0"].transpose(1, 0, 2)
    got["L0_xattn_position_bias"] = a["L0_xattn_position_bias"]
    got["L0_xattn_ln_weight"] = a["L0_xattn_ln_weight"].reshape(DC, P).T
    qk = np.stack([a["L0_xattn_w_q"], a["L0_xattn_w_k"]]).reshape(2, 16, 2, P, DC, P)
    got["L0_qk"] = qk.transpose(1, 2, 5, 0, 4, 3)
    got["L0_v"] = a["L0_xattn_w_v"].reshape(16, 2 * P, DC, P).transpose(0, 3, 2, 1)
    got["L0_o"] = a["L0_xattn_w_out"].T.reshape(16, 2, P, D).transpose(0, 2, 1, 3)
    got["L0f_wq"] = chunks(a["L0_ffn_Wq"].T)
    got["L0f_keys"] = a["L0_ffn_lora_keys"].T
    got["L0f_down"] = chunks(a["L0_ffn_lora_down"].transpose(1, 0, 2).reshape(D, -1))
    got["L0f_org"] = chunks(a["L0_ffn_W_org"].T)
    got["L0f_up"] = chunks(a["L0_ffn_lora_up"].reshape(-1, D))
    got["L1x_wq"] = chunks(a["L1_xattn_Wq"].reshape(D, 8, 4, 16).transpose(0, 2, 1, 3).reshape(D, D))
    got["L1x_wkv"] = chunks(np.concatenate([a["L1_xattn_Wk"], a["L1_xattn_Wv"]], axis=1))
    got["L1x_wo"] = chunks(a["L1_xattn_Wo"].reshape(8, 4, 16, D).transpose(1, 0, 2, 3).reshape(D, D))
    got["L1f_wq"] = chunks(a["L1_ffn_Wq"].T)
    got["L1f_wr"] = a["L1_ffn_Wr"].T
    got["L1f_keys"] = a["L1_ffn_aux_keys"].T
    got["L1f_values"] = chunks(a["L1_ffn_aux_values"].T)
    got["L1f_wvd"] = chunks(a["L1_ffn_Wvd"].T)
    got["L1f_wvu"] = a["L1_ffn_Wvu"].T
    got["L1f_wu1"] = chunks(a["L1_ffn_Wu1"].T)
    got["L1f_wu2"] = a["L1_ffn_Wu2"].T
    on_all = [np.broadcast_to(a[n].reshape(1), (P,)) for n in ("L1_ffn_bu2", "L1_ffn_gate_w1", "L1_ffn_gate_bias")]
    got["L1f_consts"] = np.stack([a["L1_ffn_bu1"]] + on_all, axis=1)
    got["L1f_log_rel"] = np.broadcast_to(a["L1_ffn_log_rel"], (P, 1, P))
    got["l2f_a"] = chunks(np.concatenate([a["L2_ffn_lora_A"].reshape(P, D), a["L2_ffn_W_router"]]).T)
    got["l2f_b"] = a["L2_ffn_lora_B"].transpose(0, 2, 1).reshape(P, D)
    got["l2f_base"] = chunks(a["L2_ffn_W_base"].T)
    got["l2f_bias"] = np.broadcast_to(a["L2_ffn_b_base"], (P, D))
    got["l3f_a"] = chunks(np.concatenate([a["L3_ffn_A"].reshape(P, D), a["L3_ffn_route_w"]]).T)
    got["l3f_b"] = a["L3_ffn_Bw"].transpose(0, 2, 1).reshape(P, D)
    got["ctx_t_rev"] = chunks(a["ctx_4096"][:, ::-1, :].reshape(T, D).T)
    got["L2x_taps"] = np.repeat(a["L2_xattn_conv_w"][0], 16, axis=0)
    got["L2x_affine"] = np.broadcast_to(np.concatenate([a["L2_xattn_bn_gamma"], a["L2_xattn_bn_beta"]]), (16, 2))
    got["L3_q"] = a["L3_xattn_wq"].reshape(DC, P, 32, P).transpose(2, 1, 0, 3)
    got["L3_kv"] = np.stack([a["L3_xattn_wk"], a["L3_xattn_wv"]]).reshape(2, DC, P, 8, P).transpose(3, 2, 0, 1, 4)
    got["L3_o"] = a["L3_xattn_wo"].reshape(16, 2, P, D).transpose(0, 2, 1, 3)
    got["L3_mask"] = a["mask_BxSxS2_ff0"].transpose(1, 0, 2)
    angle = np.arange(P)[None, :] * (1.0 / 10000.0 ** (np.arange(0, P, 2) / P))[:, None]
    got["L3_rope"] = np.stack([np.tile(np.cos(angle), (2, 1)), np.concatenate([np.sin(angle), -np.sin(angle)])],
                              axis=1).astype(np.float32)
    return {name: np.ascontiguousarray(value) for name, value in got.items()}


def kernel(**inputs):
    import concourse.bacc as bacc
    from concourse.bass_utils import run_bass_kernel_spmd

    nc = bacc.Bacc("TRN2", target_bir_lowering=False, num_devices=1)
    arrays = laid_out(inputs)
    dram = {name: nc.dram_tensor(name + "_dram", a.shape, mybir.dt.from_np(a.dtype), kind="ExternalInput").ap()
            for name, a in arrays.items()}
    out = nc.dram_tensor("out_dram", (B, P, D), F32, kind="ExternalOutput").ap()
    build(nc, dram, out)
    result = run_bass_kernel_spmd(nc, [{name + "_dram": a for name, a in arrays.items()}], core_ids=[0])
    return result.results[0]["out_dram"]
```

```python
import numpy as np
import concourse.bass as bass
from concourse import mybir
from contextlib import ExitStack

F32 = mybir.dt.float32
F32R = mybir.dt.float32r
U8 = mybir.dt.uint8
ALU = mybir.AluOpType
ACT = mybir.ActivationFunctionType
AX = mybir.AxisListType

P = 128
B = 8
D = 512
DC = D // P
T = B * P
BH = B // 2
HALF = BH * P
EPS = 1e-5
MASKED = -1e30
FLOOR = -1e29


def wait(eng, sem, value):
    if not (isinstance(value, int) and value <= 0):
        eng.wait_ge(sem, value)


def product(pe, out, lhs, rhs, start, stop):
    if len(lhs) == 1:
        return pe.matmul(out, lhs[0], rhs[0], start=start, stop=stop)
    pe.matmul(out, lhs[0], rhs[0], start=start, stop=False)
    pe.matmul(out, lhs[0], rhs[1], start=False, stop=False)
    return pe.matmul(out, lhs[1], rhs[0], start=False, stop=stop)


def as_f32(ap):
    return ap.bitcast(F32)


class Core:

    def __init__(self, nc, ctx):
        self.nc, self.ctx = nc, ctx
        self.held = []
        self.x = self.sb(ctx, "x", [P, B, D])
        self.ident = self.sb(ctx, "ident", [P, P])
        self.neg_half = self.sb(ctx, "neg_half", [P, B])
        self.stats = self.sb(ctx, "stats", [P, B, 6])
        self.mv = self.sb(ctx, "mv", [P, B, 2])
        self.var_eps = self.sb(ctx, "var_eps", [P, B])
        self.rstd = self.sb(ctx, "rstd", [P, B])
        self.crucial = self.sb(ctx, "crucial", [P, DC * B, P], U8)
        self.bank = [ctx.enter_context(nc.psum_tensor(f"bank{n}", [P, 512], F32)) for n in range(8)]
        self.x_loaded = self.sem("x_loaded")
        self.const_ready = self.sem("const_ready")
        self.stats_done = self.sem("stats_done")
        self.mv_done = self.sem("mv_done")
        self.var_done = self.sem("var_done")
        self.rstd_done = self.sem("rstd_done")
        self.xn_done = self.sem("xn_done")
        self.xt_full = self.sem("xt_full")
        self.xt_copied = self.sem("xt_copied")
        self.norms = 0
        self.held = []

    def hold_first(self, ctx):
        self.cin = self.pair(ctx, "ctx", [P, DC, T])
        self.l1_loaded, self.l1_hi, self.l1_split = self.sem("l1_loaded"), self.sem("l1_hi"), self.sem("l1_split")

    def hold_weights(self, ctx):
        self.l1_wq, self.l1_wkv = self.pair(ctx, "l1_wq", [P, DC, D]), self.pair(ctx, "l1_wkv", [P, DC, 2 * P])
        self.l1_wo = self.pair(ctx, "l1_wo", [P, L1_QUERIES, D])

    def sb(self, ctx, name, shape, dt=F32):
        return ctx.enter_context(self.nc.sbuf_tensor(name, shape, dt))

    def pair(self, ctx, name, shape):
        return (self.sb(ctx, name + "_hi", shape, F32R), self.sb(ctx, name + "_lo", shape, F32R))

    def sem(self, name):
        handle = self.nc.alloc_semaphore(name=name)
        self.held.append(handle)
        return handle

    def free_semaphores(self):
        self.nc.all_engine_barrier()
        self.nc.clear_and_free_semaphores(self.held)
        self.nc.all_engine_barrier()
        self.held = []


def norm_stage(core, xn, xt, loads):
    nc, n = core.nc, core.norms
    core.norms += 1
    with nc.Block() as block:

        @block.sync
        def _(sp):
            loads(sp)

        @block.vector
        def _(dve):
            for b in range(B):
                dve.bn_stats(core.stats[:, b, :], core.x[:, b, :]).then_inc(core.stats_done, 1)
            dve.wait_ge(core.stats_done, B * (n + 1))
            for b in range(B):
                dve.bn_aggr(core.mv[:, b, :], core.stats[:, b, :]).then_inc(core.mv_done, 1)
            dve.wait_ge(core.mv_done, B * (n + 1))
            dve.tensor_scalar_add(core.var_eps[:, :], core.mv[:, :, 1], EPS).then_inc(core.var_done, 1)
            dve.wait_ge(core.rstd_done, n + 1)
            for b in range(B):
                dve.tensor_scalar(xn[:, b, :], core.x[:, b, :], core.mv[:, b, 0:1], core.rstd[:, b:b + 1],
                                  ALU.subtract, ALU.mult).then_inc(core.xn_done, 1)
            for b in range(1, B, 2):
                dve.wait_ge(core.xt_full, B * n + b + 1)
                dve.tensor_copy(xt[:, :, b * P:(b + 1) * P], core.bank[b][:, :].rearrange("p (c t) -> p c t", c=DC)
                                ).then_inc(core.xt_copied, 1)

        @block.gpsimd
        def _(pool):
            pool.wait_ge(core.var_done, n + 1)
            pool.tensor_tensor(core.rstd[:, :], core.var_eps[:, :], core.neg_half[:, :], ALU.pow
                               ).then_inc(core.rstd_done, 1)

        @block.tensor
        def _(pe):
            for b in range(B):
                pe.wait_ge(core.xn_done, B * n + b + 1)
                for c in range(DC):
                    last = pe.transpose(core.bank[b][:, c * P:(c + 1) * P], xn[:, b, c * P:(c + 1) * P],
                                        core.ident[:, :])
                last.then_inc(core.xt_full, 1)

        @block.scalar
        def _(act):
            for b in range(0, B, 2):
                act.wait_ge(core.xt_full, B * n + b + 1)
                act.activation(xt[:, :, b * P:(b + 1) * P], core.bank[b][:, :].rearrange("p (c t) -> p c t", c=DC),
                               ACT.Copy).then_inc(core.xt_copied, 1)


L0_HEADS = 32
L0_PAIRS = L0_HEADS // 2
CRUCIAL = 76
OTHERS = P - CRUCIAL
ROUNDS, REST = OTHERS // 8, OTHERS % 8
TAKEN = -3e38
TILES = DC * B
TPT = TILES // L0_PAIRS


def l0_attention(core, dram):
    nc, x, bank = core.nc, core.x, core.bank
    with ExitStack() as ctx:
        sb = lambda name, shape, dt=F32: core.sb(ctx, "l0x_" + name, shape, dt)
        pair = lambda name, shape: core.pair(ctx, "l0x_" + name, shape)
        sem = lambda name: core.sem("l0x_" + name)

        qin = pair("qin", [P, DC, T])
        cin = core.cin
        w_qk = [pair("w_qk0", [P, 2, DC, P]), pair("w_qk1", [P, 2, DC, P])]
        w_v = pair("w_v", [P, DC, 2 * P])
        w_o = pair("w_o", [P, 2, D])

        with ExitStack() as ctx1:
            h = core.sb(ctx1, "l0x_h", [P, B, D])
            xr = core.sb(ctx1, "l0x_xr", [P, B, D])
            ctx_raw = core.sb(ctx1, "l0x_ctx_raw", [P, DC, T])
            lnw = core.sb(ctx1, "l0x_lnw", [P, DC])
            ms = core.sb(ctx1, "l0x_ms", [P, B])
            r2 = core.sb(ctx1, "l0x_r2", [P, B])
            ctx_loaded, lnw_loaded = sem("ctx_loaded"), sem("lnw_loaded")
            h_done, added = sem("h_done"), sem("added")
            ms1, ms2, r2_done = sem("ms1"), sem("ms2"), sem("r2_done")
            xt_hi, ctx_hi, ctx_lo = sem("xt_hi"), sem("ctx_hi"), sem("ctx_lo")
            cst = sem("cst")
            with nc.Block() as block:

                @block.sync
                def _(sp):
                    for b in range(B):
                        sp.dma_start(x[:, b, :], dram["x"][b, :, :]).then_inc(core.x_loaded, 16)
                    sp.dma_start(lnw[:, :], dram["L0_xattn_ln_weight"]).then_inc(lnw_loaded, 16)
                    sp.dma_start(ctx_raw[:, :, :], dram["ctx_t"]).then_inc(ctx_loaded, 16)

                @block.gpsimd
                def _(pool):
                    pool.memset(core.neg_half[:, :], -0.5).then_inc(core.const_ready, 1)
                    pool.memset(core.ident[:, :], 0.0).then_inc(cst, 1)
                    pool.wait_ge(cst, 1)
                    pool.affine_select(out=core.ident[:, :], in_=core.ident[:, :], compare_op=ALU.not_equal, fill=1.0,
                                       base=0, pattern=[[-1, P]], channel_multiplier=1).then_inc(core.const_ready, 1)
                    pool.wait_ge(core.const_ready, 2)
                    pool.wait_ge(core.var_done, 1)
                    pool.tensor_tensor(core.rstd[:, :], core.var_eps[:, :], core.neg_half[:, :], ALU.pow
                                       ).then_inc(core.rstd_done, 1)
                    pool.wait_ge(ms2, 1)
                    pool.tensor_tensor(r2[:, :], ms[:, :], core.neg_half[:, :], ALU.pow).then_inc(r2_done, 1)
                    for b in range(B):
                        pool.wait_ge(h_done, b + 1)
                        pool.tensor_tensor(x[:, b, :], x[:, b, :], h[:, b, :], ALU.add).then_inc(added, 1)
                    for c in range(DC):
                        pool.wait_ge(ctx_hi, c + 1)
                        pool.tensor_tensor(cin[1][:, c, :], ctx_raw[:, c, :], as_f32(cin[0][:, c, :]), ALU.subtract
                                           ).then_inc(ctx_lo, 1)

                @block.vector
                def _(dve):
                    for b in range(B):
                        dve.wait_ge(core.x_loaded, 16 * B)
                        dve.bn_stats(core.stats[:, b, :], x[:, b, :]).then_inc(core.stats_done, 1)
                    dve.wait_ge(core.stats_done, B)
                    for b in range(B):
                        dve.bn_aggr(core.mv[:, b, :], core.stats[:, b, :]).then_inc(core.mv_done, 1)
                    dve.wait_ge(core.mv_done, B)
                    dve.tensor_scalar_add(core.var_eps[:, :], core.mv[:, :, 1], EPS).then_inc(core.var_done, 1)
                    dve.wait_ge(core.rstd_done, 1)
                    dve.tensor_tensor(ms[:, :], core.mv[:, :, 1], core.rstd[:, :], ALU.mult).then_inc(ms1, 1)
                    for b in range(B):
                        dve.tensor_scalar(h[:, b, :], x[:, b, :], core.mv[:, b, 0:1], core.rstd[:, b:b + 1],
                                          ALU.subtract, ALU.mult).then_inc(h_done, 1)
                    dve.wait_ge(ms1, 1)
                    dve.tensor_tensor(ms[:, :], ms[:, :], core.rstd[:, :], ALU.mult).then_inc(ms1, 1)
                    dve.wait_ge(ms1, 2)
                    dve.tensor_scalar_add(ms[:, :], ms[:, :], EPS).then_inc(ms2, 1)
                    dve.wait_ge(r2_done, 1)
                    dve.wait_ge(h_done, B)
                    for b in range(B):
                        dve.tensor_scalar(xr[:, b, :], h[:, b, :], r2[:, b:b + 1], None, ALU.mult
                                          ).then_inc(core.xn_done, 1)
                    dve.wait_ge(lnw_loaded, 16)
                    for b in range(B):
                        dve.wait_ge(xt_hi, b + 1)
                        for c in range(DC):
                            last = dve.scalar_tensor_tensor(
                                qin[1][:, c, b * P:(b + 1) * P], bank[b][:, c * P:(c + 1) * P], lnw[:, c:c + 1],
                                as_f32(qin[0][:, c, b * P:(b + 1) * P]), ALU.mult, ALU.subtract)
                        last.then_inc(core.xt_copied, 1)

                @block.tensor
                def _(pe):
                    pe.wait_ge(core.const_ready, 2)
                    for b in range(B):
                        pe.wait_ge(core.xn_done, b + 1)
                        for c in range(DC):
                            last = pe.transpose(bank[b][:, c * P:(c + 1) * P], xr[:, b, c * P:(c + 1) * P],
                                                core.ident[:, :])
                        last.then_inc(core.xt_full, 1)

                @block.scalar
                def _(act):
                    act.wait_ge(lnw_loaded, 16)
                    for b in range(B):
                        act.wait_ge(core.xt_full, b + 1)
                        for c in range(DC):
                            last = act.activation(qin[0][:, c, b * P:(b + 1) * P], bank[b][:, c * P:(c + 1) * P],
                                                  ACT.Copy, scale=lnw[:, c:c + 1])
                        last.then_inc(xt_hi, 1)
                    act.wait_ge(ctx_loaded, 16)
                    for c in range(DC):
                        act.activation(cin[0][:, c, :], ctx_raw[:, c, :], ACT.Copy).then_inc(ctx_hi, 1)
            core.norms += 1

        raw_qk = [sb("raw_qk0", [P, 2, DC, P]), sb("raw_qk1", [P, 2, DC, P])]
        raw_v, raw_o = sb("raw_v", [P, DC, 2 * P]), sb("raw_o", [P, 2, D])
        q, k = sb("q", [P, T]), sb("k", [P, T])
        v = sb("v", [P, B, 2 * P])
        probs = [sb("probs0", [P, B, P]), sb("probs1", [P, B, P])]
        probs_t = sb("probs_t", [P, B, P])
        heads = pair("heads", [P, 2, T])
        bias = sb("bias", [P, 2, P])
        comb = sb("comb", [P, B, P])
        mask_u8, neg = sb("mask_u8", [P, B, P], U8), sb("neg", [P, B, P])
        top, row_sum, inv_sum = sb("top", [P, B]), sb("row_sum", [P, B]), sb("inv_sum", [P, B])
        idle = sb("idle", [P, 1])
        work, top8 = sb("work", [P, TPT, P]), sb("top8", [P, TPT, 8])

        mask_loaded, neg_ready = sem("mask_loaded"), sem("neg_ready")
        bias_loaded = [sem("bias_loaded0"), sem("bias_loaded1")]
        comb_ready = sem("comb_ready")
        qk_loaded, qk_hi, qk_ready = ([sem(f"{s}{j}") for j in range(2)] for s in ("qk_loaded", "qk_hi", "qk_ready"))
        v_loaded, v_hi, v_ready = sem("v_loaded"), sem("v_hi"), sem("v_ready")
        o_loaded, o_hi, o_ready = sem("o_loaded"), sem("o_hi"), sem("o_ready")
        ring_full, ring_drained = sem("ring_full"), sem("ring_drained")
        scores_full, scores_read, top_raw, top_ready = (sem("scores_full"), sem("scores_read"), sem("top_raw"),
                                                        sem("top_ready"))
        exp_done, sum_ok, inv_done, probs_ready = sem("exp_done"), sem("sum_ok"), sem("inv_done"), sem("probs_ready")
        t_full, t_act, t_dve = sem("t_full"), sem("t_act"), sem("t_dve")
        h_full, h_hi, h_drained = sem("h_full"), sem("h_hi"), sem("h_drained")
        work_loaded, rank_step, ranked = sem("work_loaded"), sem("rank_step"), sem("ranked")

        N = L0_PAIRS
        PER = 20
        OFFSET = {"q1": 0, "k1": 2, "v": 4, "out": 8, "q0": 16, "k0": 18}

        def ring_at(i, what):
            first = isinstance(i, int) and i == 0 and what in ("q1", "k1", "v")
            return 4 + PER * i - 8 + OFFSET[what] + (8 if first else 0)

        OUT_LAST = ring_at(N - 1, "q0")

        def turns(body, eng):
            body(0, True, False)
            with eng.Fori(1, N - 1) as i:
                body(i, False, False)
            body(N - 1, False, True)

        with nc.Block() as block:

            @block.sync
            def _(sp):
                def load_qk(i, j):
                    wait(sp, qk_ready[j], i)
                    sp.dma_start(raw_qk[j][:, :, :, :], dram["L0_qk"][i, j, :, :, :, :]).then_inc(qk_loaded[j], 16)

                def load_bias(i, j):
                    wait(sp, comb_ready, 2 * i + j - 1)
                    sp.dma_start(bias[:, j, :], dram["L0_xattn_position_bias"][2 * i + j, :, :]
                                 ).then_inc(bias_loaded[j], 16)

                def load_v(i):
                    wait(sp, v_ready, i)
                    sp.dma_start(raw_v[:, :, :], dram["L0_v"][i, :, :, :]).then_inc(v_loaded, 16)

                load_qk(0, 0)
                sp.dma_start(mask_u8[:, :, :], dram["mask_b_q"]).then_inc(mask_loaded, 16)
                load_bias(0, 0)
                load_qk(0, 1)
                load_v(0)

                def turn(i, first, last):
                    wait(sp, ranked, i)
                    sp.dma_start(work[:, :, :], dram["ctx_rank"][i, :, :, :]).then_inc(work_loaded, 16)
                    load_bias(i, 1)
                    if not last:
                        load_qk(i + 1, 0)
                        load_bias(i + 1, 0)
                    wait(sp, o_ready, i)
                    sp.dma_start(raw_o[:, :, :], dram["L0_o"][i, :, :, :]).then_inc(o_loaded, 16)
                    if not last:
                        load_qk(i + 1, 1)
                        load_v(i + 1)

                turns(turn, sp)

            @block.gpsimd
            def _(pool):
                flat = lambda t: t[:, :, :].rearrange("p a b -> p (a b)")
                flat4 = lambda t: t[:, :, :, :].rearrange("p a b c -> p (a b c)")

                def split_low(i, raw, w, hi, ready):
                    f = flat4 if len(raw.shape) == 4 else flat
                    pool.wait_ge(hi, i + 1)
                    pool.tensor_tensor(f(w[1]), f(raw), as_f32(f(w[0])), ALU.subtract).then_inc(ready, 1)

                def combine(i, j):
                    pool.wait_ge(bias_loaded[j], 16 * (i + 1))
                    wait(pool, scores_read, 2 * (2 * i + j))
                    pool.tensor_tensor(comb[:, :, :], neg[:, :, :], bias[:, j:j + 1, :].to_broadcast([P, B, P]),
                                       ALU.add).then_inc(comb_ready, 1)

                split_low(0, raw_qk[0], w_qk[0], qk_hi[0], qk_ready[0])
                pool.wait_ge(mask_loaded, 16)
                pool.tensor_copy(comb[:, :, :], mask_u8[:, :, :]).then_inc(neg_ready, 1)
                pool.wait_ge(neg_ready, 1)
                pool.tensor_scalar(neg[:, :, :], comb[:, :, :], 1.0, -MASKED, ALU.subtract, ALU.mult
                                   ).then_inc(neg_ready, 1)
                pool.wait_ge(neg_ready, 2)
                combine(0, 0)
                split_low(0, raw_qk[1], w_qk[1], qk_hi[1], qk_ready[1])
                split_low(0, raw_v, w_v, v_hi, v_ready)

                def turn(i, first, last):
                    combine(i, 1)
                    if not last:
                        split_low(i + 1, raw_qk[0], w_qk[0], qk_hi[0], qk_ready[0])
                        combine(i + 1, 0)
                        split_low(i + 1, raw_qk[1], w_qk[1], qk_hi[1], qk_ready[1])
                        split_low(i + 1, raw_v, w_v, v_hi, v_ready)
                    split_low(i, raw_o, w_o, o_hi, o_ready)

                turns(turn, pool)

            @block.tensor
            def _(pe):
                def project(n, at, bk, w, n_w, src):
                    wait(pe, ring_drained, at + n - 3)
                    part = slice(n * HALF, (n + 1) * HALF)
                    for c in range(DC):
                        mm = product(pe, bank[bk + n][:, :], [w[s][:, n_w, c, :] for s in range(2)],
                                     [src[s][:, c, part] for s in range(2)], c == 0, c == DC - 1)
                    mm.then_inc(ring_full, 1)

                def project_v(i):
                    pe.wait_ge(v_ready, i + 1)
                    for m in range(4):
                        wait(pe, ring_drained, ring_at(i, "v") + m - 3)
                        for b in (2 * m, 2 * m + 1):
                            for c in range(DC):
                                mm = product(pe, bank[m][:, (b % 2) * 2 * P:(b % 2 + 1) * 2 * P],
                                             [cin[s][:, c, b * P:(b + 1) * P] for s in range(2)],
                                             [w_v[s][:, c, :] for s in range(2)], c == 0, c == DC - 1)
                        mm.then_inc(ring_full, 1)

                def scores(h, needed):
                    pe.wait_ge(ring_drained, needed)
                    wait(pe, scores_read, 2 * h)
                    for half in range(2):
                        for y in range(BH):
                            t = slice((half * BH + y) * P, (half * BH + y + 1) * P)
                            mm = product(pe, bank[4 + half][:, y * P:(y + 1) * P], [q[:, t]], [k[:, t]], True, True)
                        mm.then_inc(scores_full, 1)

                def transpose_probs(h, j):
                    pe.wait_ge(probs_ready, h + 1)
                    wait(pe, h_drained, 2 * h)
                    for half in range(2):
                        for y in range(BH):
                            mm = pe.transpose(bank[6 + half][:, y * P:(y + 1) * P], probs[j][:, half * BH + y, :],
                                              core.ident[:, :])
                        mm.then_inc(t_full, 1)

                def weigh_values(h, j):
                    for half in range(2):
                        pe.wait_ge((t_act, t_dve)[half], h + 1)
                        for y in range(BH):
                            b = half * BH + y
                            mm = product(pe, bank[6 + half][:, y * P:(y + 1) * P], [v[:, b, j * P:(j + 1) * P]],
                                         [probs_t[:, b, :]], True, True)
                        mm.then_inc(h_full, 1)

                def project_out(i, at):
                    pe.wait_ge(o_ready, i + 1)
                    pe.wait_ge(h_drained, 4 * i + 4)
                    for b in range(B):
                        wait(pe, ring_drained, at + b - 3)
                        for j in range(2):
                            mm = product(pe, bank[b % 4][:, :], [heads[s][:, j, b * P:(b + 1) * P] for s in range(2)],
                                         [w_o[s][:, j, :] for s in range(2)], j == 0, j == 1)
                        mm.then_inc(ring_full, 1)

                def step(h, j, needed, at, project_next, weigh_last):
                    scores(h, needed)
                    if weigh_last:
                        transpose_probs(h - 1, 1 - j)
                    if project_next:
                        project(0, at, 0, w_qk[1 - j], 0, qin)
                    if weigh_last:
                        weigh_values(h - 1, 1 - j)
                    if project_next:
                        project(1, at, 0, w_qk[1 - j], 0, qin)
                        for n in range(2):
                            project(n, at + 2, 2, w_qk[1 - j], 1, cin)

                pe.wait_ge(qk_ready[0], 1)
                for n in range(2):
                    project(n, 0, 0, w_qk[0], 0, qin)
                for n in range(2):
                    project(n, 2, 2, w_qk[0], 1, cin)

                def turn(i, first, last):
                    pe.wait_ge(qk_ready[1], i + 1)
                    step(2 * i, 0, 4 if first else ring_at(i, "q1"), ring_at(i, "q1"), True, not first)
                    project_v(i)
                    if not first:
                        project_out(i - 1, ring_at(i, "out"))
                    if not last:
                        pe.wait_ge(qk_ready[0], i + 2)
                    step(2 * i + 1, 1, ring_at(i, "v") + 4, ring_at(i, "q0"), not last,
                         True)

                turns(turn, pe)
                transpose_probs(2 * N - 1, 1)
                weigh_values(2 * N - 1, 1)
                project_out(N - 1, OUT_LAST)

            @block.scalar
            def _(act):
                def exps(h, j):
                    act.wait_ge(top_ready, h + 1)
                    wait(act, inv_done, h)
                    for b in range(B):
                        act.activation(probs[j][:, b, :], probs[j][:, b, :], ACT.Exp, bias=top[:, b:b + 1],
                                       accum_out=row_sum[:, b:b + 1]).then_inc(exp_done, 1)

                def split_high(i, raw, w, loaded, hi, free):
                    act.wait_ge(loaded, 16 * (i + 1))
                    wait(act, ring_full, free)
                    sl = tuple(slice(None) for _ in raw.shape)
                    act.activation(w[0][sl], raw[sl], ACT.Copy).then_inc(hi, 1)

                def copy_probs(h):
                    act.wait_ge(t_full, 2 * h + 1)
                    act.activation(probs_t[:, 0:BH, :], bank[6][:, :].rearrange("p (b n) -> p b n", b=BH), ACT.Copy
                                   ).then_inc(t_act, 1)

                def heads_high(h, j):
                    for half in range(2):
                        act.wait_ge(h_full, 2 * h + half + 1)
                        act.activation(heads[0][:, j, half * HALF:(half + 1) * HALF], bank[6 + half][:, :], ACT.Copy
                                       ).then_inc(h_hi, 1)

                split_high(0, raw_qk[0], w_qk[0], qk_loaded[0], qk_hi[0], 0)
                split_high(0, raw_qk[1], w_qk[1], qk_loaded[1], qk_hi[1], 0)
                split_high(0, raw_v, w_v, v_loaded, v_hi, 0)

                def turn(i, first, last):
                    if not first:
                        copy_probs(2 * i - 1)
                    exps(2 * i, 0)
                    if not first:
                        heads_high(2 * i - 1, 1)
                    if not last:
                        split_high(i + 1, raw_qk[0], w_qk[0], qk_loaded[0], qk_hi[0], 4 if first else ring_at(i, "q1"))
                        split_high(i + 1, raw_qk[1], w_qk[1], qk_loaded[1], qk_hi[1], ring_at(i, "k1") + 2)
                        split_high(i + 1, raw_v, w_v, v_loaded, v_hi, ring_at(i, "v") + 4)
                    split_high(i, raw_o, w_o, o_loaded, o_hi, 0 if first else ring_at(i, "out") + 8)
                    copy_probs(2 * i)
                    exps(2 * i + 1, 1)
                    heads_high(2 * i, 0)

                turns(turn, act)
                copy_probs(2 * N - 1)
                heads_high(2 * N - 1, 1)

            @block.vector
            def _(dve):
                def add_bias(h, j):
                    dve.wait_ge(comb_ready, h + 1)
                    wait(dve, t_full, 2 * (h - 1))
                    for half in range(2):
                        part = slice(half * BH, (half + 1) * BH)
                        dve.wait_ge(scores_full, 2 * h + half + 1)
                        dve.tensor_tensor(probs[j][:, part, :], bank[4 + half][:, :].rearrange("p (b n) -> p b n", b=BH),
                                          comb[:, part, :], ALU.add).then_inc(scores_read, 1)
                    dve.wait_ge(scores_read, 2 * h + 2)
                    wait(dve, exp_done, B * h)
                    dve.tensor_reduce(top[:, :], probs[j][:, :, :], AX.X, ALU.max).then_inc(top_raw, 1)
                    dve.wait_ge(top_raw, h + 1)
                    dve.tensor_scalar(top[:, :], top[:, :], FLOOR, -1.0, ALU.max, ALU.mult).then_inc(top_ready, 1)

                def normalise(h, j):
                    dve.wait_ge(exp_done, B * (h + 1))
                    dve.tensor_scalar_max(inv_sum[:, :], row_sum[:, :], 1e-30).then_inc(sum_ok, 1)
                    dve.wait_ge(sum_ok, h + 1)
                    dve.reciprocal(inv_sum[:, :], inv_sum[:, :]).then_inc(inv_done, 1)
                    dve.wait_ge(inv_done, h + 1)
                    dve.tensor_tensor(probs[j][:, :, :], probs[j][:, :, :],
                                      inv_sum[:, :].rearrange("p (b o) -> p b o", o=1).to_broadcast([P, B, P]),
                                      ALU.mult).then_inc(probs_ready, 1)

                def drain(at, dst, bk):
                    dve.wait_ge(ring_full, at + 1)
                    dve.tensor_copy(dst, bank[bk][:, :].rearrange("p (b n) -> p b n", b=dst.shape[1])
                                    if len(dst.shape) == 3 else bank[bk][:, :]).then_inc(ring_drained, 1)

                def drain_half(n, at, dst, bk):
                    drain(at + n, dst[:, n * HALF:(n + 1) * HALF], bk + n)

                def copy_probs(h):
                    dve.wait_ge(t_full, 2 * h + 2)
                    dve.tensor_copy(probs_t[:, BH:B, :], bank[7][:, :].rearrange("p (b n) -> p b n", b=BH)
                                    ).then_inc(t_dve, 1)

                def heads_low(h, j):
                    for half in range(2):
                        part = slice(half * HALF, (half + 1) * HALF)
                        dve.wait_ge(h_hi, 2 * h + half + 1)
                        dve.tensor_tensor(heads[1][:, j, part], bank[6 + half][:, :], as_f32(heads[0][:, j, part]),
                                          ALU.subtract).then_inc(h_drained, 1)

                def add_out(at):
                    for b in range(B):
                        dve.wait_ge(ring_full, at + b + 1)
                        dve.tensor_tensor(x[:, b, :], x[:, b, :], bank[b % 4][:, :], ALU.add).then_inc(ring_drained, 1)

                def steps_before(i, r):
                    return (ROUNDS + 1) * 2 * TPT * i + 2 * TPT * r + (TPT + 1) * i

                def rank_start(i):
                    dve.wait_ge(work_loaded, 16 * (i + 1))
                    dve.tensor_scalar(work[:, :, :], work[:, :, :], -1.0, None, ALU.mult).then_inc(rank_step, 1)

                def rank_settle(steps):
                    dve.wait_ge(rank_step, steps)
                    dve.memset(idle[:, :], 0.0)

                def rank_round(i, r):
                    at = steps_before(i, r) + 1
                    rank_settle(at)
                    for n in range(TPT):
                        dve.max(top8[:, n, :], work[:, n, :]).then_inc(rank_step, 1)
                    rank_settle(at + TPT)
                    if r == ROUNDS:
                        for n in range(TPT):
                            dve.memset(top8[:, n, REST:8], TAKEN).then_inc(rank_step, 1)
                        at += TPT
                        rank_settle(at + TPT)
                    for n in range(TPT):
                        dve.match_replace(work[:, n, :], top8[:, n, :], work[:, n, :], TAKEN).then_inc(rank_step, 1)

                def rank_end(i):
                    dve.wait_ge(rank_step, steps_before(i + 1, 0))
                    dve.tensor_scalar(core.crucial[:, bass.ds(TPT * i, TPT), :], work[:, :, ::-1], TAKEN, None,
                                      ALU.not_equal).then_inc(ranked, 1)

                def step(h, j, at, drain_next, weigh_last, i, r):
                    add_bias(h, j)
                    if weigh_last:
                        copy_probs(h - 1)
                    if drain_next:
                        drain_half(0, at, q, 0)
                    if weigh_last:
                        heads_low(h - 1, 1 - j)
                    if drain_next:
                        drain_half(1, at, q, 0)
                    rank_round(i, r)
                    normalise(h, j)
                    if drain_next:
                        drain_half(0, at + 2, k, 2)
                        drain_half(1, at + 2, k, 2)
                    rank_round(i, r + 1)

                for n in range(2):
                    drain_half(n, 0, q, 0)
                for n in range(2):
                    drain_half(n, 2, k, 2)

                def turn(i, first, last):
                    rank_start(i)
                    step(2 * i, 0, ring_at(i, "q1"), True, not first, i, 0)
                    for m in range(4):
                        drain(ring_at(i, "v") + m, v[:, 2 * m:2 * m + 2, :], m)
                        if m % 2:
                            rank_round(i, 2 + m // 2)
                    if not first:
                        add_out(ring_at(i, "out"))
                    step(2 * i + 1, 1, ring_at(i, "q0"), not last, True, i, 4)
                    rank_round(i, 6)
                    rank_end(i)

                turns(turn, dve)
                copy_probs(2 * N - 1)
                heads_low(2 * N - 1, 1)
                add_out(OUT_LAST)


def l0_ffn(core, dram):
    nc, x, bank = core.nc, core.x, core.bank
    E, R, EC = 8, 64, 4
    with ExitStack() as ctx:
        sb = lambda name, shape, dt=F32: core.sb(ctx, "l0f_" + name, shape, dt)
        sem = lambda name: core.sem("l0f_" + name)
        xn, xt = sb("xn", [P, B, D]), sb("xt", [P, DC, T])
        w_q, keys = sb("w_q", [P, DC, P]), sb("keys", [P, E])
        w_down, w_org, w_up = sb("w_down", [P, DC, E * R]), sb("w_org", [P, DC, D]), sb("w_up", [P, EC, D])
        h = sb("h", [P, EC, T])
        y_sum, query = sb("y_sum", [P, DC, B]), sb("query", [P, B])
        top, total, inv = sb("top", [B, 1]), sb("total", [B, 1]), sb("inv", [B, 1])
        exps, coef = sb("exps", [B, E]), sb("coef", [B, E, R])
        coef_t = sb("coef_t", [P, EC, B])
        q_loaded, down_loaded, out_loaded = sem("q_loaded"), sem("down_loaded"), sem("out_loaded")

        next_raw = [sb("next_kv", [P, DC, 2 * P]), sb("next_q", [P, DC, D]), sb("next_o", [P, L1_QUERIES, D])]
        next_weights = (core.l1_wkv, core.l1_wq, core.l1_wo)

        def loads(sp):
            sp.dma_start(w_q[:, :, :], dram["L0f_wq"]).then_inc(q_loaded, 16)
            sp.dma_start(keys[:, :], dram["L0f_keys"]).then_inc(q_loaded, 16)
            sp.dma_start(w_down[:, :, :], dram["L0f_down"]).then_inc(down_loaded, 16)
            sp.dma_start(w_org[:, :, :], dram["L0f_org"]).then_inc(out_loaded, 16)
            sp.dma_start(w_up[:, :, :], dram["L0f_up"]).then_inc(out_loaded, 16)
            for raw, name in zip(next_raw, ("L1x_wkv", "L1x_wq", "L1x_wo")):
                sp.dma_start(raw[:, :, :], dram[name]).then_inc(core.l1_loaded, 16)

        norm_stage(core, xn, xt, loads)

        sum_done, query_full, query_done = sem("sum_done"), sem("query_full"), sem("query_done")
        scores_full, top_done, exp_done, inv_done = sem("scores_full"), sem("top_done"), sem("exp_done"), sem("inv_done")
        raw_done = sem("raw_done")
        coef_done, coef_full, coef_t_done = sem("coef_done"), sem("coef_full"), sem("coef_t_done")
        ring_full, ring_drained = sem("ring_full"), sem("ring_drained")
        scale = 1.0 / float(np.sqrt(P))
        with nc.Block() as block:

            @block.tensor
            def _(pe):
                def low_rank(n):
                    j, half = n // 2, n % 2
                    wait(pe, ring_drained, n - 3)
                    for c in range(DC):
                        mm = product(pe, bank[4 + n % 4][:, :], [w_down[:, c, j * P:(j + 1) * P]],
                                     [xt[:, c, half * HALF:(half + 1) * HALF]], c == 0, c == DC - 1)
                    mm.then_inc(ring_full, 1)

                pe.wait_ge(down_loaded, 16)
                low_rank(0)
                pe.wait_ge(q_loaded, 32)
                pe.wait_ge(sum_done, 1)
                for c in range(DC):
                    mm = product(pe, bank[0][:, 0:B], [w_q[:, c, :]], [y_sum[:, c, :]], c == 0, c == DC - 1)
                mm.then_inc(query_full, 1)
                low_rank(1)
                pe.wait_ge(query_done, 1)
                product(pe, bank[1][0:B, 0:E], [query[:, :]], [keys[:, :]], True, True).then_inc(scores_full, 1)
                low_rank(2)
                low_rank(3)
                pe.wait_ge(coef_done, 1)
                for j in range(EC):
                    mm = product(pe, bank[2][:, j * B:(j + 1) * B],
                                 [coef[:, 2 * j:2 * j + 2, :].rearrange("b e r -> b (e r)")],
                                 [core.ident[0:B, 0:B]], True, True)
                mm.then_inc(coef_full, 1)
                for n in range(4, 8):
                    low_rank(n)
                pe.wait_ge(out_loaded, 32)
                for b in range(B):
                    part = slice(b * P, (b + 1) * P)
                    wait(pe, ring_drained, 8 + b - 3)
                    if b == 0:
                        pe.wait_ge(ring_drained, 8)
                    for c in range(DC):
                        product(pe, bank[4 + b % 4][:, :], [xt[:, c, part]], [w_org[:, c, :]], c == 0, False)
                    for j in range(EC):
                        mm = product(pe, bank[4 + b % 4][:, :], [h[:, j, part]], [w_up[:, j, :]], False, j == EC - 1)
                    mm.then_inc(ring_full, 1)

            @block.gpsimd
            def _(pool):
                for n, (w, raw) in enumerate(zip(next_weights, next_raw)):
                    pool.wait_ge(core.l1_hi, n + 1)
                    pool.tensor_tensor(w[1][:, :, :], raw[:, :, :], as_f32(w[0][:, :, :]), ALU.subtract
                                       ).then_inc(core.l1_split, 1)

            @block.scalar
            def _(act):
                act.wait_ge(query_full, 1)
                act.activation(query[:, :], bank[0][:, 0:B], ACT.Copy, scale=1.0 / P).then_inc(query_done, 1)
                act.wait_ge(top_done, 1)
                act.activation(exps[:, :], bank[1][0:B, 0:E], ACT.Exp, bias=top[:, :], scale=scale,
                               accum_out=total[:, :]).then_inc(exp_done, 1)
                act.wait_ge(core.l1_loaded, 48)
                for w, raw in zip(next_weights, next_raw):
                    act.activation(w[0][:, :, :], raw[:, :, :], ACT.Copy).then_inc(core.l1_hi, 1)

            @block.vector
            def _(dve):
                dve.tensor_reduce(y_sum[:, :, :], xt[:, :, :].rearrange("p c (b t) -> p c b t", b=B), AX.X, ALU.add
                                  ).then_inc(sum_done, 1)
                dve.wait_ge(scores_full, 1)
                dve.tensor_reduce(top[:, :], bank[1][0:B, 0:E], AX.X, ALU.max).then_inc(raw_done, 1)
                dve.wait_ge(raw_done, 1)
                dve.tensor_scalar(top[:, :], top[:, :], -scale, None, ALU.mult).then_inc(top_done, 1)
                dve.wait_ge(exp_done, 1)
                dve.reciprocal(inv[:, :], total[:, :]).then_inc(inv_done, 1)
                dve.wait_ge(inv_done, 1)
                dve.tensor_scalar(coef[:, :, :], exps[:, :].rearrange("b (e o) -> b e o", o=1).to_broadcast([B, E, R]),
                                  inv[:, 0:1], None, ALU.mult).then_inc(coef_done, 1)
                dve.wait_ge(coef_full, 1)
                dve.tensor_copy(coef_t[:, :, :], bank[2][:, 0:EC * B].rearrange("p (j b) -> p j b", j=EC)
                                ).then_inc(coef_t_done, 1)
                dve.wait_ge(coef_t_done, 1)
                for n in range(8):
                    j, half = n // 2, n % 2
                    dve.wait_ge(ring_full, n + 1)
                    dve.tensor_tensor(h[:, j, half * HALF:(half + 1) * HALF].rearrange("p (b t) -> p b t", b=BH),
                                      bank[4 + n % 4][:, :].rearrange("p (b t) -> p b t", b=BH),
                                      coef_t[:, j, half * BH:(half + 1) * BH].rearrange("p (b o) -> p b o", o=1)
                                      .to_broadcast([P, BH, P]), ALU.mult).then_inc(ring_drained, 1)
                for b in range(B):
                    dve.wait_ge(ring_full, 8 + b + 1)
                    dve.tensor_tensor(x[:, b, :], x[:, b, :], bank[4 + b % 4][:, :], ALU.add).then_inc(ring_drained, 1)


L1_GROUPS, L1_QUERIES, L1_DIM = 8, 4, 16


def l1_attention(core, dram):
    nc, x, bank = core.nc, core.x, core.bank
    KV, G, HD = L1_GROUPS, L1_QUERIES, L1_DIM
    SCALE = 1.0 / float(np.sqrt(HD))
    w_q, w_kv, w_o = core.l1_wq, core.l1_wkv, core.l1_wo
    n_norm = core.norms
    core.norms += 1
    with ExitStack() as ctx:
        sb = lambda name, shape, dt=F32: core.sb(ctx, "l1x_" + name, shape, dt)
        pair = lambda name, shape: core.pair(ctx, "l1x_" + name, shape)
        sem = lambda name: core.sem("l1x_" + name)
        xn, xt = sb("xn", [P, B, D]), pair("xt", [P, DC, T])
        q = core.cin
        kt = pair("kt", [P, T])
        v = sb("v", [P, B, KV, HD + 1])
        same = sb("same", [P, KV])
        kd = [pair(f"kd{j}", [P, KV, P]) for j in range(2)]
        qb = [pair(f"qb{j}", [P, G, P]) for j in range(2)]
        top = [sb(f"top{n}", [P, KV]) for n in range(2)]
        probs = [sb(f"probs{n}", [P, KV, P]) for n in range(2)]
        probs_t = [sb(f"probs_t{n}", [P, KV, P]) for n in range(2)]
        inv = sb("inv", [P, KV])
        a, at = sb("a", [P, G, KV, HD]), pair("at", [P, G, P])
        made, same_ready, ones_ready = sem("made"), sem("same_ready"), sem("ones_ready")
        kt_full, kt_hi, kt_done, v_full, v_done = (sem("kt_full"), sem("kt_hi"), sem("kt_done"), sem("v_full"),
                                                   sem("v_done"))
        xt_hi, q_full, q_hi, q_done = sem("xt_hi"), sem("q_full"), sem("q_hi"), sem("q_done")
        batch_ready = sem("batch_ready")
        s_full, top_done, shifted, exp_done = sem("s_full"), sem("top_done"), sem("shifted"), sem("exp_done")
        t_full, t_done, a_full, inv_done, a_done = (sem("t_full"), sem("t_done"), sem("a_full"), sem("inv_done"),
                                                    sem("a_done"))
        at_full, at_hi, at_done, o_full, o_done = (sem("at_full"), sem("at_hi"), sem("at_done"), sem("o_full"),
                                                   sem("o_done"))
        xt_bank = lambda b: (b + BH) % B
        q_bank = lambda half, g: bank[xt_bank(half * BH + g)]
        half_of = lambda half: slice(half * HALF, (half + 1) * HALF)

        def turns(body, eng):
            body(0, True)
            with eng.Fori(1, B // 2) as t:
                body(t, False)

        with nc.Block() as block:

            @block.gpsimd
            def _(pool):
                pool.memset(v[:, :, :, :], 1.0).then_inc(ones_ready, 1)
                pool.memset(same[:, :], 1.0).then_inc(made, 1)
                pool.wait_ge(made, 1)
                pool.affine_select(out=same[:, :], in_=same[:, :], compare_op=ALU.is_ge, fill=0.0, base=0,
                                   pattern=[[-HD, KV]], channel_multiplier=1).then_inc(made, 1)
                pool.wait_ge(made, 2)
                pool.affine_select(out=same[:, :], in_=same[:, :], compare_op=ALU.is_ge, fill=0.0, base=HD - 1,
                                   pattern=[[HD, KV]], channel_multiplier=-1).then_inc(same_ready, 1)
                pool.wait_ge(core.var_done, n_norm + 1)
                pool.tensor_tensor(core.rstd[:, :], core.var_eps[:, :], core.neg_half[:, :], ALU.pow
                                   ).then_inc(core.rstd_done, 1)
                pool.wait_ge(same_ready, 1)
                pool.wait_ge(kt_done, 2)

                def prepare(b, j):
                    wait(pool, s_full, G * (b - 1))
                    tokens = bass.ds(b * P, P)
                    for s in range(2):
                        pool.tensor_tensor(kd[j][s][:, :, :],
                                           as_f32(kt[s][:, tokens]).rearrange("p (o k) -> p o k", o=1)
                                           .to_broadcast([P, KV, P]),
                                           same[:, :].rearrange("p (n o) -> p n o", o=1).to_broadcast([P, KV, P]),
                                           ALU.mult)
                    if isinstance(b, int):
                        pool.wait_ge(q_done, G if b == 0 else 2 * G)
                    for s in range(2):
                        last = pool.tensor_copy(qb[j][s][:, :, :], as_f32(q[s][:, :, tokens]))
                    last.then_inc(batch_ready, 1)

                def turn(t, first):
                    prepare(2 * t, 0)
                    prepare(2 * t + 1, 1)

                turns(turn, pool)

            @block.tensor
            def _(pe):
                pe.wait_ge(core.l1_split, 1)
                for half in range(2):
                    for c in range(DC):
                        mm = product(pe, bank[half][:, :], [w_kv[s][:, c, 0:P] for s in range(2)],
                                     [core.cin[s][:, c, half_of(half)] for s in range(2)], c == 0, c == DC - 1)
                    mm.then_inc(kt_full, 1)
                for half in range(2):
                    for y in range(BH):
                        b = half * BH + y
                        for c in range(DC):
                            mm = product(pe, bank[2 + half][:, y * P:(y + 1) * P],
                                         [core.cin[s][:, c, b * P:(b + 1) * P] for s in range(2)],
                                         [w_kv[s][:, c, P:2 * P] for s in range(2)], c == 0, c == DC - 1)
                    mm.then_inc(v_full, 1)
                for b in range(B):
                    pe.wait_ge(core.xn_done, B * n_norm + b + 1)
                    if b == BH:
                        pe.wait_ge(kt_done, 2)
                    if b == BH + 2:
                        pe.wait_ge(v_done, 2)
                    for c in range(DC):
                        mm = pe.transpose(bank[xt_bank(b)][:, c * P:(c + 1) * P], xn[:, b, c * P:(c + 1) * P],
                                          core.ident[:, :])
                    mm.then_inc(core.xt_full, 1)
                pe.wait_ge(core.l1_split, 2)
                for half in range(2):
                    pe.wait_ge(core.xt_copied, B * n_norm + (half + 1) * BH)
                    for g in range(G):
                        for c in range(DC):
                            mm = product(pe, q_bank(half, g)[:, :], [w_q[s][:, c, g * P:(g + 1) * P] for s in range(2)],
                                         [xt[s][:, c, half_of(half)] for s in range(2)], c == 0, c == DC - 1)
                        mm.then_inc(q_full, 1)

                def scores(b, j, g):
                    wait(pe, shifted, G * b + g - 1)
                    if g == 0:
                        pe.wait_ge(batch_ready, b + 1)
                    for n in range(2):
                        mm = product(pe, bank[2 * (g % 2) + n][:, :], [qb[j][s][:, g, :] for s in range(2)],
                                     [kd[j][s][:, n * BH:(n + 1) * BH, :].rearrange("p n k -> p (n k)") for s in range(2)],
                                     True, True)
                    mm.then_inc(s_full, 1)

                def transpose_probs(b, g):
                    pe.wait_ge(exp_done, G * b + g + 1)
                    wait(pe, t_done, 2 * (G * b + g))
                    for m in range(KV):
                        mm = pe.transpose(bank[4 + m // BH][:, (m % BH) * P:(m % BH + 1) * P], probs[g % 2][:, m, :],
                                          core.ident[:, :])
                        if m % BH == BH - 1:
                            mm.then_inc(t_full, 1)

                def weigh_values(b, g):
                    wait(pe, a_done, G * b + g)
                    for m in range(KV):
                        if m % BH == 0:
                            pe.wait_ge(t_done, 2 * (G * b + g) + m // BH + 1)
                        mm = product(pe, bank[6][:, m * (HD + 1):(m + 1) * (HD + 1)], [probs_t[g % 2][:, m, :]],
                                     [v[:, bass.ds(b, 1), m, :].rearrange("p o d -> p (o d)")], True, True)
                    mm.then_inc(a_full, 1)

                def transpose_result(b):
                    pe.wait_ge(a_done, G * b + G)
                    wait(pe, o_done, b)
                    for g in range(G):
                        mm = pe.transpose(bank[7][:, g * P:(g + 1) * P], a[:, g, :, :].rearrange("p n d -> p (n d)"),
                                          core.ident[:, :])
                    mm.then_inc(at_full, 1)

                def project_out(b):
                    pe.wait_ge(at_done, b + 1)
                    for g in range(G):
                        mm = product(pe, bank[7][:, :], [at[s][:, g, :] for s in range(2)],
                                     [w_o[s][:, g, :] for s in range(2)], g == 0, g == G - 1)
                    mm.then_inc(o_full, 1)

                def batch(b, j, first):
                    scores(b, j, 0)
                    if not first:
                        weigh_values(b - 1, 2)
                        transpose_probs(b - 1, 3)
                    scores(b, j, 1)
                    if not first:
                        weigh_values(b - 1, 3)
                    transpose_probs(b, 0)
                    scores(b, j, 2)
                    if not first:
                        transpose_result(b - 1)
                    weigh_values(b, 0)
                    transpose_probs(b, 1)
                    scores(b, j, 3)
                    if not first:
                        project_out(b - 1)
                    weigh_values(b, 1)
                    transpose_probs(b, 2)

                def turn(t, first):
                    batch(2 * t, 0, first)
                    batch(2 * t + 1, 1, False)

                pe.wait_ge(q_done, 2 * G)
                turns(turn, pe)
                weigh_values(B - 1, 2)
                transpose_probs(B - 1, 3)
                weigh_values(B - 1, 3)
                transpose_result(B - 1)
                project_out(B - 1)

            @block.scalar
            def _(act):
                for half in range(2):
                    act.wait_ge(kt_full, half + 1)
                    act.activation(kt[0][:, half_of(half)], bank[half][:, :], ACT.Copy).then_inc(kt_hi, 1)
                for b in range(B):
                    act.wait_ge(core.xt_full, B * n_norm + b + 1)
                    act.activation(xt[0][:, :, b * P:(b + 1) * P],
                                   bank[xt_bank(b)][:, :].rearrange("p (c t) -> p c t", c=DC), ACT.Copy).then_inc(xt_hi, 1)
                for half in range(2):
                    for g in range(G):
                        act.wait_ge(q_full, half * G + g + 1)
                        act.activation(q[0][:, g, half_of(half)], q_bank(half, g)[:, :], ACT.Copy).then_inc(q_hi, 1)

                def batch(b, first):
                    for g in range(G):
                        act.wait_ge(shifted, G * b + g + 1)
                        act.activation(probs[g % 2][:, :, :], probs[g % 2][:, :, :], ACT.Exp, scale=SCALE
                                       ).then_inc(exp_done, 1)
                        if g == 1 and not first:
                            result_high(b - 1)
                        for n in range(2):
                            act.wait_ge(t_full, 2 * (G * b + g) + n + 1)
                            act.activation(probs_t[g % 2][:, n * BH:(n + 1) * BH, :],
                                           bank[4 + n][:, :].rearrange("p (m k) -> p m k", m=BH), ACT.Copy
                                           ).then_inc(t_done, 1)

                def result_high(b):
                    act.wait_ge(at_full, b + 1)
                    act.activation(at[0][:, :, :], bank[7][:, :].rearrange("p (g t) -> p g t", g=G), ACT.Copy
                                   ).then_inc(at_hi, 1)

                def turn(t, first):
                    batch(2 * t, first)
                    batch(2 * t + 1, False)

                turns(turn, act)
                result_high(B - 1)

            @block.vector
            def _(dve):
                wide = lambda t: t[:, :].rearrange("p (n o) -> p n o", o=1)
                for b in range(B):
                    dve.bn_stats(core.stats[:, b, :], core.x[:, b, :]).then_inc(core.stats_done, 1)
                dve.wait_ge(core.stats_done, B * (n_norm + 1))
                for b in range(B):
                    dve.bn_aggr(core.mv[:, b, :], core.stats[:, b, :]).then_inc(core.mv_done, 1)
                dve.wait_ge(core.mv_done, B * (n_norm + 1))
                dve.tensor_scalar_add(core.var_eps[:, :], core.mv[:, :, 1], EPS).then_inc(core.var_done, 1)
                for half in range(2):
                    dve.wait_ge(kt_hi, half + 1)
                    dve.tensor_tensor(kt[1][:, half_of(half)], bank[half][:, :], as_f32(kt[0][:, half_of(half)]),
                                      ALU.subtract).then_inc(kt_done, 1)
                dve.wait_ge(core.rstd_done, n_norm + 1)
                for b in range(B):
                    dve.tensor_scalar(xn[:, b, :], core.x[:, b, :], core.mv[:, b, 0:1], core.rstd[:, b:b + 1],
                                      ALU.subtract, ALU.mult).then_inc(core.xn_done, 1)
                dve.wait_ge(ones_ready, 1)
                for half in range(2):
                    dve.wait_ge(v_full, half + 1)
                    dve.tensor_copy(v[:, half * BH:(half + 1) * BH, :, 0:HD],
                                    bank[2 + half][:, :].rearrange("p (b n d) -> p b n d", b=BH, n=KV)).then_inc(v_done, 1)
                for b in range(B):
                    dve.wait_ge(xt_hi, b + 1)
                    dve.tensor_tensor(xt[1][:, :, b * P:(b + 1) * P],
                                      bank[xt_bank(b)][:, :].rearrange("p (c t) -> p c t", c=DC),
                                      as_f32(xt[0][:, :, b * P:(b + 1) * P]), ALU.subtract).then_inc(core.xt_copied, 1)
                for half in range(2):
                    for g in range(G):
                        dve.wait_ge(q_hi, half * G + g + 1)
                        dve.tensor_tensor(q[1][:, g, half_of(half)], q_bank(half, g)[:, :],
                                          as_f32(q[0][:, g, half_of(half)]), ALU.subtract).then_inc(q_done, 1)

                def shift(b, g):
                    s = bank[2 * (g % 2):2 * (g % 2) + 2]
                    dve.wait_ge(s_full, G * b + g + 1)
                    wait(dve, shifted, G * b + g - 1)
                    for n in range(2):
                        dve.tensor_reduce(top[g % 2][:, n * BH:(n + 1) * BH], s[n][:, :].rearrange("p (m k) -> p m k", m=BH),
                                          AX.X, ALU.max).then_inc(top_done, 1)
                    wait(dve, t_full, 2 * (G * b + g - 1))
                    for n in range(2):
                        dve.wait_ge(top_done, 2 * (G * b + g) + n + 1)
                        last = dve.tensor_tensor(
                            probs[g % 2][:, n * BH:(n + 1) * BH, :], s[n][:, :].rearrange("p (m k) -> p m k", m=BH),
                            wide(top[g % 2])[:, n * BH:(n + 1) * BH, :].to_broadcast([P, BH, P]), ALU.subtract)
                    last.then_inc(shifted, 1)

                def divide(b, g):
                    bk = bank[6][:, 0:KV * (HD + 1)].rearrange("p (n d) -> p n d", d=HD + 1)
                    dve.wait_ge(a_full, G * b + g + 1)
                    dve.reciprocal(inv[:, :], bk[:, :, HD]).then_inc(inv_done, 1)
                    dve.wait_ge(inv_done, G * b + g + 1)
                    dve.tensor_tensor(a[:, g, :, :], bk[:, :, 0:HD], wide(inv).to_broadcast([P, KV, HD]), ALU.mult
                                      ).then_inc(a_done, 1)

                def result_low(b):
                    dve.wait_ge(at_hi, b + 1)
                    dve.tensor_tensor(at[1][:, :, :], bank[7][:, :].rearrange("p (g t) -> p g t", g=G),
                                      as_f32(at[0][:, :, :]), ALU.subtract).then_inc(at_done, 1)

                def add_out(b):
                    dve.wait_ge(o_full, b + 1)
                    xb = x[:, bass.ds(b, 1), :].rearrange("p o d -> p (o d)")
                    dve.tensor_tensor(xb, xb, bank[7][:, :], ALU.add).then_inc(o_done, 1)

                def batch(b, first):
                    shift(b, 0)
                    if not first:
                        divide(b - 1, 2)
                    shift(b, 1)
                    if not first:
                        divide(b - 1, 3)
                    shift(b, 2)
                    if not first:
                        result_low(b - 1)
                    divide(b, 0)
                    shift(b, 3)
                    divide(b, 1)
                    if not first:
                        add_out(b - 1)

                def turn(t, first):
                    batch(2 * t, first)
                    batch(2 * t + 1, False)

                turns(turn, dve)
                divide(B - 1, 2)
                divide(B - 1, 3)
                result_low(B - 1)
                add_out(B - 1)


def l1_ffn(core, dram):
    nc, x, bank = core.nc, core.x, core.bank
    BOT, RD, SLOTS, TOPK, VB = 64, 48, P, 8, 32
    TAU_LOW, TAU_HIGH, EARLY_EXIT = 0.5, 2.0, 0.05
    TAKEN = -3e38
    GELU = float(np.sqrt(2.0 / np.pi))
    with ExitStack() as ctx:
        sb = lambda name, shape, dt=F32: core.sb(ctx, "l1f_" + name, shape, dt)
        sem = lambda name: core.sem("l1f_" + name)
        xn, xt = sb("xn", [P, B, D]), sb("xt", [P, DC, T])
        w_q, w_r, keys = sb("w_q", [P, DC, BOT]), sb("w_r", [BOT, RD]), sb("keys", [BOT, SLOTS])
        values, w_vd, w_vu = sb("values", [P, DC, SLOTS]), sb("w_vd", [P, DC, VB]), sb("w_vu", [VB, D])
        w_u1, w_u2 = sb("w_u1", [P, DC, P]), sb("w_u2", [P, 1])
        consts = sb("consts", [P, 4])
        log_rel = sb("log_rel", [P, 1, SLOTS])
        ones = sb("ones", [P, P])
        rk, vd, table = sb("rk", [RD, SLOTS]), sb("vd", [VB, SLOTS]), sb("table", [SLOTS, D])
        q, rq = sb("q", [BOT, T]), sb("rq", [RD, T])
        z, th = sb("z", [P, T]), sb("th", [P, T])
        route, rest, attn = sb("route", [P, B, SLOTS]), sb("rest", [P, B, SLOTS]), sb("attn", [P, B, SLOTS])
        top8, top, total = sb("top8", [P, B, TOPK]), sb("top", [P, B]), sb("total", [P, B])
        attn_t = sb("attn_t", [SLOTS, T])
        lv, lsum, u, gate = sb("lv", [P, B]), sb("lsum", [P, 1]), sb("u", [P, B]), sb("gate", [P, B])
        loaded, ones_done = sem("loaded"), sem("ones_done")
        names = (("L1f_wq", w_q), ("L1f_wr", w_r), ("L1f_keys", keys), ("L1f_values", values), ("L1f_wvd", w_vd),
                 ("L1f_wvu", w_vu), ("L1f_wu1", w_u1), ("L1f_wu2", w_u2), ("L1f_consts", consts), ("L1f_log_rel", log_rel))

        def loads(sp):
            for name, t in names:
                sp.dma_start(t[tuple(slice(None) for _ in t.shape)], dram[name]).then_inc(loaded, 16)

        norm_stage(core, xn, xt, loads)

        small_full, small_done, table_full, table_done = (sem("small_full"), sem("small_done"), sem("table_full"),
                                                          sem("table_done"))
        q_full, q_done, rq_full, rq_done = sem("q_full"), sem("q_done"), sem("rq_full"), sem("rq_done")
        z_full, z_done, gelu_step, th_done, gelu_done = (sem("z_full"), sem("z_done"), sem("gelu_step"), sem("th_done"),
                                                         sem("gelu_done"))
        route_full, attn_full, route_done, top8_done, rest_done = (sem("route_full"), sem("attn_full"),
                                                                   sem("route_done"), sem("top8_done"), sem("rest_done"))
        attn_step, top_done, exp_done = sem("attn_step"), sem("top_done"), sem("exp_done")
        t_full, t_done, aux_full, aux_read = sem("t_full"), sem("t_done"), sem("aux_full"), sem("aux_read")
        learned_full, var_done, lv_done, lsum_done, mean_full = (sem("learned_full"), sem("var_done"), sem("lv_done"),
                                                                 sem("lsum_done"), sem("mean_full"))
        gate_step, tanh_in, tanh_out = sem("gate_step"), sem("tanh_in"), sem("tanh_out")
        y_added = sem("y_added")
        with nc.Block() as block:

            @block.gpsimd
            def _(pool):
                pool.memset(ones[:, :], 1.0).then_inc(ones_done, 1)
                for b in range(B):
                    pool.tensor_tensor(x[:, b, :], x[:, b, :], xn[:, b, :], ALU.add).then_inc(y_added, 1)

            @block.tensor
            def _(pe):
                pe.wait_ge(loaded, 16 * len(names))
                for half in range(2):
                    part = slice(half * HALF, (half + 1) * HALF)
                    for c in range(DC):
                        mm = product(pe, bank[half][0:BOT, :], [w_q[:, c, :]], [xt[:, c, part]], c == 0, c == DC - 1)
                    mm.then_inc(q_full, 1)
                for half in range(2):
                    part = slice(half * HALF, (half + 1) * HALF)
                    for c in range(DC):
                        mm = product(pe, bank[2 + half][:, :], [w_u1[:, c, :]], [xt[:, c, part]], c == 0, c == DC - 1)
                    mm.then_inc(z_full, 1)
                product(pe, bank[4][0:RD, 0:SLOTS], [w_r[:, :]], [keys[:, :]], True, True).then_inc(small_full, 1)
                for c in range(DC):
                    mm = product(pe, bank[5][0:VB, 0:SLOTS], [w_vd[:, c, :]], [values[:, c, :]], c == 0, c == DC - 1)
                mm.then_inc(small_full, 1)
                pe.wait_ge(q_done, 2)
                for half in range(2):
                    part = slice(half * HALF, (half + 1) * HALF)
                    product(pe, bank[6 + half][0:RD, :], [w_r[:, :]], [q[:, part]], True, True).then_inc(rq_full, 1)
                pe.wait_ge(small_done, 2)
                product(pe, bank[4][:, :], [vd[:, :]], [w_vu[:, :]], True, True).then_inc(table_full, 1)
                pe.wait_ge(rq_done, 2)
                for b in range(B):
                    mm = product(pe, bank[b // BH][:, (b % BH) * P:(b % BH + 1) * P], [rq[:, b * P:(b + 1) * P]],
                                 [rk[:, :]], True, True)
                    mm.then_inc(route_full, 1)
                for b in range(B):
                    mm = product(pe, bank[6 + b // BH][:, (b % BH) * P:(b % BH + 1) * P], [q[:, b * P:(b + 1) * P]],
                                 [keys[:, :]], True, True)
                    mm.then_inc(attn_full, 1)
                pe.wait_ge(ones_done, 1)
                pe.wait_ge(lsum_done, 1)
                product(pe, bank[5][:, 0:1], [ones[:, :]], [lsum[:, :]], True, True).then_inc(mean_full, 1)
                pe.wait_ge(gelu_done, 1)
                pe.wait_ge(z_done, 2)
                for b in range(B):
                    mm = product(pe, bank[2][:, b:b + 1], [z[:, b * P:(b + 1) * P]], [w_u2[:, :]], True, True)
                mm.then_inc(learned_full, 1)
                pe.wait_ge(route_done, 2)
                for b in range(B):
                    pe.wait_ge(exp_done, b + 1)
                    mm = pe.transpose(bank[b // BH][:, (b % BH) * P:(b % BH + 1) * P], attn[:, b, :], core.ident[:, :])
                    if b % BH == BH - 1:
                        mm.then_inc(t_full, 1)
                pe.wait_ge(table_done, 1)
                ring = (3, 4, 6, 7)
                for b in range(B):
                    if b % BH == 0:
                        pe.wait_ge(t_done, b // BH + 1)
                    wait(pe, aux_read, b - 3)
                    product(pe, bank[ring[b % 4]][:, :], [attn_t[:, b * P:(b + 1) * P]], [table[:, :]], True, True
                            ).then_inc(aux_full, 1)

            @block.scalar
            def _(act):
                act.wait_ge(var_done, 1)
                act.activation(lv[:, :], lv[:, :], ACT.Ln, bias=1.0).then_inc(lv_done, 1)
                act.wait_ge(loaded, 16 * len(names))
                for half in range(2):
                    part = slice(half * HALF, (half + 1) * HALF)
                    act.wait_ge(q_full, half + 1)
                    act.activation(q[:, part], bank[half][0:BOT, :], ACT.Copy).then_inc(q_done, 1)
                for half in range(2):
                    part = slice(half * HALF, (half + 1) * HALF)
                    act.wait_ge(z_full, half + 1)
                    act.activation(z[:, part], bank[2 + half][:, :], ACT.Identity, bias=consts[:, 0:1]
                                   ).then_inc(z_done, 1)
                act.wait_ge(small_full, 2)
                act.activation(rk[:, :], bank[4][0:RD, 0:SLOTS], ACT.Copy).then_inc(small_done, 1)
                act.activation(vd[:, :], bank[5][0:VB, 0:SLOTS], ACT.Copy).then_inc(small_done, 1)
                for half in range(2):
                    part = slice(half * HALF, (half + 1) * HALF)
                    act.wait_ge(rq_full, half + 1)
                    act.activation(rq[:, part], bank[6 + half][0:RD, :], ACT.Copy).then_inc(rq_done, 1)
                act.wait_ge(table_full, 1)
                act.activation(table[:, :], bank[4][:, :], ACT.Copy).then_inc(table_done, 1)
                act.wait_ge(gelu_step, 3)
                act.activation(th[:, :], th[:, :], ACT.Tanh, scale=GELU).then_inc(th_done, 1)
                act.wait_ge(tanh_in, 1)
                act.activation(u[:, :], u[:, :], ACT.Tanh, scale=0.5).then_inc(tanh_out, 1)
                for b in range(B):
                    act.wait_ge(top_done, 1)
                    act.activation(attn[:, b, :], attn[:, b, :], ACT.Exp, bias=top[:, b:b + 1],
                                   accum_out=total[:, b:b + 1]).then_inc(exp_done, 1)
                act.wait_ge(tanh_in, 2)
                act.activation(gate[:, :], gate[:, :], ACT.Tanh, scale=0.5).then_inc(tanh_out, 1)
                for half in range(2):
                    act.wait_ge(t_full, half + 1)
                    act.activation(attn_t[:, half * HALF:(half + 1) * HALF], bank[half][:, :], ACT.Copy
                                   ).then_inc(t_done, 1)

            @block.vector
            def _(dve):
                steps = [0]

                def then(instruction):
                    steps[0] += 1
                    instruction.then_inc(gate_step, 1)
                    dve.wait_ge(gate_step, steps[0])

                then(dve.tensor_tensor(lv[:, :], core.mv[:, :, 1], core.rstd[:, :], ALU.mult))
                dve.tensor_tensor(lv[:, :], lv[:, :], core.rstd[:, :], ALU.mult).then_inc(var_done, 1)
                dve.wait_ge(z_done, 2)
                dve.tensor_tensor(th[:, :], z[:, :], z[:, :], ALU.mult).then_inc(gelu_step, 1)
                dve.wait_ge(gelu_step, 1)
                dve.tensor_scalar(th[:, :], th[:, :], 0.044715, 1.0, ALU.mult, ALU.add).then_inc(gelu_step, 1)
                dve.wait_ge(gelu_step, 2)
                dve.tensor_tensor(th[:, :], th[:, :], z[:, :], ALU.mult).then_inc(gelu_step, 1)
                dve.wait_ge(lv_done, 1)
                dve.tensor_reduce(lsum[:, :], lv[:, :], AX.X, ALU.add).then_inc(lsum_done, 1)
                for half in range(2):
                    dve.wait_ge(route_full, BH * (half + 1))
                    dve.scalar_tensor_tensor(route[:, half * BH:(half + 1) * BH, :],
                                             bank[half][:, :].rearrange("p (b n) -> p b n", b=BH),
                                             1.0 / float(np.sqrt(RD)), log_rel[:, :, :].to_broadcast([P, BH, SLOTS]),
                                             ALU.mult, ALU.add).then_inc(route_done, 1)
                dve.wait_ge(route_done, 2)
                for b in range(B):
                    dve.max(top8[:, b, :], route[:, b, :]).then_inc(top8_done, 1)
                dve.wait_ge(th_done, 1)
                dve.scalar_tensor_tensor(z[:, :], th[:, :], 1.0, z[:, :], ALU.add, ALU.mult).then_inc(gelu_done, 1)
                dve.wait_ge(top8_done, B)
                for b in range(B):
                    dve.match_replace(rest[:, b, :], top8[:, b, :], route[:, b, :], TAKEN).then_inc(rest_done, 1)
                for half in range(2):
                    dve.wait_ge(attn_full, BH * (half + 1))
                    dve.scalar_tensor_tensor(attn[:, half * BH:(half + 1) * BH, :],
                                             bank[6 + half][:, :].rearrange("p (b n) -> p b n", b=BH),
                                             1.0 / float(np.sqrt(BOT)), log_rel[:, :, :].to_broadcast([P, BH, SLOTS]),
                                             ALU.mult, ALU.add).then_inc(attn_step, 1)
                dve.wait_ge(rest_done, B)
                dve.tensor_tensor(rest[:, :, :], rest[:, :, :], route[:, :, :], ALU.is_equal).then_inc(attn_step, 1)
                dve.wait_ge(attn_step, 3)
                dve.scalar_tensor_tensor(attn[:, :, :], rest[:, :, :], MASKED, attn[:, :, :], ALU.mult, ALU.add
                                         ).then_inc(attn_step, 1)
                dve.wait_ge(attn_step, 4)
                dve.tensor_reduce(top[:, :], attn[:, :, :], AX.X, ALU.max).then_inc(attn_step, 1)
                dve.wait_ge(attn_step, 5)
                dve.tensor_scalar(top[:, :], top[:, :], -1.0, None, ALU.mult).then_inc(top_done, 1)
                dve.wait_ge(learned_full, 1)
                dve.tensor_scalar(u[:, :], bank[2][:, 0:B], 0.5, consts[:, 1:2], ALU.mult, ALU.add
                                  ).then_inc(tanh_in, 1)
                dve.wait_ge(mean_full, 1)
                then(dve.tensor_scalar(lsum[:, :], bank[5][:, 0:1], 1.0 / T, 1e-6, ALU.mult, ALU.add))
                then(dve.reciprocal(lsum[:, :], lsum[:, :]))
                then(dve.tensor_scalar(lv[:, :], lv[:, :], lsum[:, 0:1], 0.5, ALU.mult, ALU.mult))
                dve.wait_ge(tanh_out, 1)
                then(dve.tensor_scalar(u[:, :], u[:, :], 1.25, 1.25, ALU.mult, ALU.add))
                then(dve.tensor_tensor(u[:, :], u[:, :], lv[:, :], ALU.add))
                then(dve.tensor_scalar(u[:, :], u[:, :], 0.0, 5.0, ALU.max, ALU.min))
                then(dve.tensor_scalar(u[:, :], u[:, :], -TAU_LOW, 1.0 / (TAU_HIGH - TAU_LOW), ALU.add, ALU.mult))
                then(dve.tensor_scalar(u[:, :], u[:, :], 0.0, 1.0, ALU.max, ALU.min))
                dve.tensor_scalar(gate[:, :], u[:, :], consts[:, 2:3], consts[:, 3:4], ALU.mult, ALU.add
                                  ).then_inc(tanh_in, 1)
                dve.wait_ge(tanh_out, 2)
                then(dve.tensor_scalar(gate[:, :], gate[:, :], 0.5, 0.5, ALU.mult, ALU.add))
                then(dve.scalar_tensor_tensor(gate[:, :], gate[:, :], EARLY_EXIT, gate[:, :], ALU.is_ge, ALU.mult))
                dve.wait_ge(exp_done, B)
                then(dve.reciprocal(total[:, :], total[:, :]))
                then(dve.tensor_tensor(gate[:, :], gate[:, :], total[:, :], ALU.mult))
                dve.wait_ge(y_added, B)
                for b in range(B):
                    dve.wait_ge(aux_full, b + 1)
                    dve.scalar_tensor_tensor(x[:, b, :], bank[(3, 4, 6, 7)[b % 4]][:, :], gate[:, b:b + 1],
                                             x[:, b, :], ALU.mult, ALU.add).then_inc(aux_read, 1)


def l2_attention(core, dram):
    nc, x, bank = core.nc, core.x, core.bank
    TAPS, PAD = 7, 3
    KINDS = 4
    SETS = 2
    with ExitStack() as ctx:
        sb = lambda name, shape, dt=F32: core.sb(ctx, "l2x_" + name, shape, dt)
        sem = lambda name: core.sem("l2x_" + name)
        xn, xt = sb("xn", [P, B, D]), sb("xt", [P, DC, T])
        fc, fo = sb("fc", [P, DC, T]), sb("fo", [P, DC, T])
        stat = sb("stat", [P, DC, KINDS, B])
        padded, acc = sb("padded", [KINDS * B, D + 2 * PAD]), sb("acc", [KINDS * B, D])
        taps, affine = sb("taps", [KINDS * B, TAPS]), sb("affine", [SETS * B, 2])
        pick, mean = sb("pick", [KINDS * B, SETS * B]), sb("mean", [SETS * B, SETS, B])
        z, zstat, zmv = sb("z", [SETS * B, D]), sb("zstat", [SETS * B, 6]), sb("zmv", [SETS * B, 2])
        mu, dev, rs = sb("mu", [SETS * B, 1]), sb("dev", [SETS * B, 1]), sb("rs", [SETS * B, 1])
        amap = sb("amap", [P, DC, SETS, B])
        small_loaded, made, const_done = sem("small_loaded"), sem("made"), sem("const_done")

        def loads(sp):
            sp.dma_start(taps[:, :], dram["L2x_taps"]).then_inc(small_loaded, 16)
            sp.dma_start(affine[:, :], dram["L2x_affine"]).then_inc(small_loaded, 16)

        norm_stage(core, xn, xt, loads)

        step, masked = sem("step"), sem("masked")
        stat_full, stat_done, z_full, z_done = sem("stat_full"), sem("stat_done"), sem("z_full"), sem("z_done")
        mean_in, mean_full, var_in, var_full, rs_in, rs_done = (sem("mean_in"), sem("mean_full"), sem("var_in"),
                                                                sem("var_full"), sem("rs_in"), sem("rs_done"))
        tanh_in, tanh_out, map_in, map_full, map_done = (sem("tanh_in"), sem("tanh_out"), sem("map_in"),
                                                         sem("map_full"), sem("map_done"))
        others_done, out_ready, back_full, added = (sem("others_done"), sem("out_ready"), sem("back_full"),
                                                    sem("added"))
        tiles = lambda t: t[:, :, :].rearrange("p c (b n) -> p (c b) n", b=B)
        with nc.Block() as block:

            @block.gpsimd
            def _(pool):
                pool.memset(mean[:, :, :], 1.0 / B).then_inc(made, 1)
                pool.memset(padded[:, :], 0.0).then_inc(const_done, 1)
                pool.wait_ge(made, 1)
                pool.affine_select(out=mean[:, :, :], in_=mean[:, :, :], compare_op=ALU.is_ge, fill=0.0, base=0,
                                   pattern=[[-B, SETS], [0, B]], channel_multiplier=1).then_inc(made, 1)
                pool.wait_ge(made, 2)
                pool.affine_select(out=mean[:, :, :], in_=mean[:, :, :], compare_op=ALU.is_ge, fill=0.0, base=B - 1,
                                   pattern=[[B, SETS], [0, B]], channel_multiplier=-1).then_inc(const_done, 1)
                pool.wait_ge(rs_in, 1)
                pool.tensor_tensor(rs[:, :], rs[:, :], core.neg_half[0:SETS * B, 0:1], ALU.pow).then_inc(rs_done, 1)

            @block.tensor
            def _(pe):
                pe.wait_ge(stat_done, 1)
                for c in range(DC):
                    mm = pe.transpose(bank[0][0:KINDS * B, c * P:(c + 1) * P],
                                      stat[:, c, :, :].rearrange("p k b -> p (k b)"), core.ident[:, :])
                mm.then_inc(stat_full, 1)
                pe.wait_ge(z_done, 1)
                product(pe, bank[1][0:SETS * B, :], [pick[:, :]], [acc[:, :]], True, True).then_inc(z_full, 1)
                pe.wait_ge(const_done, 2)
                group = mean[:, :, :].rearrange("p s b -> p (s b)")
                pe.wait_ge(mean_in, 1)
                product(pe, bank[2][0:SETS * B, 0:1], [group], [zmv[:, 0:1]], True, True).then_inc(mean_full, 1)
                pe.wait_ge(var_in, 1)
                product(pe, bank[3][0:SETS * B, 0:1], [group], [dev[:, :]], True, True).then_inc(var_full, 1)
                pe.wait_ge(map_in, 1)
                for c in range(DC):
                    mm = pe.transpose(bank[0][:, c * SETS * B:(c + 1) * SETS * B], z[:, c * P:(c + 1) * P],
                                      core.ident[0:SETS * B, 0:SETS * B])
                mm.then_inc(map_full, 1)
                for b in range(B):
                    pe.wait_ge(out_ready, DC)
                    for c in range(DC):
                        mm = pe.transpose(bank[b][:, c * P:(c + 1) * P], fc[:, c, b * P:(b + 1) * P], core.ident[:, :])
                    mm.then_inc(back_full, 1)

            @block.scalar
            def _(act):
                act.wait_ge(tanh_in, 1)
                act.activation(z[:, :], z[:, :], ACT.Tanh, scale=0.5).then_inc(tanh_out, 1)

            @block.vector
            def _(dve):
                steps = [0]

                def mark(instruction):
                    steps[0] += 1
                    instruction.then_inc(step, 1)

                def settle():
                    dve.wait_ge(step, steps[0])

                mark(dve.tensor_tensor(tiles(fc), tiles(xt), core.crucial[:, :, :], ALU.mult))
                settle()
                mark(dve.tensor_tensor(fo[:, :, :], xt[:, :, :], fc[:, :, :], ALU.subtract))
                settle()
                for k, (t, op) in enumerate(((fc, ALU.max), (fo, ALU.max), (fc, ALU.add), (fo, ALU.add))):
                    for c in range(DC):
                        mark(dve.tensor_reduce(stat[:, c, k, :], t[:, c, :].rearrange("p (b n) -> p b n", b=B), AX.X, op))
                settle()
                mark(dve.tensor_scalar(stat[:, :, 2, :], stat[:, :, 2, :], 1.0 / CRUCIAL, None, ALU.mult))
                dve.tensor_scalar(stat[:, :, 3, :], stat[:, :, 3, :], 1.0 / OTHERS, None, ALU.mult).then_inc(stat_done, 1)
                dve.wait_ge(small_loaded, 32)
                dve.wait_ge(const_done, 2)
                dve.wait_ge(stat_full, 1)
                mark(dve.tensor_copy(padded[:, PAD:PAD + D], bank[0][0:KINDS * B, :]))
                settle()
                mark(dve.tensor_scalar(acc[:, :], padded[:, 0:D], taps[:, 0:1], None, ALU.mult))
                for t in range(1, TAPS):
                    settle()
                    mark(dve.scalar_tensor_tensor(acc[:, :], padded[:, t:t + D], taps[:, t:t + 1], acc[:, :], ALU.mult,
                                                  ALU.add))
                settle()
                dve.tensor_tensor(pick[:, :], core.ident[0:KINDS * B, 0:SETS * B],
                                  core.ident[0:KINDS * B, SETS * B:KINDS * B], ALU.add).then_inc(z_done, 1)
                dve.wait_ge(z_full, 1)
                mark(dve.tensor_copy(z[:, :], bank[1][0:SETS * B, :]))
                settle()
                mark(dve.bn_stats(zstat[:, :], z[:, :]))
                settle()
                dve.bn_aggr(zmv[:, :], zstat[:, :]).then_inc(mean_in, 1)
                dve.wait_ge(mean_in, 1)
                dve.wait_ge(mean_full, 1)
                mark(dve.tensor_copy(mu[:, :], bank[2][0:SETS * B, 0:1]))
                settle()
                mark(dve.tensor_tensor(dev[:, :], zmv[:, 0:1], mu[:, :], ALU.subtract))
                settle()
                mark(dve.tensor_tensor(dev[:, :], dev[:, :], dev[:, :], ALU.mult))
                settle()
                dve.tensor_tensor(dev[:, :], dev[:, :], zmv[:, 1:2], ALU.add).then_inc(var_in, 1)
                dve.wait_ge(var_full, 1)
                dve.tensor_scalar_add(rs[:, :], bank[3][0:SETS * B, 0:1], EPS).then_inc(rs_in, 1)
                dve.wait_ge(rs_done, 1)
                mark(dve.tensor_scalar(z[:, :], z[:, :], mu[:, 0:1], rs[:, 0:1], ALU.subtract, ALU.mult))
                settle()
                mark(dve.tensor_scalar(z[:, :], z[:, :], affine[:, 0:1], affine[:, 1:2], ALU.mult, ALU.add))
                settle()
                dve.tensor_scalar(z[:, :], z[:, :], 0.0, None, ALU.max).then_inc(tanh_in, 1)
                dve.wait_ge(tanh_out, 1)
                dve.tensor_scalar(z[:, :], z[:, :], 0.5, 0.5, ALU.mult, ALU.add).then_inc(map_in, 1)
                dve.wait_ge(map_full, 1)
                mark(dve.tensor_copy(amap[:, :, :, :],
                                     bank[0][:, 0:DC * SETS * B].rearrange("p (c s b) -> p c s b", c=DC, s=SETS)))
                settle()
                for c in range(DC):
                    for s, t in enumerate((fc, fo)):
                        v = t[:, c, :].rearrange("p (b n) -> p b n", b=B)
                        mark(dve.tensor_tensor(v, v, amap[:, c, s, :].rearrange("p (b o) -> p b o", o=1)
                                               .to_broadcast([P, B, P]), ALU.mult))
                    settle()
                    dve.tensor_tensor(fc[:, c, :], fc[:, c, :], fo[:, c, :], ALU.add).then_inc(out_ready, 1)
                for b in range(B):
                    dve.wait_ge(back_full, b + 1)
                    dve.tensor_tensor(x[:, b, :], x[:, b, :], bank[b][:, :], ALU.add).then_inc(added, 1)


def routed_ffn(core, dram, name, top_k, softmax, base, scaling):
    nc, x, bank = core.nc, core.x, core.bank
    E, R = 8, 16
    with ExitStack() as ctx:
        sb = lambda n, shape, dt=F32: core.sb(ctx, name + "_" + n, shape, dt)
        sem = lambda n: core.sem(name + "_" + n)
        xn, xt = sb("xn", [P, B, D]), sb("xt", [P, DC, T])
        w_a, w_b = sb("w_a", [P, DC, P + E]), sb("w_b", [P, D])
        p, wide, wide2 = sb("p", [P, B, E]), sb("wide", [P, B, E, E]), sb("wide2", [P, B, E, E])
        before = sb("before", [P, 1, E, E])
        red, rank, weight = sb("red", [P, B]), sb("rank", [P, B, E]), sb("weight", [P, B, E])
        h, ht = sb("h", [P, B, E, R]), sb("ht", [P, T])
        loaded, base_loaded, made, before_done = sem("loaded"), sem("base_loaded"), sem("made"), sem("before_done")
        if base:
            w_base, bias = sb("w_base", [P, DC, D]), sb("bias", [P, D])

        def loads(sp):
            sp.dma_start(w_a[:, :, :], dram[name + "_a"]).then_inc(loaded, 16)
            sp.dma_start(w_b[:, :], dram[name + "_b"]).then_inc(loaded, 16)
            if base:
                sp.dma_start(w_base[:, :, :], dram[name + "_base"]).then_inc(base_loaded, 16)
                sp.dma_start(bias[:, :], dram[name + "_bias"]).then_inc(base_loaded, 16)

        norm_stage(core, xn, xt, loads)

        a_full, a_read, step, exp_in, exp_out = sem("a_full"), sem("a_read"), sem("step"), sem("exp_in"), sem("exp_out")
        h_done, t_full, t_done, o_full, o_read, biased = (sem("h_done"), sem("t_full"), sem("t_done"), sem("o_full"),
                                                          sem("o_read"), sem("biased"))
        low = lambda b: bank[b // 2][:, (b % 2) * (P + E):(b % 2) * (P + E) + P]
        logits = lambda n: bank[n][:, 0:2 * (P + E)].rearrange("p (b m) -> p b m", b=2)[:, :, P:P + E]
        with nc.Block() as block:

            @block.gpsimd
            def _(pool):
                pool.memset(before[:, :, :, :], 1.0).then_inc(made, 1)
                pool.wait_ge(made, 1)
                pool.affine_select(out=before[:, 0, :, :], in_=before[:, 0, :, :], compare_op=ALU.is_gt, fill=0.0,
                                   base=0, pattern=[[1, E], [-1, E]], channel_multiplier=0).then_inc(before_done, 1)
                if base:
                    pool.wait_ge(base_loaded, 32)
                    for b in range(B):
                        pool.tensor_tensor(x[:, b, :], x[:, b, :], bias[:, :], ALU.add).then_inc(biased, 1)

            @block.tensor
            def _(pe):
                pe.wait_ge(loaded, 32)
                for b in range(B):
                    for c in range(DC):
                        mm = product(pe, bank[b // 2][:, (b % 2) * (P + E):(b % 2 + 1) * (P + E)],
                                     [xt[:, c, b * P:(b + 1) * P]], [w_a[:, c, :]], c == 0, c == DC - 1)
                    if b % 2:
                        mm.then_inc(a_full, 1)

                def base_product(b):
                    wait(pe, o_read, b - 3)
                    for c in range(DC):
                        product(pe, bank[4 + b % 4][:, :], [xt[:, c, b * P:(b + 1) * P]], [w_base[:, c, :]], c == 0,
                                False)

                if base:
                    pe.wait_ge(base_loaded, 32)
                    for b in range(4):
                        base_product(b)
                for half in range(2):
                    pe.wait_ge(h_done, half + 1)
                    for y in range(BH):
                        b = half * BH + y
                        mm = pe.transpose(bank[half][:, y * P:(y + 1) * P], h[:, b, :, :].rearrange("p e r -> p (e r)"),
                                          core.ident[:, :])
                    mm.then_inc(t_full, 1)
                for b in range(B):
                    pe.wait_ge(t_done, b // BH + 1)
                    if b >= 4 and base:
                        base_product(b)
                    elif b >= 4:
                        pe.wait_ge(o_read, b - 3)
                    product(pe, bank[4 + b % 4][:, :], [ht[:, b * P:(b + 1) * P]], [w_b[:, :]], not base, True
                            ).then_inc(o_full, 1)

            @block.scalar
            def _(act):
                if softmax:
                    act.wait_ge(exp_in, 1)
                    act.activation(p[:, :, :], p[:, :, :], ACT.Exp).then_inc(exp_out, 1)
                for half in range(2):
                    act.wait_ge(t_full, half + 1)
                    act.activation(ht[:, half * HALF:(half + 1) * HALF], bank[half][:, :], ACT.Copy).then_inc(t_done, 1)

            @block.vector
            def _(dve):
                steps = [0]

                def then(instruction):
                    steps[0] += 1
                    instruction.then_inc(step, 1)
                    dve.wait_ge(step, steps[0])

                over_e = lambda t: t[:, :].rearrange("p (b o) -> p b o", o=1).to_broadcast([P, B, E])
                for n in range(4):
                    dve.wait_ge(a_full, n + 1)
                    dve.tensor_copy(p[:, 2 * n:2 * n + 2, :], logits(n)).then_inc(a_read, 1)
                dve.wait_ge(a_read, 4)
                if softmax:
                    then(dve.tensor_reduce(red[:, :], p[:, :, :], AX.X, ALU.max))
                    dve.tensor_tensor(p[:, :, :], p[:, :, :], over_e(red), ALU.subtract).then_inc(exp_in, 1)
                    dve.wait_ge(exp_out, 1)
                    then(dve.tensor_reduce(red[:, :], p[:, :, :], AX.X, ALU.add))
                    then(dve.reciprocal(red[:, :], red[:, :]))
                    then(dve.tensor_tensor(p[:, :, :], p[:, :, :], over_e(red), ALU.mult))
                other = p[:, :, :].rearrange("p b (o e) -> p b o e", o=1).to_broadcast([P, B, E, E])
                own = p[:, :, :].rearrange("p b (e o) -> p b e o", o=1).to_broadcast([P, B, E, E])
                dve.tensor_tensor(wide[:, :, :, :], other, own, ALU.is_gt).then_inc(step, 1)
                dve.tensor_tensor(wide2[:, :, :, :], other, own, ALU.is_equal).then_inc(step, 1)
                steps[0] += 2
                dve.wait_ge(step, steps[0])
                dve.wait_ge(before_done, 1)
                then(dve.tensor_tensor(wide2[:, :, :, :], wide2[:, :, :, :], before[:, :, :, :].to_broadcast([P, B, E, E]),
                                       ALU.mult))
                then(dve.tensor_tensor(wide[:, :, :, :], wide[:, :, :, :], wide2[:, :, :, :], ALU.add))
                then(dve.tensor_reduce(rank[:, :, :], wide[:, :, :, :], AX.X, ALU.add))
                then(dve.scalar_tensor_tensor(weight[:, :, :], rank[:, :, :], float(top_k), p[:, :, :], ALU.is_lt,
                                              ALU.mult))
                if softmax:
                    then(dve.tensor_reduce(red[:, :], weight[:, :, :], AX.X, ALU.add))
                    then(dve.reciprocal(red[:, :], red[:, :]))
                    then(dve.scalar_tensor_tensor(weight[:, :, :], weight[:, :, :], scaling, over_e(red), ALU.mult,
                                                  ALU.mult))
                for b in range(B):
                    mm = dve.tensor_tensor(h[:, b, :, :], low(b).rearrange("p (e r) -> p e r", e=E),
                                           weight[:, b, :].rearrange("p (e o) -> p e o", o=1).to_broadcast([P, E, R]),
                                           ALU.mult)
                    if b == B - 1:
                        mm.then_inc(h_done, 2)
                if base:
                    dve.wait_ge(biased, B)
                for b in range(B):
                    dve.wait_ge(o_full, b + 1)
                    dve.tensor_tensor(x[:, b, :], x[:, b, :], bank[4 + b % 4][:, :], ALU.add).then_inc(o_read, 1)


def l2_ffn(core, dram):
    routed_ffn(core, dram, "l2f", 2, True, True, 2.0)


def l3_ffn(core, dram):
    routed_ffn(core, dram, "l3f", 1, False, False, 1.0)


def l3_attention(core, dram):
    nc, x, bank = core.nc, core.x, core.bank
    GROUPS, G = 8, 4
    HP = P // 2
    SCALE = 1.0 / float(np.sqrt(P))
    with ExitStack() as ctx:
        sb = lambda name, shape, dt=F32: core.sb(ctx, "l3x_" + name, shape, dt)
        pair = lambda name, shape: core.pair(ctx, "l3x_" + name, shape)
        sem = lambda name: core.sem("l3x_" + name)
        qin, cin = pair("qin", [P, DC, T]), pair("cin", [P, DC, T])

        with ExitStack() as ctx1:
            xn, xt = core.sb(ctx1, "l3x_xn", [P, B, D]), core.sb(ctx1, "l3x_xt", [P, DC, T])
            ctx_raw = core.sb(ctx1, "l3x_ctx_raw", [P, DC, T])
            ctx_loaded, in_hi, ctx_lo, in_lo = sem("ctx_loaded"), sem("in_hi"), sem("ctx_lo"), sem("in_lo")

            def loads(sp):
                sp.dma_start(ctx_raw[:, :, :], dram["ctx_t"]).then_inc(ctx_loaded, 16)

            norm_stage(core, xn, xt, loads)
            with nc.Block() as block:

                @block.scalar
                def _(act):
                    for c in range(DC):
                        act.activation(qin[0][:, c, :], xt[:, c, :], ACT.Copy).then_inc(in_hi, 1)
                    act.wait_ge(ctx_loaded, 16)
                    for c in range(DC):
                        act.activation(cin[0][:, c, :], ctx_raw[:, c, :], ACT.Copy).then_inc(in_hi, 1)

                @block.vector
                def _(dve):
                    for c in range(DC):
                        dve.wait_ge(in_hi, c + 1)
                        dve.tensor_tensor(qin[1][:, c, :], xt[:, c, :], as_f32(qin[0][:, c, :]), ALU.subtract
                                          ).then_inc(in_lo, 1)
                    for c in range(DC):
                        dve.wait_ge(in_hi, DC + c + 1)
                        dve.tensor_tensor(cin[1][:, c, :], ctx_raw[:, c, :], as_f32(cin[0][:, c, :]), ALU.subtract
                                          ).then_inc(ctx_lo, 1)

        raw_kv, raw_q, raw_o = sb("raw_kv", [P, 2, DC, P]), sb("raw_q", [P, 2, DC, P]), sb("raw_o", [P, 2, D])
        w_kv = pair("w_kv", [P, 2, DC, P])
        w_q = [pair("w_q0", [P, 2, DC, P]), pair("w_q1", [P, 2, DC, P])]
        w_o = pair("w_o", [P, 2, D])
        q = [sb("q0", [P, T]), sb("q1", [P, T])]
        k, vt, v = sb("k", [P, T]), sb("vt", [P, T]), sb("v", [P, B, P])
        rope = sb("rope", [P, 2, P])
        cosine = [sb("cosine0", [P, HALF]), sb("cosine1", [P, HALF])]
        cross = [sb("cross0", [P, HALF]), sb("cross1", [P, HALF])]
        probs = [sb("probs0", [P, B, P]), sb("probs1", [P, B, P])]
        probs_t = sb("probs_t", [P, B, P])
        heads = [pair("heads01", [P, 2, T]), pair("heads23", [P, 2, T])]
        mask = sb("mask", [P, B, P])
        top, row_sum, inv_sum = sb("top", [P, B]), sb("row_sum", [P, B]), sb("inv_sum", [P, B])

        mask_loaded, rope_loaded = sem("mask_loaded"), sem("rope_loaded")
        kv_loaded, kv_hi, kv_ready = sem("kv_loaded"), sem("kv_hi"), sem("kv_ready")
        q_loaded, q_hi, q_ready = sem("q_loaded"), sem("q_hi"), sem("q_ready")
        o_loaded, o_hi, o_ready = sem("o_loaded"), sem("o_hi"), sem("o_ready")
        ring_full, ring_drained = sem("ring_full"), sem("ring_drained")
        rotated = sem("rotated")
        scores_full, scores_read, top_raw, top_ready = (sem("scores_full"), sem("scores_read"), sem("top_raw"),
                                                        sem("top_ready"))
        exp_done, inv_done, probs_ready = sem("exp_done"), sem("inv_done"), sem("probs_ready")
        t_full, t_act, t_dve = sem("t_full"), sem("t_act"), sem("t_dve")
        v_full, v_act, v_dve = sem("v_full"), sem("v_act"), sem("v_dve")
        h_full, h_hi, h_drained = sem("h_full"), sem("h_hi"), sem("h_drained")

        N = GROUPS
        PER = 28
        OFFSET = {"q1": 0, "v": 2, "out23a": 4, "q2": 8, "out23b": 10, "q3": 14, "out01a": 16, "q0": 20, "k": 22,
                  "out01b": 24}
        MISSING = {"q1": 8, "v": 8, "q2": 4}

        def ring_at(g, what):
            first = isinstance(g, int) and g == 0
            return 4 + PER * g - 8 + OFFSET[what] + (MISSING.get(what, 0) if first else 0)

        OUT_LAST = ring_at(N - 1, "q0")

        def rope_at(g, what):
            return 4 + 10 * g + {"q1": 0, "q2": 2, "q3": 4, "q0": 6, "k": 8}[what]

        def turns(body, eng):
            body(0, True, False)
            with eng.Fori(1, N - 1) as g:
                body(g, False, False)
            body(N - 1, False, True)

        with nc.Block() as block:

            @block.sync
            def _(sp):
                def load_q(n, g, s):
                    wait(sp, q_ready, n)
                    for j in range(2):
                        sp.dma_start(raw_q[:, j, :, :], dram["L3_q"][4 * g + 2 * s + j, :, :, :]).then_inc(q_loaded, 16)

                def load_o(u):
                    wait(sp, o_ready, u)
                    sp.dma_start(raw_o[:, :, :], dram["L3_o"][u, :, :, :]).then_inc(o_loaded, 16)

                load_q(0, 0, 0)
                sp.dma_start(rope[:, :, :], dram["L3_rope"]).then_inc(rope_loaded, 16)
                sp.dma_start(raw_kv[:, :, :, :], dram["L3_kv"][0, :, :, :, :]).then_inc(kv_loaded, 16)
                sp.dma_start(mask[:, :, :], dram["L3_mask"]).then_inc(mask_loaded, 16)
                load_q(1, 0, 1)

                def turn(g, first, last):
                    load_o(2 * g)
                    if not last:
                        sp.wait_ge(kv_ready, g + 1)
                        sp.dma_start(raw_kv[:, :, :, :], dram["L3_kv"][g + 1, :, :, :, :]).then_inc(kv_loaded, 16)
                        load_q(2 * g + 2, g + 1, 0)
                    load_o(2 * g + 1)
                    if not last:
                        load_q(2 * g + 3, g + 1, 1)

                turns(turn, sp)

            @block.gpsimd
            def _(pool):
                flat = lambda t: t[:, :, :].rearrange("p a b -> p (a b)")
                flat4 = lambda t: t[:, :, :, :].rearrange("p a b c -> p (a b c)")

                def split_low(n, raw, w, hi, ready):
                    f = flat4 if len(raw.shape) == 4 else flat
                    pool.wait_ge(hi, n + 1)
                    pool.tensor_tensor(f(w[1]), f(raw), as_f32(f(w[0])), ALU.subtract).then_inc(ready, 1)

                def rotate(n, ring, dst, free):
                    wait(pool, scores_full, free)
                    pool.wait_ge(ring_drained, ring + n + 1)
                    pool.tensor_tensor(dst[:, n * HALF:(n + 1) * HALF], cosine[n][:, :], cross[n][:, :], ALU.add
                                       ).then_inc(rotated, 1)

                def rotate_both(ring, dst, free):
                    rotate(0, ring, dst, free)
                    rotate(1, ring, dst, free)

                split_low(0, raw_q, w_q[0], q_hi, q_ready)
                split_low(0, raw_kv, w_kv, kv_hi, kv_ready)
                rotate_both(0, q[0], 0)
                rotate_both(2, k, 0)
                split_low(1, raw_q, w_q[1], q_hi, q_ready)

                def turn(g, first, last):
                    h = G * g
                    rotate_both(ring_at(g, "q1"), q[1], 2 * h)
                    if not last:
                        split_low(g + 1, raw_kv, w_kv, kv_hi, kv_ready)
                    rotate_both(ring_at(g, "q2"), q[0], 2 * h + 2)
                    split_low(2 * g, raw_o, w_o, o_hi, o_ready)
                    if not last:
                        split_low(2 * g + 2, raw_q, w_q[0], q_hi, q_ready)
                    rotate_both(ring_at(g, "q3"), q[1], 2 * h + 4)
                    if not last:
                        rotate_both(ring_at(g, "q0"), q[0], 2 * h + 6)
                        rotate_both(ring_at(g, "k"), k, 2 * h + 8)
                    split_low(2 * g + 1, raw_o, w_o, o_hi, o_ready)
                    if not last:
                        split_low(2 * g + 3, raw_q, w_q[1], q_hi, q_ready)

                turns(turn, pool)

            @block.tensor
            def _(pe):
                def project(n, at, bk, w, n_w, src):
                    wait(pe, ring_drained, at + n - 3)
                    part = slice(n * HALF, (n + 1) * HALF)
                    for c in range(DC):
                        mm = product(pe, bank[bk + n][:, :], [w[s][:, n_w, c, :] for s in range(2)],
                                     [src[s][:, c, part] for s in range(2)], c == 0, c == DC - 1)
                    mm.then_inc(ring_full, 1)

                def project_both(at, bk, w, n_w, src):
                    project(0, at, bk, w, n_w, src)
                    project(1, at, bk, w, n_w, src)

                def transpose_values(g):
                    pe.wait_ge(ring_drained, ring_at(g, "v") + 2)
                    wait(pe, h_drained, 2 * G * g)
                    for half in range(2):
                        for y in range(BH):
                            b = half * BH + y
                            mm = pe.transpose(bank[6 + half][:, y * P:(y + 1) * P], vt[:, b * P:(b + 1) * P],
                                              core.ident[:, :])
                        mm.then_inc(v_full, 1)

                def scores(h, j, needed):
                    pe.wait_ge(rotated, needed)
                    wait(pe, scores_read, 2 * h)
                    for half in range(2):
                        for y in range(BH):
                            t = slice((half * BH + y) * P, (half * BH + y + 1) * P)
                            mm = product(pe, bank[4 + half][:, y * P:(y + 1) * P], [q[j % 2][:, t]], [k[:, t]], True,
                                         True)
                        mm.then_inc(scores_full, 1)

                def transpose_probs(h, j):
                    pe.wait_ge(probs_ready, h + 1)
                    wait(pe, h_drained, 2 * h)
                    for half in range(2):
                        for y in range(BH):
                            mm = pe.transpose(bank[6 + half][:, y * P:(y + 1) * P], probs[j % 2][:, half * BH + y, :],
                                              core.ident[:, :])
                        mm.then_inc(t_full, 1)

                def weigh_values(h):
                    for half in range(2):
                        pe.wait_ge((t_act, t_dve)[half], h + 1)
                        for y in range(BH):
                            b = half * BH + y
                            mm = product(pe, bank[6 + half][:, y * P:(y + 1) * P], [v[:, b, :]], [probs_t[:, b, :]],
                                         True, True)
                        mm.then_inc(h_full, 1)

                def project_out(u, s, at, batches, first_bank):
                    pe.wait_ge(o_ready, u + 1)
                    pe.wait_ge(h_drained, 4 * u + 4)
                    for n, b in enumerate(batches):
                        wait(pe, ring_drained, at + n - 3)
                        for j in range(2):
                            mm = product(pe, bank[(first_bank + n) % 4][:, :],
                                         [heads[s][t][:, j, b * P:(b + 1) * P] for t in range(2)],
                                         [w_o[t][:, j, :] for t in range(2)], j == 0, j == 1)
                        mm.then_inc(ring_full, 1)

                pe.wait_ge(q_ready, 1)
                project_both(0, 0, w_q[0], 0, qin)
                pe.wait_ge(kv_ready, 1)
                project_both(2, 2, w_kv, 0, cin)

                def step(h, j, needed, at, bk, w, n_w, project_next, weigh_last):
                    scores(h, j, needed)
                    if weigh_last:
                        transpose_probs(h - 1, j + 3)
                    if project_next:
                        project(0, at, bk, w, n_w, qin)
                    if weigh_last:
                        weigh_values(h - 1)
                    if project_next:
                        project(1, at, bk, w, n_w, qin)

                def turn(g, first, last):
                    step(G * g, 0, rope_at(g, "q1"), ring_at(g, "q1"), 0, w_q[0], 1, True, not first)
                    for n in range(2):
                        project(n, ring_at(g, "v"), 2, w_kv, 1, cin)
                    if not first:
                        project_out(2 * g - 1, 1, ring_at(g, "out23a"), range(BH), 0)
                    transpose_values(g)
                    pe.wait_ge(q_ready, 2 * g + 2)
                    pe.wait_ge(v_act, g + 1)
                    pe.wait_ge(v_dve, g + 1)
                    step(G * g + 1, 1, rope_at(g, "q1") + 2, ring_at(g, "q2"), 0, w_q[1], 0, True, True)
                    if not first:
                        project_out(2 * g - 1, 1, ring_at(g, "out23b"), range(BH, B), 2)
                    step(G * g + 2, 2, rope_at(g, "q2") + 2, ring_at(g, "q3"), 2, w_q[1], 1, True, True)
                    project_out(2 * g, 0, ring_at(g, "out01a"), range(BH), 0)
                    if not last:
                        pe.wait_ge(q_ready, 2 * g + 3)
                    step(G * g + 3, 3, rope_at(g, "q3") + 2, ring_at(g, "q0"), 0, w_q[0], 0, not last, True)
                    if not last:
                        pe.wait_ge(kv_ready, g + 2)
                        project_both(ring_at(g, "k"), 2, w_kv, 0, cin)
                    project_out(2 * g, 0, ring_at(g, "out01b") - (4 if last else 0), range(BH, B), 0)

                turns(turn, pe)
                transpose_probs(G * N - 1, 3)
                weigh_values(G * N - 1)
                project_out(2 * N - 1, 1, OUT_LAST + 4, range(B), 0)

            @block.scalar
            def _(act):
                def exps(h, j):
                    act.wait_ge(top_ready, h + 1)
                    wait(act, inv_done, h)
                    for b in range(B):
                        act.activation(probs[j % 2][:, b, :], probs[j % 2][:, b, :], ACT.Exp, bias=top[:, b:b + 1],
                                       accum_out=row_sum[:, b:b + 1]).then_inc(exp_done, 1)

                def split_high(n, raw, w, loaded, per, hi, free):
                    act.wait_ge(loaded, per * (n + 1))
                    wait(act, ring_full, free)
                    sl = tuple(slice(None) for _ in raw.shape)
                    act.activation(w[0][sl], raw[sl], ACT.Copy).then_inc(hi, 1)

                def copy_probs(h):
                    act.wait_ge(t_full, 2 * h + 1)
                    act.activation(probs_t[:, 0:BH, :], bank[6][:, :].rearrange("p (b n) -> p b n", b=BH), ACT.Copy
                                   ).then_inc(t_act, 1)

                def heads_high(h, j):
                    for half in range(2):
                        act.wait_ge(h_full, 2 * h + half + 1)
                        act.activation(heads[j // 2][0][:, j % 2, half * HALF:(half + 1) * HALF], bank[6 + half][:, :],
                                       ACT.Copy).then_inc(h_hi, 1)

                split_high(0, raw_q, w_q[0], q_loaded, 32, q_hi, 0)
                split_high(0, raw_kv, w_kv, kv_loaded, 16, kv_hi, 0)
                split_high(1, raw_q, w_q[1], q_loaded, 32, q_hi, 0)

                def turn(g, first, last):
                    h = G * g
                    if not first:
                        copy_probs(h - 1)
                    exps(h, 0)
                    if not first:
                        wait(act, ring_full, ring_at(g - 1, "out01b") + 4)
                        heads_high(h - 1, 3)
                    if not last:
                        split_high(g + 1, raw_kv, w_kv, kv_loaded, 16, kv_hi, ring_at(g, "v") + 2)
                        split_high(2 * g + 2, raw_q, w_q[0], q_loaded, 32, q_hi, ring_at(g, "q1") + 2)
                    act.wait_ge(v_full, 2 * g + 1)
                    act.activation(v[:, 0:BH, :], bank[6][:, :].rearrange("p (b n) -> p b n", b=BH), ACT.Copy
                                   ).then_inc(v_act, 1)
                    copy_probs(h)
                    exps(h + 1, 1)
                    heads_high(h, 0)
                    split_high(2 * g, raw_o, w_o, o_loaded, 16, o_hi, 0 if first else ring_at(g, "out23b") + 4)
                    copy_probs(h + 1)
                    exps(h + 2, 2)
                    heads_high(h + 1, 1)
                    copy_probs(h + 2)
                    exps(h + 3, 3)
                    heads_high(h + 2, 2)
                    if not last:
                        split_high(2 * g + 3, raw_q, w_q[1], q_loaded, 32, q_hi, ring_at(g, "q3") + 2)
                    split_high(2 * g + 1, raw_o, w_o, o_loaded, 16, o_hi,
                               ring_at(g, "out01b") + 4 - (4 if last else 0))

                turns(turn, act)
                copy_probs(G * N - 1)
                heads_high(G * N - 1, 3)

            @block.vector
            def _(dve):
                def mask_scores(h, j):
                    wait(dve, t_full, 2 * (h - 1))
                    for half in range(2):
                        part = slice(half * BH, (half + 1) * BH)
                        dve.wait_ge(scores_full, 2 * h + half + 1)
                        dve.scalar_tensor_tensor(probs[j % 2][:, part, :],
                                                 bank[4 + half][:, :].rearrange("p (b n) -> p b n", b=BH), SCALE,
                                                 mask[:, part, :], ALU.mult, ALU.add).then_inc(scores_read, 1)
                    dve.wait_ge(scores_read, 2 * h + 2)
                    wait(dve, exp_done, B * h)
                    dve.tensor_reduce(top[:, :], probs[j % 2][:, :, :], AX.X, ALU.max).then_inc(top_raw, 1)
                    dve.wait_ge(top_raw, h + 1)
                    dve.tensor_scalar(top[:, :], top[:, :], -1.0, None, ALU.mult).then_inc(top_ready, 1)

                def normalise(h, j):
                    dve.wait_ge(exp_done, B * (h + 1))
                    dve.reciprocal(inv_sum[:, :], row_sum[:, :]).then_inc(inv_done, 1)
                    dve.wait_ge(inv_done, h + 1)
                    dve.tensor_tensor(probs[j % 2][:, :, :], probs[j % 2][:, :, :],
                                      inv_sum[:, :].rearrange("p (b o) -> p b o", o=1).to_broadcast([P, B, P]),
                                      ALU.mult).then_inc(probs_ready, 1)

                def rotate(n, ring, at, bk):
                    table = lambda part, n: rope[part, n:n + 1, :].to_broadcast([part.stop - part.start, BH, P])
                    low, high, whole = slice(0, HP), slice(HP, P), slice(0, P)
                    src = bank[bk + n][:, :].rearrange("p (b t) -> p b t", b=BH)
                    cos, sine = (t[n][:, :].rearrange("p (b t) -> p b t", b=BH) for t in (cosine, cross))
                    dve.wait_ge(ring_full, ring + n + 1)
                    wait(dve, rotated, at + n - 1)
                    dve.tensor_tensor(cos, src, table(whole, 0), ALU.mult)
                    dve.tensor_tensor(sine[high, :, :], src[low, :, :], table(low, 1), ALU.mult)
                    dve.tensor_tensor(sine[low, :, :], src[high, :, :], table(high, 1), ALU.mult
                                      ).then_inc(ring_drained, 1)

                def copy_probs(h):
                    dve.wait_ge(t_full, 2 * h + 2)
                    dve.tensor_copy(probs_t[:, BH:B, :], bank[7][:, :].rearrange("p (b n) -> p b n", b=BH)
                                    ).then_inc(t_dve, 1)

                def heads_low(h, j):
                    for half in range(2):
                        part = slice(half * HALF, (half + 1) * HALF)
                        hi, lo = heads[j // 2]
                        dve.wait_ge(h_hi, 2 * h + half + 1)
                        dve.tensor_tensor(lo[:, j % 2, part], bank[6 + half][:, :], as_f32(hi[:, j % 2, part]),
                                          ALU.subtract).then_inc(h_drained, 1)

                def add_out(at, batches, first_bank):
                    for n, b in enumerate(batches):
                        dve.wait_ge(ring_full, at + n + 1)
                        dve.tensor_tensor(x[:, b, :], x[:, b, :], bank[(first_bank + n) % 4][:, :], ALU.add
                                          ).then_inc(ring_drained, 1)

                dve.wait_ge(rope_loaded, 16)
                for n in range(2):
                    rotate(n, 0, 0, 0)
                for n in range(2):
                    rotate(n, 2, 2, 2)
                dve.wait_ge(mask_loaded, 16)

                def step(h, j, ring, at, bk, rotate_next, weigh_last):
                    mask_scores(h, j)
                    if weigh_last:
                        copy_probs(h - 1)
                    if rotate_next:
                        rotate(0, ring, at, bk)
                    if weigh_last:
                        heads_low(h - 1, (j + 3) % 4)
                    if rotate_next:
                        rotate(1, ring, at, bk)
                    normalise(h, j)

                def turn(g, first, last):
                    step(G * g, 0, ring_at(g, "q1"), rope_at(g, "q1"), 0, True, not first)
                    for n in range(2):
                        dve.wait_ge(ring_full, ring_at(g, "v") + n + 1)
                        dve.tensor_copy(vt[:, n * HALF:(n + 1) * HALF], bank[2 + n][:, :]).then_inc(ring_drained, 1)
                    if not first:
                        add_out(ring_at(g, "out23a"), range(BH), 0)
                    dve.wait_ge(v_full, 2 * g + 2)
                    dve.tensor_copy(v[:, BH:B, :], bank[7][:, :].rearrange("p (b n) -> p b n", b=BH)
                                    ).then_inc(v_dve, 1)
                    step(G * g + 1, 1, ring_at(g, "q2"), rope_at(g, "q2"), 0, True, True)
                    if not first:
                        add_out(ring_at(g, "out23b"), range(BH, B), 2)
                    step(G * g + 2, 2, ring_at(g, "q3"), rope_at(g, "q3"), 2, True, True)
                    add_out(ring_at(g, "out01a"), range(BH), 0)
                    step(G * g + 3, 3, ring_at(g, "q0"), rope_at(g, "q0"), 0, not last, True)
                    if not last:
                        for n in range(2):
                            rotate(n, ring_at(g, "k"), rope_at(g, "k"), 2)
                    add_out(ring_at(g, "out01b") - (4 if last else 0), range(BH, B), 0)

                turns(turn, dve)
                copy_probs(G * N - 1)
                heads_low(G * N - 1, 3)
                add_out(OUT_LAST + 4, range(B), 0)


def build(nc, dram, out):
    ctx = ExitStack()
    with ctx:
        core = Core(nc, ctx)
        with ExitStack() as early:
            core.hold_first(early)
            l0_attention(core, dram)
            core.hold_weights(early)
            l0_ffn(core, dram)
            l1_attention(core, dram)
        l1_ffn(core, dram)
        core.free_semaphores()
        l2_attention(core, dram)
        l2_ffn(core, dram)
        l3_attention(core, dram)
        l3_ffn(core, dram)
        stored = core.sem("stored")
        with nc.Block() as block:

            @block.sync
            def _(sp):
                for b in range(B):
                    sp.dma_start(out[b, :, :], core.x[:, b, :]).then_inc(stored, 16)
                sp.wait_ge(stored, 16 * B)


def laid_out(inputs):
    a = {name: np.asarray(value) for name, value in inputs.items()}
    chunks = lambda w: w.reshape(DC, P, -1).transpose(1, 0, 2)
    got = {"x": a["x"]}
    got["ctx_t"] = chunks(a["ctx_4096"].reshape(T, D).T)
    got["mask_b_q"] = a["mask_BxSxS2_bk0"].transpose(1, 0, 2)
    got["L0_xattn_position_bias"] = a["L0_xattn_position_bias"]
    got["L0_xattn_ln_weight"] = a["L0_xattn_ln_weight"].reshape(DC, P).T
    qk = np.stack([a["L0_xattn_w_q"], a["L0_xattn_w_k"]]).reshape(2, 16, 2, P, DC, P)
    got["L0_qk"] = qk.transpose(1, 2, 5, 0, 4, 3)
    got["L0_v"] = a["L0_xattn_w_v"].reshape(16, 2 * P, DC, P).transpose(0, 3, 2, 1)
    got["L0_o"] = a["L0_xattn_w_out"].T.reshape(16, 2, P, D).transpose(0, 2, 1, 3)
    got["L0f_wq"] = chunks(a["L0_ffn_Wq"].T)
    got["L0f_keys"] = a["L0_ffn_lora_keys"].T
    got["L0f_down"] = chunks(a["L0_ffn_lora_down"].transpose(1, 0, 2).reshape(D, -1))
    got["L0f_org"] = chunks(a["L0_ffn_W_org"].T)
    got["L0f_up"] = chunks(a["L0_ffn_lora_up"].reshape(-1, D))
    got["L1x_wq"] = chunks(a["L1_xattn_Wq"].reshape(D, 8, 4, 16).transpose(0, 2, 1, 3).reshape(D, D))
    got["L1x_wkv"] = chunks(np.concatenate([a["L1_xattn_Wk"], a["L1_xattn_Wv"]], axis=1))
    got["L1x_wo"] = chunks(a["L1_xattn_Wo"].reshape(8, 4, 16, D).transpose(1, 0, 2, 3).reshape(D, D))
    got["L1f_wq"] = chunks(a["L1_ffn_Wq"].T)
    got["L1f_wr"] = a["L1_ffn_Wr"].T
    got["L1f_keys"] = a["L1_ffn_aux_keys"].T
    got["L1f_values"] = chunks(a["L1_ffn_aux_values"].T)
    got["L1f_wvd"] = chunks(a["L1_ffn_Wvd"].T)
    got["L1f_wvu"] = a["L1_ffn_Wvu"].T
    got["L1f_wu1"] = chunks(a["L1_ffn_Wu1"].T)
    got["L1f_wu2"] = a["L1_ffn_Wu2"].T
    on_all = [np.broadcast_to(a[n].reshape(1), (P,)) for n in ("L1_ffn_bu2", "L1_ffn_gate_w1", "L1_ffn_gate_bias")]
    got["L1f_consts"] = np.stack([a["L1_ffn_bu1"]] + on_all, axis=1)
    got["L1f_log_rel"] = np.broadcast_to(a["L1_ffn_log_rel"], (P, 1, P))
    got["l2f_a"] = chunks(np.concatenate([a["L2_ffn_lora_A"].reshape(P, D), a["L2_ffn_W_router"]]).T)
    got["l2f_b"] = a["L2_ffn_lora_B"].transpose(0, 2, 1).reshape(P, D)
    got["l2f_base"] = chunks(a["L2_ffn_W_base"].T)
    got["l2f_bias"] = np.broadcast_to(a["L2_ffn_b_base"], (P, D))
    got["l3f_a"] = chunks(np.concatenate([a["L3_ffn_A"].reshape(P, D), a["L3_ffn_route_w"]]).T)
    got["l3f_b"] = a["L3_ffn_Bw"].transpose(0, 2, 1).reshape(P, D)
    rank = a["ctx_4096"][:, ::-1, :].reshape(B, P, DC, P).transpose(2, 0, 3, 1).reshape(L0_PAIRS, TPT, P, P)
    got["ctx_rank"] = rank.transpose(0, 2, 1, 3)
    got["L2x_taps"] = np.repeat(a["L2_xattn_conv_w"][0], 16, axis=0)
    got["L2x_affine"] = np.broadcast_to(np.concatenate([a["L2_xattn_bn_gamma"], a["L2_xattn_bn_beta"]]), (16, 2))
    got["L3_q"] = a["L3_xattn_wq"].reshape(DC, P, 32, P).transpose(2, 1, 0, 3)
    got["L3_kv"] = np.stack([a["L3_xattn_wk"], a["L3_xattn_wv"]]).reshape(2, DC, P, 8, P).transpose(3, 2, 0, 1, 4)
    got["L3_o"] = a["L3_xattn_wo"].reshape(16, 2, P, D).transpose(0, 2, 1, 3)
    got["L3_mask"] = a["mask_BxSxS2_ff0"].transpose(1, 0, 2)
    angle = np.arange(P)[None, :] * (1.0 / 10000.0 ** (np.arange(0, P, 2) / P))[:, None]
    got["L3_rope"] = np.stack([np.tile(np.cos(angle), (2, 1)), np.concatenate([np.sin(angle), -np.sin(angle)])],
                              axis=1).astype(np.float32)
    return {name: np.ascontiguousarray(value) for name, value in got.items()}


def kernel(**inputs):
    import concourse.bacc as bacc
    from concourse.bass_utils import run_bass_kernel_spmd

    nc = bacc.Bacc("TRN2", target_bir_lowering=False, num_devices=1)
    arrays = laid_out(inputs)
    dram = {name: nc.dram_tensor(name + "_dram", a.shape, mybir.dt.from_np(a.dtype), kind="ExternalInput").ap()
            for name, a in arrays.items()}
    out = nc.dram_tensor("out_dram", (B, P, D), F32, kind="ExternalOutput").ap()
    build(nc, dram, out)
    result = run_bass_kernel_spmd(nc, [{name + "_dram": a for name, a in arrays.items()}], core_ids=[0])
    return result.results[0]["out_dram"]
```

```python
import numpy as np
import concourse.bass as bass
from concourse import mybir
from contextlib import ExitStack

F32 = mybir.dt.float32
F32R = mybir.dt.float32r
U8 = mybir.dt.uint8
ALU = mybir.AluOpType
ACT = mybir.ActivationFunctionType
AX = mybir.AxisListType

P = 128
B = 8
D = 512
DC = D // P
T = B * P
BH = B // 2
HALF = BH * P
EPS = 1e-5
MASKED = -1e30
FLOOR = -1e29


def wait(eng, sem, value):
    if not (isinstance(value, int) and value <= 0):
        eng.wait_ge(sem, value)


def product(pe, out, lhs, rhs, start, stop):
    if len(lhs) == 1:
        return pe.matmul(out, lhs[0], rhs[0], start=start, stop=stop)
    pe.matmul(out, lhs[0], rhs[0], start=start, stop=False)
    pe.matmul(out, lhs[0], rhs[1], start=False, stop=False)
    return pe.matmul(out, lhs[1], rhs[0], start=False, stop=stop)


def as_f32(ap):
    return ap.bitcast(F32)


class Core:

    def __init__(self, nc, ctx):
        self.nc, self.ctx = nc, ctx
        self.held = []
        self.x = self.sb(ctx, "x", [P, B, D])
        self.ident = self.sb(ctx, "ident", [P, P])
        self.neg_half = self.sb(ctx, "neg_half", [P, B])
        self.stats = self.sb(ctx, "stats", [P, B, 6])
        self.mv = self.sb(ctx, "mv", [P, B, 2])
        self.var_eps = self.sb(ctx, "var_eps", [P, B])
        self.rstd = self.sb(ctx, "rstd", [P, B])
        self.crucial = self.sb(ctx, "crucial", [P, DC * B, P], U8)
        self.bank = [ctx.enter_context(nc.psum_tensor(f"bank{n}", [P, 512], F32)) for n in range(8)]
        self.const_ready = self.sem("const_ready")
        self.stats_done = self.sem("stats_done")
        self.mv_done = self.sem("mv_done")
        self.var_done = self.sem("var_done")
        self.rstd_done = self.sem("rstd_done")
        self.xn_done = self.sem("xn_done")
        self.xt_full = self.sem("xt_full")
        self.xt_copied = self.sem("xt_copied")
        self.xt_hi = self.sem("xt_hi")
        self.norms, self.split_norms = 0, 0
        self.held = []

    def hold_first(self, ctx):
        self.cin = self.pair(ctx, "ctx", [P, DC, T])

    def hold_kv(self, ctx):
        self.l1_wkv = self.pair(ctx, "l1_wkv", [P, DC, 2 * P])
        self.l1_kv_split = self.sem("l1_kv_split")

    def hold_second(self, ctx):
        self.cin2 = self.pair(ctx, "ctx2", [P, DC, T])
        self.ctx2_split = self.sem("ctx2_split")

    def statistics(self, dve, b):
        dve.bn_stats(self.stats[:, b, :], self.x[:, b, :]).then_inc(self.stats_done, 1)

    def sb(self, ctx, name, shape, dt=F32):
        return ctx.enter_context(self.nc.sbuf_tensor(name, shape, dt))

    def pair(self, ctx, name, shape):
        return (self.sb(ctx, name + "_hi", shape, F32R), self.sb(ctx, name + "_lo", shape, F32R))

    def sem(self, name):
        handle = self.nc.alloc_semaphore(name=name)
        self.held.append(handle)
        return handle

    def free_semaphores(self):
        self.nc.all_engine_barrier()
        self.nc.clear_and_free_semaphores(self.held)
        self.nc.all_engine_barrier()
        self.held = []


def norm_stage(core, xn, xt, loads, act_first=None, pool_then=None, act_then=None, dve_then=None):
    nc, n, n_split = core.nc, core.norms, core.split_norms
    core.norms += 1
    split = isinstance(xt, tuple)
    core.split_norms += split
    with nc.Block() as block:

        @block.sync
        def _(sp):
            loads(sp)

        @block.vector
        def _(dve):
            dve.wait_ge(core.stats_done, B * (n + 1))
            for b in range(B):
                dve.bn_aggr(core.mv[:, b, :], core.stats[:, b, :]).then_inc(core.mv_done, 1)
            dve.wait_ge(core.mv_done, B * (n + 1))
            dve.tensor_scalar_add(core.var_eps[:, :], core.mv[:, :, 1], EPS).then_inc(core.var_done, 1)
            dve.wait_ge(core.rstd_done, n + 1)
            for b in range(B):
                dve.tensor_scalar(xn[:, b, :], core.x[:, b, :], core.mv[:, b, 0:1], core.rstd[:, b:b + 1],
                                  ALU.subtract, ALU.mult).then_inc(core.xn_done, 1)
            if split:
                for b in range(B):
                    dve.wait_ge(core.xt_hi, B * n_split + b + 1)
                    dve.tensor_tensor(xt[1][:, :, b * P:(b + 1) * P],
                                      core.bank[b][:, :].rearrange("p (c t) -> p c t", c=DC),
                                      as_f32(xt[0][:, :, b * P:(b + 1) * P]), ALU.subtract).then_inc(core.xt_copied, 1)
                if dve_then:
                    dve_then(dve)
                return
            for b in range(1, B, 2):
                dve.wait_ge(core.xt_full, B * n + b + 1)
                dve.tensor_copy(xt[:, :, b * P:(b + 1) * P], core.bank[b][:, :].rearrange("p (c t) -> p c t", c=DC)
                                ).then_inc(core.xt_copied, 1)

        @block.gpsimd
        def _(pool):
            pool.wait_ge(core.var_done, n + 1)
            pool.tensor_tensor(core.rstd[:, :], core.var_eps[:, :], core.neg_half[:, :], ALU.pow
                               ).then_inc(core.rstd_done, 1)
            if pool_then:
                pool_then(pool)

        @block.tensor
        def _(pe):
            for b in range(B):
                pe.wait_ge(core.xn_done, B * n + b + 1)
                for c in range(DC):
                    last = pe.transpose(core.bank[b][:, c * P:(c + 1) * P], xn[:, b, c * P:(c + 1) * P],
                                        core.ident[:, :])
                last.then_inc(core.xt_full, 1)

        @block.scalar
        def _(act):
            if act_first:
                act_first(act)
            if split:
                for b in range(B):
                    act.wait_ge(core.xt_full, B * n + b + 1)
                    act.activation(xt[0][:, :, b * P:(b + 1) * P],
                                   core.bank[b][:, :].rearrange("p (c t) -> p c t", c=DC), ACT.Copy
                                   ).then_inc(core.xt_hi, 1)
                if act_then:
                    act_then(act)
                return
            for b in range(0, B, 2):
                act.wait_ge(core.xt_full, B * n + b + 1)
                act.activation(xt[:, :, b * P:(b + 1) * P], core.bank[b][:, :].rearrange("p (c t) -> p c t", c=DC),
                               ACT.Copy).then_inc(core.xt_copied, 1)


L0_HEADS = 32
L0_PAIRS = L0_HEADS // 2
CRUCIAL = 76
OTHERS = P - CRUCIAL
ROUNDS, REST = OTHERS // 8, OTHERS % 8
TAKEN = -3e38
TILES = DC * B
TPT = TILES // L0_PAIRS


def l0_attention(core, dram):
    nc, x, bank = core.nc, core.x, core.bank
    with ExitStack() as ctx:
        sb = lambda name, shape, dt=F32: core.sb(ctx, "l0x_" + name, shape, dt)
        pair = lambda name, shape: core.pair(ctx, "l0x_" + name, shape)
        sem = lambda name: core.sem("l0x_" + name)

        qin = pair("qin", [P, DC, T])
        cin = core.cin
        w_qk = [pair("w_qk0", [P, 2, DC, P]), pair("w_qk1", [P, 2, DC, P])]
        w_v = pair("w_v", [P, DC, 2 * P])
        w_o = pair("w_o", [P, 2, D])

        raw_qk = [sb("raw_qk0", [P, 2, DC, P]), sb("raw_qk1", [P, 2, DC, P])]
        raw_v, raw_o = sb("raw_v", [P, DC, 2 * P]), sb("raw_o", [P, 2, D])
        h = sb("h", [P, B, D])
        qk_loaded, qk_hi, qk_ready = ([sem(f"{s}{j}") for j in range(2)] for s in ("qk_loaded", "qk_hi", "qk_ready"))
        v_loaded, v_hi, v_ready = sem("v_loaded"), sem("v_hi"), sem("v_ready")
        h_done = sem("h_done")

        FIRST_H = 3

        def hidden(dve, b):
            dve.tensor_scalar(h[:, b, :], x[:, b, :], core.mv[:, b, 0:1], core.rstd[:, b:b + 1], ALU.subtract, ALU.mult
                              ).then_inc(h_done, 1)

        with ExitStack() as ctx1:
            xr = core.sb(ctx1, "l0x_xr", [P, B, D])
            ctx_raw = core.sb(ctx1, "l0x_ctx_raw", [P, DC, T])
            lnw = core.sb(ctx1, "l0x_lnw", [P, DC])
            ms = core.sb(ctx1, "l0x_ms", [P, B])
            r2 = core.sb(ctx1, "l0x_r2", [P, B])
            x_loaded = [sem(f"x_loaded{b}") for b in range(B)]
            rr_done = sem("rr_done")
            ctx_loaded, lnw_loaded = sem("ctx_loaded"), sem("lnw_loaded")
            ms1, ms2, r2_done = sem("ms1"), sem("ms2"), sem("r2_done")
            xt_hi, ctx_hi, ctx_lo = sem("xt_hi"), sem("ctx_hi"), sem("ctx_lo")
            cst = sem("cst")
            with nc.Block() as block:

                @block.sync
                def _(sp):
                    for b in range(B):
                        sp.dma_start(x[:, b, :], dram["x"][b, :, :]).then_inc(x_loaded[b], 16)
                    sp.dma_start(lnw[:, :], dram["L0_xattn_ln_weight"]).then_inc(lnw_loaded, 16)
                    sp.dma_start(ctx_raw[:, :, :], dram["ctx_t"]).then_inc(ctx_loaded, 16)
                    for j in range(2):
                        sp.dma_start(raw_qk[j][:, :, :, :], dram["L0_qk"][0, j, :, :, :, :]).then_inc(qk_loaded[j], 16)
                    sp.dma_start(raw_v[:, :, :], dram["L0_v"][0, :, :, :]).then_inc(v_loaded, 16)

                @block.gpsimd
                def _(pool):
                    pool.memset(core.neg_half[:, :], -0.5).then_inc(core.const_ready, 1)
                    pool.memset(core.ident[:, :], 0.0).then_inc(cst, 1)
                    pool.wait_ge(cst, 1)
                    pool.affine_select(out=core.ident[:, :], in_=core.ident[:, :], compare_op=ALU.not_equal, fill=1.0,
                                       base=0, pattern=[[-1, P]], channel_multiplier=1).then_inc(core.const_ready, 1)
                    pool.wait_ge(core.const_ready, 2)
                    pool.wait_ge(core.var_done, 1)
                    pool.tensor_tensor(core.rstd[:, :], core.var_eps[:, :], core.neg_half[:, :], ALU.pow
                                       ).then_inc(core.rstd_done, 1)
                    pool.wait_ge(ms2, 1)
                    pool.tensor_tensor(r2[:, :], ms[:, :], core.neg_half[:, :], ALU.pow).then_inc(r2_done, 1)
                    for c in range(DC):
                        pool.wait_ge(ctx_hi, c + 1)
                        pool.tensor_tensor(cin[1][:, c, :], ctx_raw[:, c, :], as_f32(cin[0][:, c, :]), ALU.subtract
                                           ).then_inc(ctx_lo, 1)
                    pool.wait_ge(qk_hi[0], 1)
                    pool.tensor_tensor(w_qk[0][1][:, :, :, :], raw_qk[0][:, :, :, :], as_f32(w_qk[0][0][:, :, :, :]),
                                       ALU.subtract).then_inc(qk_ready[0], 1)

                @block.vector
                def _(dve):
                    for b in range(B):
                        dve.wait_ge(x_loaded[b], 16)
                        core.statistics(dve, b)
                    dve.wait_ge(core.stats_done, B)
                    for b in range(B):
                        dve.bn_aggr(core.mv[:, b, :], core.stats[:, b, :]).then_inc(core.mv_done, 1)
                    dve.wait_ge(core.mv_done, B)
                    dve.tensor_scalar_add(core.var_eps[:, :], core.mv[:, :, 1], EPS).then_inc(core.var_done, 1)
                    dve.wait_ge(core.rstd_done, 1)
                    dve.tensor_tensor(ms[:, :], core.mv[:, :, 1], core.rstd[:, :], ALU.mult).then_inc(ms1, 1)
                    dve.wait_ge(ms1, 1)
                    dve.tensor_tensor(ms[:, :], ms[:, :], core.rstd[:, :], ALU.mult).then_inc(ms1, 1)
                    dve.wait_ge(ms1, 2)
                    dve.tensor_scalar_add(ms[:, :], ms[:, :], EPS).then_inc(ms2, 1)

                    for b in range(FIRST_H):
                        hidden(dve, b)
                    dve.wait_ge(r2_done, 1)
                    dve.tensor_tensor(r2[:, :], r2[:, :], core.rstd[:, :], ALU.mult).then_inc(rr_done, 1)
                    dve.wait_ge(rr_done, 1)
                    for b in range(B):
                        dve.tensor_scalar(xr[:, b, :], x[:, b, :], core.mv[:, b, 0:1], r2[:, b:b + 1],
                                          ALU.subtract, ALU.mult).then_inc(core.xn_done, 1)
                    dve.wait_ge(lnw_loaded, 16)
                    for b in range(B):
                        dve.wait_ge(xt_hi, b + 1)
                        for c in range(DC):
                            last = dve.scalar_tensor_tensor(
                                qin[1][:, c, b * P:(b + 1) * P], bank[b][:, c * P:(c + 1) * P], lnw[:, c:c + 1],
                                as_f32(qin[0][:, c, b * P:(b + 1) * P]), ALU.mult, ALU.subtract)
                        last.then_inc(core.xt_copied, 1)

                @block.tensor
                def _(pe):
                    pe.wait_ge(core.const_ready, 2)
                    for b in range(B):
                        pe.wait_ge(core.xn_done, b + 1)
                        for c in range(DC):
                            last = pe.transpose(bank[b][:, c * P:(c + 1) * P], xr[:, b, c * P:(c + 1) * P],
                                                core.ident[:, :])
                        last.then_inc(core.xt_full, 1)

                @block.scalar
                def _(act):
                    act.wait_ge(ctx_loaded, 16)
                    for c in range(DC):
                        act.activation(cin[0][:, c, :], ctx_raw[:, c, :], ACT.Copy).then_inc(ctx_hi, 1)
                    act.wait_ge(qk_loaded[0], 16)
                    act.activation(w_qk[0][0][:, :, :, :], raw_qk[0][:, :, :, :], ACT.Copy).then_inc(qk_hi[0], 1)
                    act.wait_ge(lnw_loaded, 16)
                    for b in range(B):
                        act.wait_ge(core.xt_full, b + 1)
                        for c in range(DC):
                            last = act.activation(qin[0][:, c, b * P:(b + 1) * P], bank[b][:, c * P:(c + 1) * P],
                                                  ACT.Copy, scale=lnw[:, c:c + 1])
                        last.then_inc(xt_hi, 1)
            core.norms += 1

        q, k = sb("q", [P, T]), sb("k", [P, T])
        v = sb("v", [P, B, 2 * P])
        probs = [sb("probs0", [P, B, P]), sb("probs1", [P, B, P])]
        probs_t = sb("probs_t", [P, B, P])
        heads = pair("heads", [P, 2, T])
        bias = sb("bias", [P, 2, P])
        comb = sb("comb", [P, B, P])
        mask_u8, neg = sb("mask_u8", [P, B, P], U8), sb("neg", [P, B, P])
        top, row_sum, inv_sum = sb("top", [P, B]), sb("row_sum", [P, B]), sb("inv_sum", [P, B])
        idle = sb("idle", [P, 1])
        work, top8 = sb("work", [P, TPT, P]), sb("top8", [P, TPT, 8])

        mask_loaded, neg_ready = sem("mask_loaded"), sem("neg_ready")
        bias_loaded = [sem("bias_loaded0"), sem("bias_loaded1")]
        comb_ready = sem("comb_ready")
        h_added = sem("h_added")
        o_loaded, o_hi, o_ready = sem("o_loaded"), sem("o_hi"), sem("o_ready")
        ring_full, ring_drained = sem("ring_full"), sem("ring_drained")
        scores_full, scores_read, top_raw, top_ready = (sem("scores_full"), sem("scores_read"), sem("top_raw"),
                                                        sem("top_ready"))
        exp_done, sum_ok, inv_done, probs_ready = sem("exp_done"), sem("sum_ok"), sem("inv_done"), sem("probs_ready")
        t_full, t_act, t_dve = sem("t_full"), sem("t_act"), sem("t_dve")
        h_full, h_hi, h_drained = sem("h_full"), sem("h_hi"), sem("h_drained")
        work_loaded, rank_step, ranked = sem("work_loaded"), sem("rank_step"), sem("ranked")

        N = L0_PAIRS
        PER = 20
        OFFSET = {"q1": 0, "k1": 2, "v": 4, "out": 8, "q0": 16, "k0": 18}

        def ring_at(i, what):
            first = isinstance(i, int) and i == 0 and what in ("q1", "k1", "v")
            return 4 + PER * i - 8 + OFFSET[what] + (8 if first else 0)

        OUT_LAST = ring_at(N - 1, "q0")

        def turns(body, eng):
            body(0, True, False)
            with eng.Fori(1, N - 1) as i:
                body(i, False, False)
            body(N - 1, False, True)

        with nc.Block() as block:

            @block.sync
            def _(sp):
                def load_qk(i, j):
                    wait(sp, qk_ready[j], i)
                    sp.dma_start(raw_qk[j][:, :, :, :], dram["L0_qk"][i, j, :, :, :, :]).then_inc(qk_loaded[j], 16)

                def load_bias(i, j):
                    wait(sp, comb_ready, 2 * i + j - 1)
                    sp.dma_start(bias[:, j, :], dram["L0_xattn_position_bias"][2 * i + j, :, :]
                                 ).then_inc(bias_loaded[j], 16)

                def load_v(i):
                    wait(sp, v_ready, i)
                    sp.dma_start(raw_v[:, :, :], dram["L0_v"][i, :, :, :]).then_inc(v_loaded, 16)

                sp.dma_start(mask_u8[:, :, :], dram["mask_b_q"]).then_inc(mask_loaded, 16)
                load_bias(0, 0)

                def turn(i, first, last):
                    wait(sp, ranked, i)
                    sp.dma_start(work[:, :, :], dram["ctx_rank"][i, :, :, :]).then_inc(work_loaded, 16)
                    load_bias(i, 1)
                    if not last:
                        load_qk(i + 1, 0)
                        load_bias(i + 1, 0)
                    wait(sp, o_ready, i)
                    sp.dma_start(raw_o[:, :, :], dram["L0_o"][i, :, :, :]).then_inc(o_loaded, 16)
                    if not last:
                        load_qk(i + 1, 1)
                        load_v(i + 1)

                turns(turn, sp)

            @block.gpsimd
            def _(pool):
                flat = lambda t: t[:, :, :].rearrange("p a b -> p (a b)")
                flat4 = lambda t: t[:, :, :, :].rearrange("p a b c -> p (a b c)")

                def split_low(i, raw, w, hi, ready):
                    f = flat4 if len(raw.shape) == 4 else flat
                    pool.wait_ge(hi, i + 1)
                    pool.tensor_tensor(f(w[1]), f(raw), as_f32(f(w[0])), ALU.subtract).then_inc(ready, 1)

                def combine(i, j):
                    pool.wait_ge(bias_loaded[j], 16 * (i + 1))
                    wait(pool, scores_read, 2 * (2 * i + j))
                    pool.tensor_tensor(comb[:, :, :], neg[:, :, :], bias[:, j:j + 1, :].to_broadcast([P, B, P]),
                                       ALU.add).then_inc(comb_ready, 1)

                split_low(0, raw_qk[1], w_qk[1], qk_hi[1], qk_ready[1])
                pool.wait_ge(mask_loaded, 16)
                pool.tensor_copy(comb[:, :, :], mask_u8[:, :, :]).then_inc(neg_ready, 1)
                pool.wait_ge(neg_ready, 1)
                pool.tensor_scalar(neg[:, :, :], comb[:, :, :], 1.0, -MASKED, ALU.subtract, ALU.mult
                                   ).then_inc(neg_ready, 1)
                pool.wait_ge(neg_ready, 2)
                combine(0, 0)
                split_low(0, raw_v, w_v, v_hi, v_ready)
                for b in range(B):
                    pool.wait_ge(h_done, b + 1)
                    pool.tensor_tensor(x[:, b, :], x[:, b, :], h[:, b, :], ALU.add).then_inc(h_added, 1)

                def turn(i, first, last):
                    combine(i, 1)
                    if not last:
                        split_low(i + 1, raw_qk[0], w_qk[0], qk_hi[0], qk_ready[0])
                        combine(i + 1, 0)
                        split_low(i + 1, raw_qk[1], w_qk[1], qk_hi[1], qk_ready[1])
                        split_low(i + 1, raw_v, w_v, v_hi, v_ready)
                    split_low(i, raw_o, w_o, o_hi, o_ready)

                turns(turn, pool)

            @block.tensor
            def _(pe):
                def project(n, at, bk, w, n_w, src):
                    wait(pe, ring_drained, at + n - 3)
                    part = slice(n * HALF, (n + 1) * HALF)
                    for c in range(DC):
                        mm = product(pe, bank[bk + n][:, :], [w[s][:, n_w, c, :] for s in range(2)],
                                     [src[s][:, c, part] for s in range(2)], c == 0, c == DC - 1)
                    mm.then_inc(ring_full, 1)

                def project_v(i):
                    pe.wait_ge(v_ready, i + 1)
                    for m in range(4):
                        wait(pe, ring_drained, ring_at(i, "v") + m - 3)
                        for b in (2 * m, 2 * m + 1):
                            for c in range(DC):
                                mm = product(pe, bank[m][:, (b % 2) * 2 * P:(b % 2 + 1) * 2 * P],
                                             [cin[s][:, c, b * P:(b + 1) * P] for s in range(2)],
                                             [w_v[s][:, c, :] for s in range(2)], c == 0, c == DC - 1)
                        mm.then_inc(ring_full, 1)

                def scores(h, needed):
                    pe.wait_ge(ring_drained, needed)
                    wait(pe, scores_read, 2 * h)
                    for half in range(2):
                        for y in range(BH):
                            t = slice((half * BH + y) * P, (half * BH + y + 1) * P)
                            mm = product(pe, bank[4 + half][:, y * P:(y + 1) * P], [q[:, t]], [k[:, t]], True, True)
                        mm.then_inc(scores_full, 1)

                def transpose_probs(h, j):
                    pe.wait_ge(probs_ready, h + 1)
                    wait(pe, h_drained, 2 * h)
                    for half in range(2):
                        for y in range(BH):
                            mm = pe.transpose(bank[6 + half][:, y * P:(y + 1) * P], probs[j][:, half * BH + y, :],
                                              core.ident[:, :])
                        mm.then_inc(t_full, 1)

                def weigh_values(h, j):
                    for half in range(2):
                        pe.wait_ge((t_act, t_dve)[half], h + 1)
                        for y in range(BH):
                            b = half * BH + y
                            mm = product(pe, bank[6 + half][:, y * P:(y + 1) * P], [v[:, b, j * P:(j + 1) * P]],
                                         [probs_t[:, b, :]], True, True)
                        mm.then_inc(h_full, 1)

                def project_out(i, at):
                    pe.wait_ge(o_ready, i + 1)
                    pe.wait_ge(h_drained, 4 * i + 4)
                    for b in range(B):
                        wait(pe, ring_drained, at + b - 3)
                        for j in range(2):
                            mm = product(pe, bank[b % 4][:, :], [heads[s][:, j, b * P:(b + 1) * P] for s in range(2)],
                                         [w_o[s][:, j, :] for s in range(2)], j == 0, j == 1)
                        mm.then_inc(ring_full, 1)

                def step(h, j, needed, at, project_next, weigh_last):
                    scores(h, needed)
                    if weigh_last:
                        transpose_probs(h - 1, 1 - j)
                    if project_next:
                        project(0, at, 0, w_qk[1 - j], 0, qin)
                    if weigh_last:
                        weigh_values(h - 1, 1 - j)
                    if project_next:
                        project(1, at, 0, w_qk[1 - j], 0, qin)
                        for n in range(2):
                            project(n, at + 2, 2, w_qk[1 - j], 1, cin)

                pe.wait_ge(qk_ready[0], 1)
                for n in range(2):
                    project(n, 0, 0, w_qk[0], 0, qin)
                for n in range(2):
                    project(n, 2, 2, w_qk[0], 1, cin)

                def turn(i, first, last):
                    pe.wait_ge(qk_ready[1], i + 1)
                    step(2 * i, 0, 4 if first else ring_at(i, "q1"), ring_at(i, "q1"), True, not first)
                    project_v(i)
                    if not first:
                        project_out(i - 1, ring_at(i, "out"))
                    if not last:
                        pe.wait_ge(qk_ready[0], i + 2)
                    step(2 * i + 1, 1, ring_at(i, "v") + 4, ring_at(i, "q0"), not last,
                         True)

                turns(turn, pe)
                transpose_probs(2 * N - 1, 1)
                weigh_values(2 * N - 1, 1)
                project_out(N - 1, OUT_LAST)

            @block.scalar
            def _(act):
                def exps(h, j):
                    act.wait_ge(top_ready, h + 1)
                    wait(act, inv_done, h)
                    for b in range(B):
                        act.activation(probs[j][:, b, :], probs[j][:, b, :], ACT.Exp, bias=top[:, b:b + 1],
                                       accum_out=row_sum[:, b:b + 1]).then_inc(exp_done, 1)

                def split_high(i, raw, w, loaded, hi, free):
                    act.wait_ge(loaded, 16 * (i + 1))
                    wait(act, ring_full, free)
                    sl = tuple(slice(None) for _ in raw.shape)
                    act.activation(w[0][sl], raw[sl], ACT.Copy).then_inc(hi, 1)

                def copy_probs(h):
                    act.wait_ge(t_full, 2 * h + 1)
                    act.activation(probs_t[:, 0:BH, :], bank[6][:, :].rearrange("p (b n) -> p b n", b=BH), ACT.Copy
                                   ).then_inc(t_act, 1)

                def heads_high(h, j):
                    for half in range(2):
                        act.wait_ge(h_full, 2 * h + half + 1)
                        act.activation(heads[0][:, j, half * HALF:(half + 1) * HALF], bank[6 + half][:, :], ACT.Copy
                                       ).then_inc(h_hi, 1)

                split_high(0, raw_qk[1], w_qk[1], qk_loaded[1], qk_hi[1], 0)
                split_high(0, raw_v, w_v, v_loaded, v_hi, 0)

                def turn(i, first, last):
                    if not first:
                        copy_probs(2 * i - 1)
                    exps(2 * i, 0)
                    if not first:
                        heads_high(2 * i - 1, 1)
                    if not last:
                        split_high(i + 1, raw_qk[0], w_qk[0], qk_loaded[0], qk_hi[0], 4 if first else ring_at(i, "q1"))
                        split_high(i + 1, raw_qk[1], w_qk[1], qk_loaded[1], qk_hi[1], ring_at(i, "k1") + 2)
                        split_high(i + 1, raw_v, w_v, v_loaded, v_hi, ring_at(i, "v") + 4)
                    split_high(i, raw_o, w_o, o_loaded, o_hi, 0 if first else ring_at(i, "out") + 8)
                    copy_probs(2 * i)
                    exps(2 * i + 1, 1)
                    heads_high(2 * i, 0)

                turns(turn, act)
                copy_probs(2 * N - 1)
                heads_high(2 * N - 1, 1)

            @block.vector
            def _(dve):
                def add_bias(h, j):
                    dve.wait_ge(comb_ready, h + 1)
                    wait(dve, t_full, 2 * (h - 1))
                    for half in range(2):
                        part = slice(half * BH, (half + 1) * BH)
                        dve.wait_ge(scores_full, 2 * h + half + 1)
                        dve.tensor_tensor(probs[j][:, part, :], bank[4 + half][:, :].rearrange("p (b n) -> p b n", b=BH),
                                          comb[:, part, :], ALU.add).then_inc(scores_read, 1)
                    dve.wait_ge(scores_read, 2 * h + 2)
                    wait(dve, exp_done, B * h)
                    dve.tensor_reduce(top[:, :], probs[j][:, :, :], AX.X, ALU.max).then_inc(top_raw, 1)
                    dve.wait_ge(top_raw, h + 1)
                    dve.tensor_scalar(top[:, :], top[:, :], FLOOR, -1.0, ALU.max, ALU.mult).then_inc(top_ready, 1)

                def normalise(h, j):
                    dve.wait_ge(exp_done, B * (h + 1))
                    dve.tensor_scalar_max(inv_sum[:, :], row_sum[:, :], 1e-30).then_inc(sum_ok, 1)
                    dve.wait_ge(sum_ok, h + 1)
                    dve.reciprocal(inv_sum[:, :], inv_sum[:, :]).then_inc(inv_done, 1)
                    dve.wait_ge(inv_done, h + 1)
                    dve.tensor_tensor(probs[j][:, :, :], probs[j][:, :, :],
                                      inv_sum[:, :].rearrange("p (b o) -> p b o", o=1).to_broadcast([P, B, P]),
                                      ALU.mult).then_inc(probs_ready, 1)

                def drain(at, dst, bk):
                    dve.wait_ge(ring_full, at + 1)
                    dve.tensor_copy(dst, bank[bk][:, :].rearrange("p (b n) -> p b n", b=dst.shape[1])
                                    if len(dst.shape) == 3 else bank[bk][:, :]).then_inc(ring_drained, 1)

                def drain_half(n, at, dst, bk):
                    drain(at + n, dst[:, n * HALF:(n + 1) * HALF], bk + n)

                def copy_probs(h):
                    dve.wait_ge(t_full, 2 * h + 2)
                    dve.tensor_copy(probs_t[:, BH:B, :], bank[7][:, :].rearrange("p (b n) -> p b n", b=BH)
                                    ).then_inc(t_dve, 1)

                def heads_low(h, j):
                    for half in range(2):
                        part = slice(half * HALF, (half + 1) * HALF)
                        dve.wait_ge(h_hi, 2 * h + half + 1)
                        dve.tensor_tensor(heads[1][:, j, part], bank[6 + half][:, :], as_f32(heads[0][:, j, part]),
                                          ALU.subtract).then_inc(h_drained, 1)

                def add_out(at, final=False):
                    for b in range(B):
                        dve.wait_ge(ring_full, at + b + 1)
                        dve.tensor_tensor(x[:, b, :], x[:, b, :], bank[b % 4][:, :], ALU.add).then_inc(ring_drained, 1)
                        if final:
                            dve.wait_ge(ring_drained, at + b + 1)
                            core.statistics(dve, b)

                def steps_before(i, r):
                    return (ROUNDS + 1) * 2 * TPT * i + 2 * TPT * r + (TPT + 1) * i

                def rank_start(i):
                    dve.wait_ge(work_loaded, 16 * (i + 1))
                    dve.tensor_scalar(work[:, :, :], work[:, :, :], -1.0, None, ALU.mult).then_inc(rank_step, 1)

                def rank_settle(steps):
                    dve.wait_ge(rank_step, steps)
                    dve.memset(idle[:, :], 0.0)

                def rank_round(i, r):
                    at = steps_before(i, r) + 1
                    rank_settle(at)
                    for n in range(TPT):
                        dve.max(top8[:, n, :], work[:, n, :]).then_inc(rank_step, 1)
                    rank_settle(at + TPT)
                    if r == ROUNDS:
                        for n in range(TPT):
                            dve.memset(top8[:, n, REST:8], TAKEN).then_inc(rank_step, 1)
                        at += TPT
                        rank_settle(at + TPT)
                    for n in range(TPT):
                        dve.match_replace(work[:, n, :], top8[:, n, :], work[:, n, :], TAKEN).then_inc(rank_step, 1)

                def rank_end(i):
                    dve.wait_ge(rank_step, steps_before(i + 1, 0))
                    dve.tensor_scalar(core.crucial[:, bass.ds(TPT * i, TPT), :], work[:, :, ::-1], TAKEN, None,
                                      ALU.not_equal).then_inc(ranked, 1)

                def step(h, j, at, drain_next, weigh_last, i, r):
                    add_bias(h, j)
                    if weigh_last:
                        copy_probs(h - 1)
                    if drain_next:
                        drain_half(0, at, q, 0)
                    if weigh_last:
                        heads_low(h - 1, 1 - j)
                    if drain_next:
                        drain_half(1, at, q, 0)
                    if r == 0:
                        rank_start(i)
                    rank_round(i, r)
                    normalise(h, j)
                    if drain_next:
                        drain_half(0, at + 2, k, 2)
                        drain_half(1, at + 2, k, 2)
                    rank_round(i, r + 1)

                for n in range(2):
                    drain_half(n, 0, q, 0)
                for n in range(2):
                    drain_half(n, 2, k, 2)
                for b in range(FIRST_H, B):
                    hidden(dve, b)

                def turn(i, first, last):
                    step(2 * i, 0, ring_at(i, "q1"), True, not first, i, 0)
                    for m in range(4):
                        drain(ring_at(i, "v") + m, v[:, 2 * m:2 * m + 2, :], m)
                        if m % 2:
                            rank_round(i, 2 + m // 2)
                    if not first:
                        dve.wait_ge(h_added, B)
                        add_out(ring_at(i, "out"))
                    step(2 * i + 1, 1, ring_at(i, "q0"), not last, True, i, 4)
                    rank_round(i, 6)
                    rank_end(i)

                turns(turn, dve)
                copy_probs(2 * N - 1)
                heads_low(2 * N - 1, 1)
                add_out(OUT_LAST, True)


def l0_ffn(core, dram):
    nc, x, bank = core.nc, core.x, core.bank
    E, R, EC = 8, 64, 4
    with ExitStack() as ctx:
        sb = lambda name, shape, dt=F32: core.sb(ctx, "l0f_" + name, shape, dt)
        sem = lambda name: core.sem("l0f_" + name)
        pair = lambda name, shape: core.pair(ctx, "l0f_" + name, shape)
        xn, xt = sb("xn", [P, B, D]), pair("xt", [P, DC, T])
        w_q, keys = pair("w_q", [P, DC, P]), sb("keys", [P, E])
        w_down, w_org, w_up = pair("w_down", [P, DC, E * R]), pair("w_org", [P, DC, D]), pair("w_up", [P, EC, D])
        RAWS = 3
        raw = [sb(f"raw{n}", [P, 2, D]) for n in range(RAWS)]
        h = pair("h", [P, EC, T])
        query, query_parts = sb("query", [P, B]), sb("query_parts", [P, B])
        top, total, inv = sb("top", [B, 1]), sb("total", [B, 1]), sb("inv", [B, 1])
        exps = sb("exps", [B, E])
        coef = xn[0:B, 0, :].rearrange("b (e r) -> b e r", e=E)
        coef_t = sb("coef_t", [P, EC, B])
        keys_loaded, w_hi = sem("keys_loaded"), sem("w_hi")
        by_pool, by_dve = sem("by_pool"), sem("by_dve")
        raw_loaded = [sem(f"raw_loaded{n}") for n in range(RAWS)]
        pieces = [("L0f_wq", w_q, 0, DC, P)]
        for name, w in (("L0f_down", w_down), ("L0f_org", w_org), ("L0f_up", w_up)):
            pieces += [(name, w, 0, 2, D), (name, w, 2, 2, D)]
        pieces.append(("L1x_wkv", core.l1_wkv, 0, DC, 2 * P))
        raw_view = lambda n: (raw[n % RAWS][:, :, :].rearrange("p a b -> p (a b)")[:, 0:pieces[n][3] * pieces[n][4]]
                              .rearrange("p (c d) -> p c d", c=pieces[n][3]))
        target = lambda n, s: pieces[n][1][s][:, pieces[n][2]:pieces[n][2] + pieces[n][3], :]

        def load(sp, n):
            name, w, first, chunks, width = pieces[n]
            sp.dma_start(raw_view(n), dram[name][:, first:first + chunks, :]).then_inc(raw_loaded[n % RAWS], 16)

        def high(act, n):
            act.wait_ge(raw_loaded[n % RAWS], 16 * (n // RAWS + 1))
            act.activation(target(n, 0), raw_view(n), ACT.Copy).then_inc(w_hi, 1)

        def low(eng, n, done):
            eng.wait_ge(w_hi, n + 1)
            eng.tensor_tensor(target(n, 1), raw_view(n), as_f32(target(n, 0)), ALU.subtract).then_inc(done, 1)

        def loads(sp):
            for n in range(RAWS):
                load(sp, n)
            sp.dma_start(keys[:, :], dram["L0f_keys"]).then_inc(keys_loaded, 16)

        def first_low(pool):
            low(pool, 0, by_pool)
            low(pool, 1, by_pool)

        def next_high(act):
            high(act, 1)
            high(act, 2)

        norm_stage(core, xn, xt, loads, lambda act: high(act, 0), first_low, next_high, lambda dve: low(dve, 2, by_dve))

        query_full, parts_done, query_done = sem("query_full"), sem("parts_done"), sem("query_done")
        scores_full, top_done, exp_done, inv_done = sem("scores_full"), sem("top_done"), sem("exp_done"), sem("inv_done")
        raw_done, h_hi = sem("raw_done"), sem("h_hi")
        coef_done, coef_full, coef_t_done = sem("coef_done"), sem("coef_full"), sem("coef_t_done")
        ring_full, ring_drained = sem("ring_full"), sem("ring_drained")
        scale = 1.0 / float(np.sqrt(P))
        with nc.Block() as block:

            @block.sync
            def _(sp):
                sp.wait_ge(by_pool, 1)
                load(sp, 3)
                sp.wait_ge(by_pool, 2)
                load(sp, 4)
                sp.wait_ge(by_dve, 1)
                load(sp, 5)
                sp.wait_ge(by_pool, 3)
                load(sp, 6)
                sp.wait_ge(by_pool, 4)
                load(sp, 7)

            @block.tensor
            def _(pe):
                def low_rank(n):
                    j, half = n // 2, n % 2
                    wait(pe, ring_drained, n - 3)
                    for c in range(DC):
                        mm = product(pe, bank[4 + n % 4][:, :], [w_down[s][:, c, j * P:(j + 1) * P] for s in range(2)],
                                     [xt[s][:, c, half * HALF:(half + 1) * HALF] for s in range(2)], c == 0, c == DC - 1)
                    mm.then_inc(ring_full, 1)

                pe.wait_ge(by_pool, 1)
                for half in range(2):
                    for c in range(DC):
                        mm = product(pe, bank[half][:, :], [w_q[s][:, c, :] for s in range(2)],
                                     [xt[s][:, c, half * HALF:(half + 1) * HALF] for s in range(2)], c == 0, c == DC - 1)
                    mm.then_inc(query_full, 1)
                pe.wait_ge(by_pool, 2)
                pe.wait_ge(by_dve, 1)
                low_rank(0)
                pe.wait_ge(keys_loaded, 16)
                pe.wait_ge(query_done, 1)
                product(pe, bank[3][0:B, 0:E], [query[:, :]], [keys[:, :]], True, True).then_inc(scores_full, 1)
                low_rank(1)
                pe.wait_ge(coef_done, 1)
                for j in range(EC):
                    mm = product(pe, bank[2][:, j * B:(j + 1) * B],
                                 [coef[:, 2 * j:2 * j + 2, :].rearrange("b e r -> b (e r)")],
                                 [core.ident[0:B, 0:B]], True, True)
                mm.then_inc(coef_full, 1)
                for n in range(2, 8):
                    low_rank(n)
                pe.wait_ge(by_pool, 6)
                for b in range(B):
                    part = slice(b * P, (b + 1) * P)
                    wait(pe, ring_drained, 8 + b - 3)
                    for c in range(DC):
                        product(pe, bank[4 + b % 4][:, :], [xt[s][:, c, part] for s in range(2)],
                                [w_org[s][:, c, :] for s in range(2)], c == 0, False)
                    if b == 0:
                        pe.wait_ge(ring_drained, 8)
                    for j in range(EC):
                        mm = product(pe, bank[4 + b % 4][:, :], [h[s][:, j, part] for s in range(2)],
                                     [w_up[s][:, j, :] for s in range(2)], False, j == EC - 1)
                    mm.then_inc(ring_full, 1)

            @block.gpsimd
            def _(pool):
                for n in range(3, 7):
                    low(pool, n, by_pool)
                low(pool, 7, core.l1_kv_split)

            @block.scalar
            def _(act):
                for n in range(3, 5):
                    high(act, n)
                act.wait_ge(parts_done, 2)
                act.activation(query[:, :], query_parts[:, :], ACT.Copy, scale=1.0 / P).then_inc(query_done, 1)
                act.wait_ge(top_done, 1)
                act.activation(exps[:, :], bank[3][0:B, 0:E], ACT.Exp, bias=top[:, :], scale=scale,
                               accum_out=total[:, :]).then_inc(exp_done, 1)
                for n in range(5, 8):
                    high(act, n)

            @block.vector
            def _(dve):
                for half in range(2):
                    dve.wait_ge(query_full, half + 1)
                    dve.tensor_reduce(query_parts[:, half * BH:(half + 1) * BH],
                                      bank[half][:, :].rearrange("p (b t) -> p b t", b=BH), AX.X, ALU.add
                                      ).then_inc(parts_done, 1)
                dve.wait_ge(scores_full, 1)
                dve.tensor_reduce(top[:, :], bank[3][0:B, 0:E], AX.X, ALU.max).then_inc(raw_done, 1)
                dve.wait_ge(raw_done, 1)
                dve.tensor_scalar(top[:, :], top[:, :], -scale, None, ALU.mult).then_inc(top_done, 1)
                dve.wait_ge(exp_done, 1)
                dve.reciprocal(inv[:, :], total[:, :]).then_inc(inv_done, 1)
                dve.wait_ge(inv_done, 1)
                dve.tensor_scalar(coef, exps[:, :].rearrange("b (e o) -> b e o", o=1).to_broadcast([B, E, R]),
                                  inv[:, 0:1], None, ALU.mult).then_inc(coef_done, 1)
                dve.wait_ge(coef_full, 1)
                dve.tensor_copy(coef_t[:, :, :], bank[2][:, 0:EC * B].rearrange("p (j b) -> p j b", j=EC)
                                ).then_inc(coef_t_done, 1)
                dve.wait_ge(coef_t_done, 1)
                for n in range(8):
                    j, half = n // 2, n % 2
                    dve.wait_ge(ring_full, n + 1)
                    dve.tensor_tensor(h[0][:, j, half * HALF:(half + 1) * HALF].rearrange("p (b t) -> p b t", b=BH),
                                      bank[4 + n % 4][:, :].rearrange("p (b t) -> p b t", b=BH),
                                      coef_t[:, j, half * BH:(half + 1) * BH].rearrange("p (b o) -> p b o", o=1)
                                      .to_broadcast([P, BH, P]), ALU.mult).then_inc(h_hi, 1)
                    dve.wait_ge(h_hi, n + 1)
                    for y in range(BH):
                        b = half * BH + y
                        last = dve.scalar_tensor_tensor(
                            h[1][:, j, b * P:(b + 1) * P], bank[4 + n % 4][:, y * P:(y + 1) * P], coef_t[:, j, b:b + 1],
                            as_f32(h[0][:, j, b * P:(b + 1) * P]), ALU.mult, ALU.subtract)
                    last.then_inc(ring_drained, 1)
                for b in range(B):
                    dve.wait_ge(ring_full, 8 + b + 1)
                    dve.tensor_tensor(x[:, b, :], x[:, b, :], bank[4 + b % 4][:, :], ALU.add).then_inc(ring_drained, 1)
                    dve.wait_ge(ring_drained, 8 + b + 1)
                    core.statistics(dve, b)


L1_GROUPS, L1_QUERIES, L1_DIM = 8, 4, 16


def l1_attention(core, dram):
    nc, x, bank = core.nc, core.x, core.bank
    KV, G, HD = L1_GROUPS, L1_QUERIES, L1_DIM
    SCALE = 1.0 / float(np.sqrt(HD))
    w_kv = core.l1_wkv
    n_norm = core.norms
    core.norms += 1
    with ExitStack() as ctx:
        sb = lambda name, shape, dt=F32: core.sb(ctx, "l1x_" + name, shape, dt)
        pair = lambda name, shape: core.pair(ctx, "l1x_" + name, shape)
        sem = lambda name: core.sem("l1x_" + name)
        xn, xt = sb("xn", [P, B, D]), pair("xt", [P, DC, T])
        w_q, w_o = pair("w_q", [P, DC, D]), pair("w_o", [P, G, D])
        raw = sb("raw", [P, DC, D])
        raw_loaded, w_hi, w_ready = sem("raw_loaded"), sem("w_hi"), sem("w_ready")
        q = core.cin
        kt = pair("kt", [P, T])
        v = sb("v", [P, B, KV, HD + 1])
        same = sb("same", [P, KV])
        kd = [pair(f"kd{j}", [P, KV, P]) for j in range(2)]
        qb = [pair(f"qb{j}", [P, G, P]) for j in range(2)]
        top = [sb(f"top{n}", [P, KV]) for n in range(2)]
        probs = [sb(f"probs{n}", [P, KV, P]) for n in range(2)]
        probs_t = [sb(f"probs_t{n}", [P, KV, P]) for n in range(2)]
        inv = sb("inv", [P, KV])
        a, at = sb("a", [P, G, KV, HD]), pair("at", [P, G, P])
        made, same_ready, ones_ready = sem("made"), sem("same_ready"), sem("ones_ready")
        kt_full, kt_hi, kt_done, v_full, v_done = (sem("kt_full"), sem("kt_hi"), sem("kt_done"), sem("v_full"),
                                                   sem("v_done"))
        xt_hi, q_full, q_hi, q_done = sem("xt_hi"), sem("q_full"), sem("q_hi"), sem("q_done")
        batch_ready = sem("batch_ready")
        s_full, top_done, shifted, exp_done = sem("s_full"), sem("top_done"), sem("shifted"), sem("exp_done")
        t_full, t_done, a_full, inv_done, a_done = (sem("t_full"), sem("t_done"), sem("a_full"), sem("inv_done"),
                                                    sem("a_done"))
        at_full, at_hi, at_done, o_full, o_done = (sem("at_full"), sem("at_hi"), sem("at_done"), sem("o_full"),
                                                   sem("o_done"))
        xt_bank = lambda b: (b + BH) % B
        q_bank = lambda half, g: bank[xt_bank(half * BH + g)]
        half_of = lambda half: slice(half * HALF, (half + 1) * HALF)

        def turns(body, eng):
            body(0, True)
            with eng.Fori(1, B // 2) as t:
                body(t, False)

        with nc.Block() as block:

            @block.sync
            def _(sp):
                sp.dma_start(raw[:, :, :], dram["L1x_wq"]).then_inc(raw_loaded, 16)
                sp.wait_ge(w_ready, 1)
                sp.wait_ge(raw_loaded, 16)
                sp.dma_start(raw[:, :, :], dram["L1x_wo"]).then_inc(raw_loaded, 16)

            @block.gpsimd
            def _(pool):
                pool.memset(v[:, :, :, :], 1.0).then_inc(ones_ready, 1)
                pool.memset(same[:, :], 1.0).then_inc(made, 1)
                pool.wait_ge(made, 1)
                pool.affine_select(out=same[:, :], in_=same[:, :], compare_op=ALU.is_ge, fill=0.0, base=0,
                                   pattern=[[-HD, KV]], channel_multiplier=1).then_inc(made, 1)
                pool.wait_ge(made, 2)
                pool.affine_select(out=same[:, :], in_=same[:, :], compare_op=ALU.is_ge, fill=0.0, base=HD - 1,
                                   pattern=[[HD, KV]], channel_multiplier=-1).then_inc(same_ready, 1)
                pool.wait_ge(core.var_done, n_norm + 1)
                pool.tensor_tensor(core.rstd[:, :], core.var_eps[:, :], core.neg_half[:, :], ALU.pow
                                   ).then_inc(core.rstd_done, 1)
                for n, w in enumerate((w_q, w_o)):
                    pool.wait_ge(w_hi, n + 1)
                    pool.tensor_tensor(w[1][:, :, :], raw[:, :, :], as_f32(w[0][:, :, :]), ALU.subtract
                                       ).then_inc(w_ready, 1)
                pool.wait_ge(same_ready, 1)
                pool.wait_ge(kt_done, 2)

                def prepare(b, j):
                    wait(pool, s_full, G * (b - 1))
                    tokens = bass.ds(b * P, P)
                    for s in range(2):
                        pool.tensor_tensor(kd[j][s][:, :, :],
                                           as_f32(kt[s][:, tokens]).rearrange("p (o k) -> p o k", o=1)
                                           .to_broadcast([P, KV, P]),
                                           same[:, :].rearrange("p (n o) -> p n o", o=1).to_broadcast([P, KV, P]),
                                           ALU.mult)
                    if isinstance(b, int):
                        pool.wait_ge(q_done, G if b == 0 else 2 * G)
                    for s in range(2):
                        last = pool.tensor_copy(qb[j][s][:, :, :], as_f32(q[s][:, :, tokens]))
                    last.then_inc(batch_ready, 1)

                def turn(t, first):
                    prepare(2 * t, 0)
                    prepare(2 * t + 1, 1)

                turns(turn, pool)

            @block.tensor
            def _(pe):
                pe.wait_ge(core.l1_kv_split, 1)
                for half in range(2):
                    for c in range(DC):
                        mm = product(pe, bank[half][:, :], [w_kv[s][:, c, 0:P] for s in range(2)],
                                     [core.cin[s][:, c, half_of(half)] for s in range(2)], c == 0, c == DC - 1)
                    mm.then_inc(kt_full, 1)
                for half in range(2):
                    for y in range(BH):
                        b = half * BH + y
                        for c in range(DC):
                            mm = product(pe, bank[2 + half][:, y * P:(y + 1) * P],
                                         [core.cin[s][:, c, b * P:(b + 1) * P] for s in range(2)],
                                         [w_kv[s][:, c, P:2 * P] for s in range(2)], c == 0, c == DC - 1)
                    mm.then_inc(v_full, 1)
                for b in range(B):
                    pe.wait_ge(core.xn_done, B * n_norm + b + 1)
                    if b == BH:
                        pe.wait_ge(kt_done, 2)
                    if b == BH + 2:
                        pe.wait_ge(v_done, 2)
                    for c in range(DC):
                        mm = pe.transpose(bank[xt_bank(b)][:, c * P:(c + 1) * P], xn[:, b, c * P:(c + 1) * P],
                                          core.ident[:, :])
                    mm.then_inc(core.xt_full, 1)
                pe.wait_ge(w_ready, 1)
                for half in range(2):
                    pe.wait_ge(core.xt_copied, B * n_norm + (half + 1) * BH)
                    for g in range(G):
                        for c in range(DC):
                            mm = product(pe, q_bank(half, g)[:, :], [w_q[s][:, c, g * P:(g + 1) * P] for s in range(2)],
                                         [xt[s][:, c, half_of(half)] for s in range(2)], c == 0, c == DC - 1)
                        mm.then_inc(q_full, 1)

                def scores(b, j, g):
                    wait(pe, shifted, G * b + g - 1)
                    if g == 0:
                        pe.wait_ge(batch_ready, b + 1)
                    for n in range(2):
                        mm = product(pe, bank[2 * (g % 2) + n][:, :], [qb[j][s][:, g, :] for s in range(2)],
                                     [kd[j][s][:, n * BH:(n + 1) * BH, :].rearrange("p n k -> p (n k)") for s in range(2)],
                                     True, True)
                    mm.then_inc(s_full, 1)

                def transpose_probs(b, g):
                    pe.wait_ge(exp_done, G * b + g + 1)
                    wait(pe, t_done, 2 * (G * b + g))
                    for m in range(KV):
                        mm = pe.transpose(bank[4 + m // BH][:, (m % BH) * P:(m % BH + 1) * P], probs[g % 2][:, m, :],
                                          core.ident[:, :])
                        if m % BH == BH - 1:
                            mm.then_inc(t_full, 1)

                def weigh_values(b, g):
                    wait(pe, a_done, G * b + g)
                    for m in range(KV):
                        if m % BH == 0:
                            pe.wait_ge(t_done, 2 * (G * b + g) + m // BH + 1)
                        mm = product(pe, bank[6][:, m * (HD + 1):(m + 1) * (HD + 1)], [probs_t[g % 2][:, m, :]],
                                     [v[:, bass.ds(b, 1), m, :].rearrange("p o d -> p (o d)")], True, True)
                    mm.then_inc(a_full, 1)

                def transpose_result(b):
                    pe.wait_ge(a_done, G * b + G)
                    wait(pe, o_done, b)
                    for g in range(G):
                        mm = pe.transpose(bank[7][:, g * P:(g + 1) * P], a[:, g, :, :].rearrange("p n d -> p (n d)"),
                                          core.ident[:, :])
                    mm.then_inc(at_full, 1)

                def project_out(b):
                    pe.wait_ge(at_done, b + 1)
                    for g in range(G):
                        mm = product(pe, bank[7][:, :], [at[s][:, g, :] for s in range(2)],
                                     [w_o[s][:, g, :] for s in range(2)], g == 0, g == G - 1)
                    mm.then_inc(o_full, 1)

                def batch(b, j, first):
                    scores(b, j, 0)
                    if not first:
                        weigh_values(b - 1, 2)
                        transpose_probs(b - 1, 3)
                    scores(b, j, 1)
                    if not first:
                        weigh_values(b - 1, 3)
                    transpose_probs(b, 0)
                    scores(b, j, 2)
                    if not first:
                        transpose_result(b - 1)
                    weigh_values(b, 0)
                    transpose_probs(b, 1)
                    scores(b, j, 3)
                    if not first:
                        project_out(b - 1)
                    weigh_values(b, 1)
                    transpose_probs(b, 2)

                def turn(t, first):
                    batch(2 * t, 0, first)
                    batch(2 * t + 1, 1, False)

                pe.wait_ge(q_done, 2 * G)
                pe.wait_ge(w_ready, 2)
                turns(turn, pe)
                weigh_values(B - 1, 2)
                transpose_probs(B - 1, 3)
                weigh_values(B - 1, 3)
                transpose_result(B - 1)
                project_out(B - 1)

            @block.scalar
            def _(act):
                act.wait_ge(raw_loaded, 16)
                act.activation(w_q[0][:, :, :], raw[:, :, :], ACT.Copy).then_inc(w_hi, 1)
                for half in range(2):
                    act.wait_ge(kt_full, half + 1)
                    act.activation(kt[0][:, half_of(half)], bank[half][:, :], ACT.Copy).then_inc(kt_hi, 1)
                for b in range(B):
                    act.wait_ge(core.xt_full, B * n_norm + b + 1)
                    act.activation(xt[0][:, :, b * P:(b + 1) * P],
                                   bank[xt_bank(b)][:, :].rearrange("p (c t) -> p c t", c=DC), ACT.Copy).then_inc(xt_hi, 1)
                act.wait_ge(raw_loaded, 32)
                act.activation(w_o[0][:, :, :], raw[:, :, :], ACT.Copy).then_inc(w_hi, 1)
                for half in range(2):
                    for g in range(G):
                        act.wait_ge(q_full, half * G + g + 1)
                        act.activation(q[0][:, g, half_of(half)], q_bank(half, g)[:, :], ACT.Copy).then_inc(q_hi, 1)

                def batch(b, first):
                    for g in range(G):
                        act.wait_ge(shifted, G * b + g + 1)
                        act.activation(probs[g % 2][:, :, :], probs[g % 2][:, :, :], ACT.Exp, scale=SCALE
                                       ).then_inc(exp_done, 1)
                        if g == 1 and not first:
                            result_high(b - 1)
                        for n in range(2):
                            act.wait_ge(t_full, 2 * (G * b + g) + n + 1)
                            act.activation(probs_t[g % 2][:, n * BH:(n + 1) * BH, :],
                                           bank[4 + n][:, :].rearrange("p (m k) -> p m k", m=BH), ACT.Copy
                                           ).then_inc(t_done, 1)

                def result_high(b):
                    act.wait_ge(at_full, b + 1)
                    act.activation(at[0][:, :, :], bank[7][:, :].rearrange("p (g t) -> p g t", g=G), ACT.Copy
                                   ).then_inc(at_hi, 1)

                def turn(t, first):
                    batch(2 * t, first)
                    batch(2 * t + 1, False)

                turns(turn, act)
                result_high(B - 1)

            @block.vector
            def _(dve):
                wide = lambda t: t[:, :].rearrange("p (n o) -> p n o", o=1)
                dve.wait_ge(core.stats_done, B * (n_norm + 1))
                for b in range(B):
                    dve.bn_aggr(core.mv[:, b, :], core.stats[:, b, :]).then_inc(core.mv_done, 1)
                dve.wait_ge(core.mv_done, B * (n_norm + 1))
                dve.tensor_scalar_add(core.var_eps[:, :], core.mv[:, :, 1], EPS).then_inc(core.var_done, 1)
                for half in range(2):
                    dve.wait_ge(kt_hi, half + 1)
                    dve.tensor_tensor(kt[1][:, half_of(half)], bank[half][:, :], as_f32(kt[0][:, half_of(half)]),
                                      ALU.subtract).then_inc(kt_done, 1)
                dve.wait_ge(core.rstd_done, n_norm + 1)
                for b in range(B):
                    dve.tensor_scalar(xn[:, b, :], core.x[:, b, :], core.mv[:, b, 0:1], core.rstd[:, b:b + 1],
                                      ALU.subtract, ALU.mult).then_inc(core.xn_done, 1)
                dve.wait_ge(ones_ready, 1)
                for half in range(2):
                    dve.wait_ge(v_full, half + 1)
                    dve.tensor_copy(v[:, half * BH:(half + 1) * BH, :, 0:HD],
                                    bank[2 + half][:, :].rearrange("p (b n d) -> p b n d", b=BH, n=KV)).then_inc(v_done, 1)
                for b in range(B):
                    dve.wait_ge(xt_hi, b + 1)
                    dve.tensor_tensor(xt[1][:, :, b * P:(b + 1) * P],
                                      bank[xt_bank(b)][:, :].rearrange("p (c t) -> p c t", c=DC),
                                      as_f32(xt[0][:, :, b * P:(b + 1) * P]), ALU.subtract).then_inc(core.xt_copied, 1)
                for half in range(2):
                    for g in range(G):
                        dve.wait_ge(q_hi, half * G + g + 1)
                        dve.tensor_tensor(q[1][:, g, half_of(half)], q_bank(half, g)[:, :],
                                          as_f32(q[0][:, g, half_of(half)]), ALU.subtract).then_inc(q_done, 1)

                def shift(b, g):
                    s = bank[2 * (g % 2):2 * (g % 2) + 2]
                    dve.wait_ge(s_full, G * b + g + 1)
                    wait(dve, shifted, G * b + g - 1)
                    for n in range(2):
                        dve.tensor_reduce(top[g % 2][:, n * BH:(n + 1) * BH], s[n][:, :].rearrange("p (m k) -> p m k", m=BH),
                                          AX.X, ALU.max).then_inc(top_done, 1)
                    wait(dve, t_full, 2 * (G * b + g - 1))
                    for n in range(2):
                        dve.wait_ge(top_done, 2 * (G * b + g) + n + 1)
                        last = dve.tensor_tensor(
                            probs[g % 2][:, n * BH:(n + 1) * BH, :], s[n][:, :].rearrange("p (m k) -> p m k", m=BH),
                            wide(top[g % 2])[:, n * BH:(n + 1) * BH, :].to_broadcast([P, BH, P]), ALU.subtract)
                    last.then_inc(shifted, 1)

                def divide(b, g):
                    bk = bank[6][:, 0:KV * (HD + 1)].rearrange("p (n d) -> p n d", d=HD + 1)
                    dve.wait_ge(a_full, G * b + g + 1)
                    dve.reciprocal(inv[:, :], bk[:, :, HD]).then_inc(inv_done, 1)
                    dve.wait_ge(inv_done, G * b + g + 1)
                    dve.tensor_tensor(a[:, g, :, :], bk[:, :, 0:HD], wide(inv).to_broadcast([P, KV, HD]), ALU.mult
                                      ).then_inc(a_done, 1)

                def result_low(b):
                    dve.wait_ge(at_hi, b + 1)
                    dve.tensor_tensor(at[1][:, :, :], bank[7][:, :].rearrange("p (g t) -> p g t", g=G),
                                      as_f32(at[0][:, :, :]), ALU.subtract).then_inc(at_done, 1)

                def add_out(b):
                    dve.wait_ge(o_full, b + 1)
                    xb = x[:, bass.ds(b, 1), :].rearrange("p o d -> p (o d)")
                    dve.tensor_tensor(xb, xb, bank[7][:, :], ALU.add).then_inc(o_done, 1)

                def batch(b, first):
                    shift(b, 0)
                    if not first:
                        divide(b - 1, 2)
                    shift(b, 1)
                    if not first:
                        divide(b - 1, 3)
                    shift(b, 2)
                    if not first:
                        result_low(b - 1)
                    divide(b, 0)
                    shift(b, 3)
                    divide(b, 1)
                    if not first:
                        add_out(b - 1)

                def turn(t, first):
                    batch(2 * t, first)
                    batch(2 * t + 1, False)

                turns(turn, dve)
                dve.wait_ge(o_done, B - 1)
                for b in range(B - 1):
                    core.statistics(dve, b)
                divide(B - 1, 2)
                divide(B - 1, 3)
                result_low(B - 1)
                add_out(B - 1)
                dve.wait_ge(o_done, B)
                core.statistics(dve, B - 1)


def l1_ffn(core, dram):
    nc, x, bank = core.nc, core.x, core.bank
    BOT, RD, SLOTS, TOPK, VB = 64, 48, P, 8, 32
    TAU_LOW, TAU_HIGH, EARLY_EXIT = 0.5, 2.0, 0.05
    TAKEN = -3e38
    GELU = float(np.sqrt(2.0 / np.pi))
    with ExitStack() as ctx:
        sb = lambda name, shape, dt=F32: core.sb(ctx, "l1f_" + name, shape, dt)
        sem = lambda name: core.sem("l1f_" + name)
        xn, xt = sb("xn", [P, B, D]), sb("xt", [P, DC, T])
        w_q, w_r, keys = sb("w_q", [P, DC, BOT]), sb("w_r", [BOT, RD]), sb("keys", [BOT, SLOTS])
        values, w_vd, w_vu = sb("values", [P, DC, SLOTS]), sb("w_vd", [P, DC, VB]), sb("w_vu", [VB, D])
        w_u1, w_u2 = sb("w_u1", [P, DC, P]), sb("w_u2", [P, 1])
        consts = sb("consts", [P, 4])
        log_rel = sb("log_rel", [P, 1, SLOTS])
        ones = sb("ones", [P, P])
        rk, vd, table = sb("rk", [RD, SLOTS]), sb("vd", [VB, SLOTS]), sb("table", [SLOTS, D])
        q, rq = sb("q", [BOT, T]), sb("rq", [RD, T])
        z, th = sb("z", [P, T]), sb("th", [P, T])
        route, rest, attn = sb("route", [P, B, SLOTS]), sb("rest", [P, B, SLOTS]), sb("attn", [P, B, SLOTS])
        top8, top, total = sb("top8", [P, B, TOPK]), sb("top", [P, B]), sb("total", [P, B])
        attn_t = sb("attn_t", [SLOTS, T])
        lv, lsum, u, gate = sb("lv", [P, B]), sb("lsum", [P, 1]), sb("u", [P, B]), sb("gate", [P, B])
        loaded, ones_done = sem("loaded"), sem("ones_done")
        names = (("L1f_wq", w_q), ("L1f_wr", w_r), ("L1f_keys", keys), ("L1f_values", values), ("L1f_wvd", w_vd),
                 ("L1f_wvu", w_vu), ("L1f_wu1", w_u1), ("L1f_wu2", w_u2), ("L1f_consts", consts), ("L1f_log_rel", log_rel))

        def loads(sp):
            for name, t in names:
                sp.dma_start(t[tuple(slice(None) for _ in t.shape)], dram[name]).then_inc(loaded, 16)

        norm_stage(core, xn, xt, loads)

        small_full, small_done, table_full, table_done = (sem("small_full"), sem("small_done"), sem("table_full"),
                                                          sem("table_done"))
        q_full, q_done, rq_full, rq_done = sem("q_full"), sem("q_done"), sem("rq_full"), sem("rq_done")
        z_full, z_done, gelu_step, th_done, gelu_done = (sem("z_full"), sem("z_done"), sem("gelu_step"), sem("th_done"),
                                                         sem("gelu_done"))
        route_full, attn_full, route_done, top8_done, rest_done = (sem("route_full"), sem("attn_full"),
                                                                   sem("route_done"), sem("top8_done"), sem("rest_done"))
        attn_step, top_done, exp_done = sem("attn_step"), sem("top_done"), sem("exp_done")
        t_full, t_done, aux_full, aux_read = sem("t_full"), sem("t_done"), sem("aux_full"), sem("aux_read")
        learned_full, var_done, lv_done, lsum_done, mean_full = (sem("learned_full"), sem("var_done"), sem("lv_done"),
                                                                 sem("lsum_done"), sem("mean_full"))
        gate_step, tanh_in, tanh_out = sem("gate_step"), sem("tanh_in"), sem("tanh_out")
        y_added = sem("y_added")
        with nc.Block() as block:

            @block.gpsimd
            def _(pool):
                pool.memset(ones[:, :], 1.0).then_inc(ones_done, 1)
                for b in range(B):
                    pool.tensor_tensor(x[:, b, :], x[:, b, :], xn[:, b, :], ALU.add).then_inc(y_added, 1)

            @block.tensor
            def _(pe):
                pe.wait_ge(loaded, 16 * len(names))
                for half in range(2):
                    part = slice(half * HALF, (half + 1) * HALF)
                    for c in range(DC):
                        mm = product(pe, bank[half][0:BOT, :], [w_q[:, c, :]], [xt[:, c, part]], c == 0, c == DC - 1)
                    mm.then_inc(q_full, 1)
                for half in range(2):
                    part = slice(half * HALF, (half + 1) * HALF)
                    for c in range(DC):
                        mm = product(pe, bank[2 + half][:, :], [w_u1[:, c, :]], [xt[:, c, part]], c == 0, c == DC - 1)
                    mm.then_inc(z_full, 1)
                product(pe, bank[4][0:RD, 0:SLOTS], [w_r[:, :]], [keys[:, :]], True, True).then_inc(small_full, 1)
                for c in range(DC):
                    mm = product(pe, bank[5][0:VB, 0:SLOTS], [w_vd[:, c, :]], [values[:, c, :]], c == 0, c == DC - 1)
                mm.then_inc(small_full, 1)
                pe.wait_ge(q_done, 2)
                for half in range(2):
                    part = slice(half * HALF, (half + 1) * HALF)
                    product(pe, bank[6 + half][0:RD, :], [w_r[:, :]], [q[:, part]], True, True).then_inc(rq_full, 1)
                pe.wait_ge(small_done, 2)
                product(pe, bank[4][:, :], [vd[:, :]], [w_vu[:, :]], True, True).then_inc(table_full, 1)
                pe.wait_ge(rq_done, 2)
                for b in range(B):
                    mm = product(pe, bank[b // BH][:, (b % BH) * P:(b % BH + 1) * P], [rq[:, b * P:(b + 1) * P]],
                                 [rk[:, :]], True, True)
                    mm.then_inc(route_full, 1)
                for b in range(B):
                    mm = product(pe, bank[6 + b // BH][:, (b % BH) * P:(b % BH + 1) * P], [q[:, b * P:(b + 1) * P]],
                                 [keys[:, :]], True, True)
                    mm.then_inc(attn_full, 1)
                pe.wait_ge(ones_done, 1)
                pe.wait_ge(lsum_done, 1)
                product(pe, bank[5][:, 0:1], [ones[:, :]], [lsum[:, :]], True, True).then_inc(mean_full, 1)
                pe.wait_ge(gelu_done, 1)
                pe.wait_ge(z_done, 2)
                for b in range(B):
                    mm = product(pe, bank[2][:, b:b + 1], [z[:, b * P:(b + 1) * P]], [w_u2[:, :]], True, True)
                mm.then_inc(learned_full, 1)
                pe.wait_ge(route_done, 2)
                for b in range(B):
                    pe.wait_ge(exp_done, b + 1)
                    mm = pe.transpose(bank[b // BH][:, (b % BH) * P:(b % BH + 1) * P], attn[:, b, :], core.ident[:, :])
                    if b % BH == BH - 1:
                        mm.then_inc(t_full, 1)
                pe.wait_ge(table_done, 1)
                ring = (3, 4, 6, 7)
                for b in range(B):
                    if b % BH == 0:
                        pe.wait_ge(t_done, b // BH + 1)
                    wait(pe, aux_read, b - 3)
                    product(pe, bank[ring[b % 4]][:, :], [attn_t[:, b * P:(b + 1) * P]], [table[:, :]], True, True
                            ).then_inc(aux_full, 1)

            @block.scalar
            def _(act):
                act.wait_ge(var_done, 1)
                act.activation(lv[:, :], lv[:, :], ACT.Ln, bias=1.0).then_inc(lv_done, 1)
                act.wait_ge(loaded, 16 * len(names))
                for half in range(2):
                    part = slice(half * HALF, (half + 1) * HALF)
                    act.wait_ge(q_full, half + 1)
                    act.activation(q[:, part], bank[half][0:BOT, :], ACT.Copy).then_inc(q_done, 1)
                for half in range(2):
                    part = slice(half * HALF, (half + 1) * HALF)
                    act.wait_ge(z_full, half + 1)
                    act.activation(z[:, part], bank[2 + half][:, :], ACT.Identity, bias=consts[:, 0:1]
                                   ).then_inc(z_done, 1)
                act.wait_ge(small_full, 2)
                act.activation(rk[:, :], bank[4][0:RD, 0:SLOTS], ACT.Copy).then_inc(small_done, 1)
                act.activation(vd[:, :], bank[5][0:VB, 0:SLOTS], ACT.Copy).then_inc(small_done, 1)
                for half in range(2):
                    part = slice(half * HALF, (half + 1) * HALF)
                    act.wait_ge(rq_full, half + 1)
                    act.activation(rq[:, part], bank[6 + half][0:RD, :], ACT.Copy).then_inc(rq_done, 1)
                act.wait_ge(table_full, 1)
                act.activation(table[:, :], bank[4][:, :], ACT.Copy).then_inc(table_done, 1)
                act.wait_ge(gelu_step, 3)
                act.activation(th[:, :], th[:, :], ACT.Tanh, scale=GELU).then_inc(th_done, 1)
                act.wait_ge(tanh_in, 1)
                act.activation(u[:, :], u[:, :], ACT.Tanh, scale=0.5).then_inc(tanh_out, 1)
                for b in range(B):
                    act.wait_ge(top_done, 1)
                    act.activation(attn[:, b, :], attn[:, b, :], ACT.Exp, bias=top[:, b:b + 1],
                                   accum_out=total[:, b:b + 1]).then_inc(exp_done, 1)
                act.wait_ge(tanh_in, 2)
                act.activation(gate[:, :], gate[:, :], ACT.Tanh, scale=0.5).then_inc(tanh_out, 1)
                for half in range(2):
                    act.wait_ge(t_full, half + 1)
                    act.activation(attn_t[:, half * HALF:(half + 1) * HALF], bank[half][:, :], ACT.Copy
                                   ).then_inc(t_done, 1)

            @block.vector
            def _(dve):
                steps = [0]

                def then(instruction):
                    steps[0] += 1
                    instruction.then_inc(gate_step, 1)
                    dve.wait_ge(gate_step, steps[0])

                then(dve.tensor_tensor(lv[:, :], core.mv[:, :, 1], core.rstd[:, :], ALU.mult))
                dve.tensor_tensor(lv[:, :], lv[:, :], core.rstd[:, :], ALU.mult).then_inc(var_done, 1)
                dve.wait_ge(z_done, 2)
                dve.tensor_tensor(th[:, :], z[:, :], z[:, :], ALU.mult).then_inc(gelu_step, 1)
                dve.wait_ge(gelu_step, 1)
                dve.tensor_scalar(th[:, :], th[:, :], 0.044715, 1.0, ALU.mult, ALU.add).then_inc(gelu_step, 1)
                dve.wait_ge(gelu_step, 2)
                dve.tensor_tensor(th[:, :], th[:, :], z[:, :], ALU.mult).then_inc(gelu_step, 1)
                dve.wait_ge(lv_done, 1)
                dve.tensor_reduce(lsum[:, :], lv[:, :], AX.X, ALU.add).then_inc(lsum_done, 1)
                for half in range(2):
                    dve.wait_ge(route_full, BH * (half + 1))
                    dve.scalar_tensor_tensor(route[:, half * BH:(half + 1) * BH, :],
                                             bank[half][:, :].rearrange("p (b n) -> p b n", b=BH),
                                             1.0 / float(np.sqrt(RD)), log_rel[:, :, :].to_broadcast([P, BH, SLOTS]),
                                             ALU.mult, ALU.add).then_inc(route_done, 1)
                dve.wait_ge(route_done, 2)
                for b in range(B):
                    dve.max(top8[:, b, :], route[:, b, :]).then_inc(top8_done, 1)
                dve.wait_ge(th_done, 1)
                dve.scalar_tensor_tensor(z[:, :], th[:, :], 1.0, z[:, :], ALU.add, ALU.mult).then_inc(gelu_done, 1)
                dve.wait_ge(top8_done, B)
                for b in range(B):
                    dve.match_replace(rest[:, b, :], top8[:, b, :], route[:, b, :], TAKEN).then_inc(rest_done, 1)
                for half in range(2):
                    dve.wait_ge(attn_full, BH * (half + 1))
                    dve.scalar_tensor_tensor(attn[:, half * BH:(half + 1) * BH, :],
                                             bank[6 + half][:, :].rearrange("p (b n) -> p b n", b=BH),
                                             1.0 / float(np.sqrt(BOT)), log_rel[:, :, :].to_broadcast([P, BH, SLOTS]),
                                             ALU.mult, ALU.add).then_inc(attn_step, 1)
                dve.wait_ge(rest_done, B)
                dve.tensor_tensor(rest[:, :, :], rest[:, :, :], route[:, :, :], ALU.is_equal).then_inc(attn_step, 1)
                dve.wait_ge(attn_step, 3)
                dve.scalar_tensor_tensor(attn[:, :, :], rest[:, :, :], MASKED, attn[:, :, :], ALU.mult, ALU.add
                                         ).then_inc(attn_step, 1)
                dve.wait_ge(attn_step, 4)
                dve.tensor_reduce(top[:, :], attn[:, :, :], AX.X, ALU.max).then_inc(attn_step, 1)
                dve.wait_ge(attn_step, 5)
                dve.tensor_scalar(top[:, :], top[:, :], -1.0, None, ALU.mult).then_inc(top_done, 1)
                dve.wait_ge(learned_full, 1)
                dve.tensor_scalar(u[:, :], bank[2][:, 0:B], 0.5, consts[:, 1:2], ALU.mult, ALU.add
                                  ).then_inc(tanh_in, 1)
                dve.wait_ge(mean_full, 1)
                then(dve.tensor_scalar(lsum[:, :], bank[5][:, 0:1], 1.0 / T, 1e-6, ALU.mult, ALU.add))
                then(dve.reciprocal(lsum[:, :], lsum[:, :]))
                then(dve.tensor_scalar(lv[:, :], lv[:, :], lsum[:, 0:1], 0.5, ALU.mult, ALU.mult))
                dve.wait_ge(tanh_out, 1)
                then(dve.tensor_scalar(u[:, :], u[:, :], 1.25, 1.25, ALU.mult, ALU.add))
                then(dve.tensor_tensor(u[:, :], u[:, :], lv[:, :], ALU.add))
                then(dve.tensor_scalar(u[:, :], u[:, :], 0.0, 5.0, ALU.max, ALU.min))
                then(dve.tensor_scalar(u[:, :], u[:, :], -TAU_LOW, 1.0 / (TAU_HIGH - TAU_LOW), ALU.add, ALU.mult))
                then(dve.tensor_scalar(u[:, :], u[:, :], 0.0, 1.0, ALU.max, ALU.min))
                dve.tensor_scalar(gate[:, :], u[:, :], consts[:, 2:3], consts[:, 3:4], ALU.mult, ALU.add
                                  ).then_inc(tanh_in, 1)
                dve.wait_ge(tanh_out, 2)
                then(dve.tensor_scalar(gate[:, :], gate[:, :], 0.5, 0.5, ALU.mult, ALU.add))
                then(dve.scalar_tensor_tensor(gate[:, :], gate[:, :], EARLY_EXIT, gate[:, :], ALU.is_ge, ALU.mult))
                dve.wait_ge(exp_done, B)
                then(dve.reciprocal(total[:, :], total[:, :]))
                then(dve.tensor_tensor(gate[:, :], gate[:, :], total[:, :], ALU.mult))
                dve.wait_ge(y_added, B)
                for b in range(B):
                    dve.wait_ge(aux_full, b + 1)
                    dve.scalar_tensor_tensor(x[:, b, :], bank[(3, 4, 6, 7)[b % 4]][:, :], gate[:, b:b + 1],
                                             x[:, b, :], ALU.mult, ALU.add).then_inc(aux_read, 1)
                    dve.wait_ge(aux_read, b + 1)
                    core.statistics(dve, b)


def l2_attention(core, dram):
    nc, x, bank = core.nc, core.x, core.bank
    TAPS, PAD = 7, 3
    KINDS = 4
    SETS = 2
    BY_DVE = 2
    with ExitStack() as ctx:
        sb = lambda name, shape, dt=F32: core.sb(ctx, "l2x_" + name, shape, dt)
        sem = lambda name: core.sem("l2x_" + name)
        xn, xt = sb("xn", [P, B, D]), sb("xt", [P, DC, T])
        fc, fo = sb("fc", [P, DC, T]), sb("fo", [P, DC, T])
        stat = sb("stat", [P, DC, KINDS, B])
        padded, acc = sb("padded", [KINDS * B, D + 2 * PAD]), sb("acc", [KINDS * B, D])
        taps, affine = sb("taps", [KINDS * B, TAPS]), sb("affine", [SETS * B, 2])
        pick, mean = sb("pick", [KINDS * B, SETS * B]), sb("mean", [SETS * B, SETS, B])
        z, zstat, zmv = sb("z", [SETS * B, D]), sb("zstat", [SETS * B, 6]), sb("zmv", [SETS * B, 2])
        mu, dev, rs = sb("mu", [SETS * B, 1]), sb("dev", [SETS * B, 1]), sb("rs", [SETS * B, 1])
        amap = sb("amap", [P, DC, SETS, B])
        small_loaded, made, const_done = sem("small_loaded"), sem("made"), sem("const_done")

        def loads(sp):
            sp.dma_start(taps[:, :], dram["L2x_taps"]).then_inc(small_loaded, 16)
            sp.dma_start(affine[:, :], dram["L2x_affine"]).then_inc(small_loaded, 16)

        norm_stage(core, xn, xt, loads)

        step = sem("step")
        stat_full, stat_done, z_full, z_done = sem("stat_full"), sem("stat_done"), sem("z_full"), sem("z_done")
        mean_in, mean_full, var_in, var_full, rs_in, rs_done = (sem("mean_in"), sem("mean_full"), sem("var_in"),
                                                                sem("var_full"), sem("rs_in"), sem("rs_done"))
        tanh_in, tanh_out, map_in, map_full, map_done = (sem("tanh_in"), sem("tanh_out"), sem("map_in"),
                                                         sem("map_full"), sem("map_done"))
        out_ready, back_full, added = sem("out_ready"), sem("back_full"), sem("added")
        fc_done, fo_done, means_done = sem("fc_done"), sem("fo_done"), sem("means_done")
        crucial_scaled, others_scaled = sem("crucial_scaled"), sem("others_scaled")
        by_batch = lambda t, c: t[:, c, :].rearrange("p (b n) -> p b n", b=B)
        with nc.Block() as block:

            def scale_others(eng, c):
                return eng.tensor_tensor(by_batch(fo, c), by_batch(fo, c),
                                         amap[:, c, 1, :].rearrange("p (b o) -> p b o", o=1).to_broadcast([P, B, P]),
                                         ALU.mult)

            @block.gpsimd
            def _(pool):
                for c in range(DC):
                    pool.wait_ge(fc_done, c + 1)
                    pool.tensor_tensor(fo[:, c, :], xt[:, c, :], fc[:, c, :], ALU.subtract).then_inc(fo_done, 1)
                pool.memset(mean[:, :, :], 1.0 / B).then_inc(made, 1)
                pool.memset(padded[:, :], 0.0).then_inc(const_done, 1)
                pool.wait_ge(made, 1)
                pool.affine_select(out=mean[:, :, :], in_=mean[:, :, :], compare_op=ALU.is_ge, fill=0.0, base=0,
                                   pattern=[[-B, SETS], [0, B]], channel_multiplier=1).then_inc(made, 1)
                pool.wait_ge(made, 2)
                pool.affine_select(out=mean[:, :, :], in_=mean[:, :, :], compare_op=ALU.is_ge, fill=0.0, base=B - 1,
                                   pattern=[[B, SETS], [0, B]], channel_multiplier=-1).then_inc(const_done, 1)
                pool.wait_ge(rs_in, 1)
                pool.tensor_tensor(rs[:, :], rs[:, :], core.neg_half[0:SETS * B, 0:1], ALU.pow).then_inc(rs_done, 1)
                pool.wait_ge(map_done, 1)
                scale_others(pool, DC - 1).then_inc(others_scaled, 1)

            @block.tensor
            def _(pe):
                pe.wait_ge(stat_done, 1)
                pe.wait_ge(means_done, 2)
                for c in range(DC):
                    mm = pe.transpose(bank[0][0:KINDS * B, c * P:(c + 1) * P],
                                      stat[:, c, :, :].rearrange("p k b -> p (k b)"), core.ident[:, :])
                mm.then_inc(stat_full, 1)
                pe.wait_ge(z_done, 1)
                product(pe, bank[1][0:SETS * B, :], [pick[:, :]], [acc[:, :]], True, True).then_inc(z_full, 1)
                pe.wait_ge(const_done, 2)
                group = mean[:, :, :].rearrange("p s b -> p (s b)")
                pe.wait_ge(mean_in, 1)
                product(pe, bank[2][0:SETS * B, 0:1], [group], [zmv[:, 0:1]], True, True).then_inc(mean_full, 1)
                pe.wait_ge(var_in, 1)
                product(pe, bank[3][0:SETS * B, 0:1], [group], [dev[:, :]], True, True).then_inc(var_full, 1)
                pe.wait_ge(map_in, 1)
                for c in range(DC):
                    mm = pe.transpose(bank[0][:, c * SETS * B:(c + 1) * SETS * B], z[:, c * P:(c + 1) * P],
                                      core.ident[0:SETS * B, 0:SETS * B])
                mm.then_inc(map_full, 1)
                for b in range(B):
                    pe.wait_ge(out_ready, DC)
                    for c in range(DC):
                        mm = pe.transpose(bank[b][:, c * P:(c + 1) * P], fc[:, c, b * P:(b + 1) * P], core.ident[:, :])
                    mm.then_inc(back_full, 1)

            @block.scalar
            def _(act):
                for k, (t, done, count) in enumerate(((fc, fc_done, CRUCIAL), (fo, fo_done, OTHERS))):
                    wait(act, means_done, k)
                    for c in range(DC - k * BY_DVE):
                        act.wait_ge(done, c + 1)
                        for b in range(B):
                            last = act.activation(xn[:, b, c * P:(c + 1) * P], t[:, c, b * P:(b + 1) * P], ACT.Copy,
                                                  scale=1.0 / count, accum_out=stat[:, c, 2 + k, b:b + 1])
                    last.then_inc(means_done, 1)
                act.wait_ge(tanh_in, 1)
                act.activation(z[:, :], z[:, :], ACT.Tanh, scale=0.5).then_inc(tanh_out, 1)
                act.wait_ge(map_done, 1)
                for c in range(DC):
                    for b in range(B):
                        last = act.activation(fc[:, c, b * P:(b + 1) * P], fc[:, c, b * P:(b + 1) * P], ACT.Copy,
                                              scale=amap[:, c, 0, b:b + 1])
                    last.then_inc(crucial_scaled, 1)

            @block.vector
            def _(dve):
                steps = [0]

                def mark(instruction):
                    steps[0] += 1
                    instruction.then_inc(step, 1)

                def settle():
                    dve.wait_ge(step, steps[0])

                for c in range(DC):
                    dve.tensor_tensor(by_batch(fc, c), by_batch(xt, c), core.crucial[:, c * B:(c + 1) * B, :], ALU.mult
                                      ).then_inc(fc_done, 1)
                for k, (t, done) in enumerate(((fc, fc_done), (fo, fo_done))):
                    for c in range(DC):
                        dve.wait_ge(done, c + 1)
                        dve.tensor_reduce(stat[:, c, k, :], by_batch(t, c), AX.X, ALU.max)
                for c in range(DC - BY_DVE, DC):
                    mark(dve.tensor_reduce(stat[:, c, 3, :], by_batch(fo, c), AX.X, ALU.add))
                settle()
                dve.tensor_scalar(stat[:, DC - BY_DVE:DC, 3, :], stat[:, DC - BY_DVE:DC, 3, :], 1.0 / OTHERS, None,
                                  ALU.mult).then_inc(stat_done, 1)
                dve.wait_ge(small_loaded, 32)
                dve.wait_ge(const_done, 2)
                dve.wait_ge(stat_full, 1)
                mark(dve.tensor_copy(padded[:, PAD:PAD + D], bank[0][0:KINDS * B, :]))
                settle()
                mark(dve.tensor_scalar(acc[:, :], padded[:, 0:D], taps[:, 0:1], None, ALU.mult))
                for t in range(1, TAPS):
                    settle()
                    mark(dve.scalar_tensor_tensor(acc[:, :], padded[:, t:t + D], taps[:, t:t + 1], acc[:, :], ALU.mult,
                                                  ALU.add))
                settle()
                dve.tensor_tensor(pick[:, :], core.ident[0:KINDS * B, 0:SETS * B],
                                  core.ident[0:KINDS * B, SETS * B:KINDS * B], ALU.add).then_inc(z_done, 1)
                dve.wait_ge(z_full, 1)
                mark(dve.tensor_copy(z[:, :], bank[1][0:SETS * B, :]))
                settle()
                mark(dve.bn_stats(zstat[:, :], z[:, :]))
                settle()
                dve.bn_aggr(zmv[:, :], zstat[:, :]).then_inc(mean_in, 1)
                dve.wait_ge(mean_in, 1)
                dve.wait_ge(mean_full, 1)
                mark(dve.tensor_copy(mu[:, :], bank[2][0:SETS * B, 0:1]))
                settle()
                mark(dve.tensor_tensor(dev[:, :], zmv[:, 0:1], mu[:, :], ALU.subtract))
                settle()
                mark(dve.tensor_tensor(dev[:, :], dev[:, :], dev[:, :], ALU.mult))
                settle()
                dve.tensor_tensor(dev[:, :], dev[:, :], zmv[:, 1:2], ALU.add).then_inc(var_in, 1)
                dve.wait_ge(var_full, 1)
                dve.tensor_scalar_add(rs[:, :], bank[3][0:SETS * B, 0:1], EPS).then_inc(rs_in, 1)
                dve.wait_ge(rs_done, 1)
                mark(dve.tensor_scalar(z[:, :], z[:, :], mu[:, 0:1], rs[:, 0:1], ALU.subtract, ALU.mult))
                settle()
                mark(dve.tensor_scalar(z[:, :], z[:, :], affine[:, 0:1], affine[:, 1:2], ALU.mult, ALU.add))
                settle()
                dve.tensor_scalar(z[:, :], z[:, :], 0.0, None, ALU.max).then_inc(tanh_in, 1)
                dve.wait_ge(tanh_out, 1)
                dve.tensor_scalar(z[:, :], z[:, :], 0.5, 0.5, ALU.mult, ALU.add).then_inc(map_in, 1)
                dve.wait_ge(map_full, 1)
                dve.tensor_copy(amap[:, :, :, :], bank[0][:, 0:DC * SETS * B].rearrange("p (c s b) -> p c s b", c=DC, s=SETS)
                                ).then_inc(map_done, 1)
                dve.wait_ge(map_done, 1)
                for c in range(DC + 1):
                    if c < DC - 1:
                        mark(scale_others(dve, c))
                    if c >= 1:
                        settle()
                        if c == DC:
                            dve.wait_ge(others_scaled, 1)
                        dve.wait_ge(crucial_scaled, c)
                        dve.tensor_tensor(fc[:, c - 1, :], fc[:, c - 1, :], fo[:, c - 1, :], ALU.add
                                          ).then_inc(out_ready, 1)
                for b in range(B):
                    dve.wait_ge(back_full, b + 1)
                    dve.tensor_tensor(x[:, b, :], x[:, b, :], bank[b][:, :], ALU.add).then_inc(added, 1)
                    dve.wait_ge(added, b + 1)
                    core.statistics(dve, b)


def routed_ffn(core, dram, name, top_k, softmax, base, scaling, out=None):
    nc, x, bank = core.nc, core.x, core.bank
    E, R = 8, 16
    with ExitStack() as ctx:
        sb = lambda n, shape, dt=F32: core.sb(ctx, name + "_" + n, shape, dt)
        sem = lambda n: core.sem(name + "_" + n)
        xn, xt = sb("xn", [P, B, D]), sb("xt", [P, DC, T])
        w_a, w_b = sb("w_a", [P, DC, P + E]), sb("w_b", [P, D])
        p, wide, wide2 = sb("p", [P, B, E]), sb("wide", [P, B, E, E]), sb("wide2", [P, B, E, E])
        before = sb("before", [P, 1, E, E])
        red, rank, weight = sb("red", [P, B]), sb("rank", [P, B, E]), sb("weight", [P, B, E])
        h, ht = sb("h", [P, B, E, R]), sb("ht", [P, T])
        loaded, base_loaded, made, before_done = sem("loaded"), sem("base_loaded"), sem("made"), sem("before_done")
        if out is None:
            ctx_raw, ctx_loaded, ctx_hi = sb("ctx_raw", [P, DC, T]), sem("ctx_loaded"), sem("ctx_hi")
        if base:
            w_base, bias = sb("w_base", [P, DC, D]), sb("bias", [P, D])

        def loads(sp):
            sp.dma_start(w_a[:, :, :], dram[name + "_a"]).then_inc(loaded, 16)
            sp.dma_start(w_b[:, :], dram[name + "_b"]).then_inc(loaded, 16)
            if base:
                sp.dma_start(w_base[:, :, :], dram[name + "_base"]).then_inc(base_loaded, 16)
                sp.dma_start(bias[:, :], dram[name + "_bias"]).then_inc(base_loaded, 16)
            if out is None:
                sp.dma_start(ctx_raw[:, :, :], dram["ctx_t"]).then_inc(ctx_loaded, 16)

        norm_stage(core, xn, xt, loads)

        a_full, a_read, step, exp_in, exp_out = sem("a_full"), sem("a_read"), sem("step"), sem("exp_in"), sem("exp_out")
        h_done, t_full, t_done, o_full, o_read, biased = (sem("h_done"), sem("t_full"), sem("t_done"), sem("o_full"),
                                                          sem("o_read"), sem("biased"))
        low = lambda b: bank[b // 2][:, (b % 2) * (P + E):(b % 2) * (P + E) + P]
        logits = lambda n: bank[n][:, 0:2 * (P + E)].rearrange("p (b m) -> p b m", b=2)[:, :, P:P + E]
        with nc.Block() as block:

            if out is not None:
                stored = sem("stored")

                @block.sync
                def _(sp):
                    for b in range(B):
                        sp.wait_ge(o_read, b + 1)
                        sp.dma_start(out[b, :, :], x[:, b, :]).then_inc(stored, 16)
                    sp.wait_ge(stored, 16 * B)

            @block.gpsimd
            def _(pool):
                pool.memset(before[:, :, :, :], 1.0).then_inc(made, 1)
                pool.wait_ge(made, 1)
                pool.affine_select(out=before[:, 0, :, :], in_=before[:, 0, :, :], compare_op=ALU.is_gt, fill=0.0,
                                   base=0, pattern=[[1, E], [-1, E]], channel_multiplier=0).then_inc(before_done, 1)
                if base:
                    pool.wait_ge(base_loaded, 32)
                    for b in range(B):
                        pool.tensor_tensor(x[:, b, :], x[:, b, :], bias[:, :], ALU.add).then_inc(biased, 1)
                if out is None:
                    for c in range(DC):
                        pool.wait_ge(ctx_hi, c + 1)
                        pool.tensor_tensor(core.cin2[1][:, c, :], ctx_raw[:, c, :], as_f32(core.cin2[0][:, c, :]),
                                           ALU.subtract).then_inc(core.ctx2_split, 1)

            @block.tensor
            def _(pe):
                pe.wait_ge(loaded, 32)
                for b in range(B):
                    for c in range(DC):
                        mm = product(pe, bank[b // 2][:, (b % 2) * (P + E):(b % 2 + 1) * (P + E)],
                                     [xt[:, c, b * P:(b + 1) * P]], [w_a[:, c, :]], c == 0, c == DC - 1)
                    if b % 2:
                        mm.then_inc(a_full, 1)

                def base_product(b):
                    wait(pe, o_read, b - 3)
                    for c in range(DC):
                        product(pe, bank[4 + b % 4][:, :], [xt[:, c, b * P:(b + 1) * P]], [w_base[:, c, :]], c == 0,
                                False)

                if base:
                    pe.wait_ge(base_loaded, 32)
                    for b in range(4):
                        base_product(b)
                for half in range(2):
                    pe.wait_ge(h_done, half + 1)
                    for y in range(BH):
                        b = half * BH + y
                        mm = pe.transpose(bank[half][:, y * P:(y + 1) * P], h[:, b, :, :].rearrange("p e r -> p (e r)"),
                                          core.ident[:, :])
                    mm.then_inc(t_full, 1)
                for b in range(B):
                    pe.wait_ge(t_done, b // BH + 1)
                    if b >= 4 and base:
                        base_product(b)
                    elif b >= 4:
                        pe.wait_ge(o_read, b - 3)
                    product(pe, bank[4 + b % 4][:, :], [ht[:, b * P:(b + 1) * P]], [w_b[:, :]], not base, True
                            ).then_inc(o_full, 1)

            @block.scalar
            def _(act):
                if out is None:
                    act.wait_ge(ctx_loaded, 16)
                    for c in range(DC):
                        act.activation(core.cin2[0][:, c, :], ctx_raw[:, c, :], ACT.Copy).then_inc(ctx_hi, 1)
                if softmax:
                    act.wait_ge(exp_in, 1)
                    act.activation(p[:, :, :], p[:, :, :], ACT.Exp).then_inc(exp_out, 1)
                for half in range(2):
                    act.wait_ge(t_full, half + 1)
                    act.activation(ht[:, half * HALF:(half + 1) * HALF], bank[half][:, :], ACT.Copy).then_inc(t_done, 1)

            @block.vector
            def _(dve):
                steps = [0]

                def then(instruction):
                    steps[0] += 1
                    instruction.then_inc(step, 1)
                    dve.wait_ge(step, steps[0])

                over_e = lambda t: t[:, :].rearrange("p (b o) -> p b o", o=1).to_broadcast([P, B, E])
                for n in range(4):
                    dve.wait_ge(a_full, n + 1)
                    dve.tensor_copy(p[:, 2 * n:2 * n + 2, :], logits(n)).then_inc(a_read, 1)
                dve.wait_ge(a_read, 4)
                if softmax:
                    then(dve.tensor_reduce(red[:, :], p[:, :, :], AX.X, ALU.max))
                    dve.tensor_tensor(p[:, :, :], p[:, :, :], over_e(red), ALU.subtract).then_inc(exp_in, 1)
                    dve.wait_ge(exp_out, 1)
                    then(dve.tensor_reduce(red[:, :], p[:, :, :], AX.X, ALU.add))
                    then(dve.reciprocal(red[:, :], red[:, :]))
                    then(dve.tensor_tensor(p[:, :, :], p[:, :, :], over_e(red), ALU.mult))
                other = p[:, :, :].rearrange("p b (o e) -> p b o e", o=1).to_broadcast([P, B, E, E])
                own = p[:, :, :].rearrange("p b (e o) -> p b e o", o=1).to_broadcast([P, B, E, E])
                dve.tensor_tensor(wide[:, :, :, :], other, own, ALU.is_gt).then_inc(step, 1)
                dve.tensor_tensor(wide2[:, :, :, :], other, own, ALU.is_equal).then_inc(step, 1)
                steps[0] += 2
                dve.wait_ge(step, steps[0])
                dve.wait_ge(before_done, 1)
                then(dve.tensor_tensor(wide2[:, :, :, :], wide2[:, :, :, :], before[:, :, :, :].to_broadcast([P, B, E, E]),
                                       ALU.mult))
                then(dve.tensor_tensor(wide[:, :, :, :], wide[:, :, :, :], wide2[:, :, :, :], ALU.add))
                then(dve.tensor_reduce(rank[:, :, :], wide[:, :, :, :], AX.X, ALU.add))
                then(dve.scalar_tensor_tensor(weight[:, :, :], rank[:, :, :], float(top_k), p[:, :, :], ALU.is_lt,
                                              ALU.mult))
                if softmax:
                    then(dve.tensor_reduce(red[:, :], weight[:, :, :], AX.X, ALU.add))
                    then(dve.reciprocal(red[:, :], red[:, :]))
                    then(dve.scalar_tensor_tensor(weight[:, :, :], weight[:, :, :], scaling, over_e(red), ALU.mult,
                                                  ALU.mult))
                for b in range(B):
                    mm = dve.tensor_tensor(h[:, b, :, :], low(b).rearrange("p (e r) -> p e r", e=E),
                                           weight[:, b, :].rearrange("p (e o) -> p e o", o=1).to_broadcast([P, E, R]),
                                           ALU.mult)
                    if b == B - 1:
                        mm.then_inc(h_done, 2)
                if base:
                    dve.wait_ge(biased, B)
                for b in range(B):
                    dve.wait_ge(o_full, b + 1)
                    dve.tensor_tensor(x[:, b, :], x[:, b, :], bank[4 + b % 4][:, :], ALU.add).then_inc(o_read, 1)
                    if out is None:
                        dve.wait_ge(o_read, b + 1)
                        core.statistics(dve, b)


def l2_ffn(core, dram):
    routed_ffn(core, dram, "l2f", 2, True, True, 2.0)


def l3_ffn(core, dram, out):
    routed_ffn(core, dram, "l3f", 1, False, False, 1.0, out)


def l3_attention(core, dram):
    nc, x, bank = core.nc, core.x, core.bank
    GROUPS, G = 8, 4
    HP = P // 2
    SCALE = 1.0 / float(np.sqrt(P))
    with ExitStack() as ctx:
        sb = lambda name, shape, dt=F32: core.sb(ctx, "l3x_" + name, shape, dt)
        pair = lambda name, shape: core.pair(ctx, "l3x_" + name, shape)
        sem = lambda name: core.sem("l3x_" + name)
        qin, cin = pair("qin", [P, DC, T]), core.cin2
        raw_kv, raw_q, raw_o = sb("raw_kv", [P, 2, DC, P]), sb("raw_q", [P, 2, DC, P]), sb("raw_o", [P, 2, D])
        w_kv = pair("w_kv", [P, 2, DC, P])
        w_q = [pair("w_q0", [P, 2, DC, P]), pair("w_q1", [P, 2, DC, P])]
        w_o = pair("w_o", [P, 2, D])
        kv_loaded, kv_hi, kv_ready = sem("kv_loaded"), sem("kv_hi"), sem("kv_ready")
        q_loaded, q_hi, q_ready = sem("q_loaded"), sem("q_hi"), sem("q_ready")

        def first_loads(sp):
            for j in range(2):
                sp.dma_start(raw_q[:, j, :, :], dram["L3_q"][j, :, :, :]).then_inc(q_loaded, 16)
            sp.dma_start(raw_kv[:, :, :, :], dram["L3_kv"][0, :, :, :, :]).then_inc(kv_loaded, 16)

        def first_high(act):
            act.wait_ge(q_loaded, 32)
            act.activation(w_q[0][0][:, :, :, :], raw_q[:, :, :, :], ACT.Copy).then_inc(q_hi, 1)
            act.wait_ge(kv_loaded, 16)
            act.activation(w_kv[0][:, :, :, :], raw_kv[:, :, :, :], ACT.Copy).then_inc(kv_hi, 1)

        def first_low(pool):
            pool.wait_ge(q_hi, 1)
            pool.tensor_tensor(w_q[0][1][:, :, :, :], raw_q[:, :, :, :], as_f32(w_q[0][0][:, :, :, :]), ALU.subtract
                               ).then_inc(q_ready, 1)
            pool.wait_ge(kv_hi, 1)
            pool.tensor_tensor(w_kv[1][:, :, :, :], raw_kv[:, :, :, :], as_f32(w_kv[0][:, :, :, :]), ALU.subtract
                               ).then_inc(kv_ready, 1)

        with ExitStack() as ctx1:
            xn = core.sb(ctx1, "l3x_xn", [P, B, D])
            norm_stage(core, xn, qin, first_loads, first_high, first_low)

        q = [sb("q0", [P, T]), sb("q1", [P, T])]
        k, vt, v = sb("k", [P, T]), sb("vt", [P, T]), sb("v", [P, B, P])
        rope = sb("rope", [P, 2, P])
        cosine = [sb("cosine0", [P, HALF]), sb("cosine1", [P, HALF])]
        cross = [sb("cross0", [P, HALF]), sb("cross1", [P, HALF])]
        probs = [sb("probs0", [P, B, P]), sb("probs1", [P, B, P])]
        probs_t = sb("probs_t", [P, B, P])
        heads = [pair("heads01", [P, 2, T]), pair("heads23", [P, 2, T])]
        mask = sb("mask", [P, B, P])
        top, row_sum, inv_sum = sb("top", [P, B]), sb("row_sum", [P, B]), sb("inv_sum", [P, B])

        mask_loaded, rope_loaded = sem("mask_loaded"), sem("rope_loaded")
        o_loaded, o_hi, o_ready = sem("o_loaded"), sem("o_hi"), sem("o_ready")
        ring_full, ring_drained = sem("ring_full"), sem("ring_drained")
        rotated = sem("rotated")
        scores_full, scores_read, top_raw, top_ready = (sem("scores_full"), sem("scores_read"), sem("top_raw"),
                                                        sem("top_ready"))
        exp_done, inv_done, probs_ready = sem("exp_done"), sem("inv_done"), sem("probs_ready")
        t_full, t_act, t_dve = sem("t_full"), sem("t_act"), sem("t_dve")
        v_full, v_act, v_dve = sem("v_full"), sem("v_act"), sem("v_dve")
        h_full, h_hi, h_drained = sem("h_full"), sem("h_hi"), sem("h_drained")

        N = GROUPS
        PER = 28
        OFFSET = {"q1": 0, "v": 2, "out23a": 4, "q2": 8, "out23b": 10, "q3": 14, "out01a": 16, "q0": 20, "k": 22,
                  "out01b": 24}
        MISSING = {"q1": 8, "v": 8, "q2": 4}

        def ring_at(g, what):
            first = isinstance(g, int) and g == 0
            return 4 + PER * g - 8 + OFFSET[what] + (MISSING.get(what, 0) if first else 0)

        OUT_LAST = ring_at(N - 1, "q0")

        def rope_at(g, what):
            return 4 + 10 * g + {"q1": 0, "q2": 2, "q3": 4, "q0": 6, "k": 8}[what]

        def turns(body, eng):
            body(0, True, False)
            with eng.Fori(1, N - 1) as g:
                body(g, False, False)
            body(N - 1, False, True)

        with nc.Block() as block:

            @block.sync
            def _(sp):
                def load_q(n, g, s):
                    wait(sp, q_ready, n)
                    for j in range(2):
                        sp.dma_start(raw_q[:, j, :, :], dram["L3_q"][4 * g + 2 * s + j, :, :, :]).then_inc(q_loaded, 16)

                def load_o(u):
                    wait(sp, o_ready, u)
                    sp.dma_start(raw_o[:, :, :], dram["L3_o"][u, :, :, :]).then_inc(o_loaded, 16)

                sp.dma_start(rope[:, :, :], dram["L3_rope"]).then_inc(rope_loaded, 16)
                sp.dma_start(mask[:, :, :], dram["L3_mask"]).then_inc(mask_loaded, 16)
                load_q(1, 0, 1)

                def turn(g, first, last):
                    load_o(2 * g)
                    if not last:
                        sp.wait_ge(kv_ready, g + 1)
                        sp.dma_start(raw_kv[:, :, :, :], dram["L3_kv"][g + 1, :, :, :, :]).then_inc(kv_loaded, 16)
                        load_q(2 * g + 2, g + 1, 0)
                    load_o(2 * g + 1)
                    if not last:
                        load_q(2 * g + 3, g + 1, 1)

                turns(turn, sp)

            @block.gpsimd
            def _(pool):
                flat = lambda t: t[:, :, :].rearrange("p a b -> p (a b)")
                flat4 = lambda t: t[:, :, :, :].rearrange("p a b c -> p (a b c)")

                def split_low(n, raw, w, hi, ready):
                    f = flat4 if len(raw.shape) == 4 else flat
                    pool.wait_ge(hi, n + 1)
                    pool.tensor_tensor(f(w[1]), f(raw), as_f32(f(w[0])), ALU.subtract).then_inc(ready, 1)

                def rotate(n, ring, dst, free):
                    wait(pool, scores_full, free)
                    pool.wait_ge(ring_drained, ring + n + 1)
                    pool.tensor_tensor(dst[:, n * HALF:(n + 1) * HALF], cosine[n][:, :], cross[n][:, :], ALU.add
                                       ).then_inc(rotated, 1)

                def rotate_both(ring, dst, free):
                    rotate(0, ring, dst, free)
                    rotate(1, ring, dst, free)

                rotate_both(0, q[0], 0)
                rotate_both(2, k, 0)
                split_low(1, raw_q, w_q[1], q_hi, q_ready)

                def turn(g, first, last):
                    h = G * g
                    rotate_both(ring_at(g, "q1"), q[1], 2 * h)
                    if not last:
                        split_low(g + 1, raw_kv, w_kv, kv_hi, kv_ready)
                    rotate_both(ring_at(g, "q2"), q[0], 2 * h + 2)
                    split_low(2 * g, raw_o, w_o, o_hi, o_ready)
                    if not last:
                        split_low(2 * g + 2, raw_q, w_q[0], q_hi, q_ready)
                    rotate_both(ring_at(g, "q3"), q[1], 2 * h + 4)
                    if not last:
                        rotate_both(ring_at(g, "q0"), q[0], 2 * h + 6)
                        rotate_both(ring_at(g, "k"), k, 2 * h + 8)
                    split_low(2 * g + 1, raw_o, w_o, o_hi, o_ready)
                    if not last:
                        split_low(2 * g + 3, raw_q, w_q[1], q_hi, q_ready)

                turns(turn, pool)

            @block.tensor
            def _(pe):
                def project(n, at, bk, w, n_w, src):
                    wait(pe, ring_drained, at + n - 3)
                    part = slice(n * HALF, (n + 1) * HALF)
                    for c in range(DC):
                        mm = product(pe, bank[bk + n][:, :], [w[s][:, n_w, c, :] for s in range(2)],
                                     [src[s][:, c, part] for s in range(2)], c == 0, c == DC - 1)
                    mm.then_inc(ring_full, 1)

                def project_both(at, bk, w, n_w, src):
                    project(0, at, bk, w, n_w, src)
                    project(1, at, bk, w, n_w, src)

                def transpose_values(g):
                    pe.wait_ge(ring_drained, ring_at(g, "v") + 2)
                    wait(pe, h_drained, 2 * G * g)
                    for half in range(2):
                        for y in range(BH):
                            b = half * BH + y
                            mm = pe.transpose(bank[6 + half][:, y * P:(y + 1) * P], vt[:, b * P:(b + 1) * P],
                                              core.ident[:, :])
                        mm.then_inc(v_full, 1)

                def scores(h, j, needed):
                    pe.wait_ge(rotated, needed)
                    wait(pe, scores_read, 2 * h)
                    for half in range(2):
                        for y in range(BH):
                            t = slice((half * BH + y) * P, (half * BH + y + 1) * P)
                            mm = product(pe, bank[4 + half][:, y * P:(y + 1) * P], [q[j % 2][:, t]], [k[:, t]], True,
                                         True)
                        mm.then_inc(scores_full, 1)

                def transpose_probs(h, j):
                    pe.wait_ge(probs_ready, h + 1)
                    wait(pe, h_drained, 2 * h)
                    for half in range(2):
                        for y in range(BH):
                            mm = pe.transpose(bank[6 + half][:, y * P:(y + 1) * P], probs[j % 2][:, half * BH + y, :],
                                              core.ident[:, :])
                        mm.then_inc(t_full, 1)

                def weigh_values(h):
                    for half in range(2):
                        pe.wait_ge((t_act, t_dve)[half], h + 1)
                        for y in range(BH):
                            b = half * BH + y
                            mm = product(pe, bank[6 + half][:, y * P:(y + 1) * P], [v[:, b, :]], [probs_t[:, b, :]],
                                         True, True)
                        mm.then_inc(h_full, 1)

                def project_out(u, s, at, batches, first_bank):
                    pe.wait_ge(o_ready, u + 1)
                    pe.wait_ge(h_drained, 4 * u + 4)
                    for n, b in enumerate(batches):
                        wait(pe, ring_drained, at + n - 3)
                        for j in range(2):
                            mm = product(pe, bank[(first_bank + n) % 4][:, :],
                                         [heads[s][t][:, j, b * P:(b + 1) * P] for t in range(2)],
                                         [w_o[t][:, j, :] for t in range(2)], j == 0, j == 1)
                        mm.then_inc(ring_full, 1)

                pe.wait_ge(q_ready, 1)
                project_both(0, 0, w_q[0], 0, qin)
                pe.wait_ge(kv_ready, 1)
                pe.wait_ge(core.ctx2_split, DC)
                project_both(2, 2, w_kv, 0, cin)

                def step(h, j, needed, at, bk, w, n_w, project_next, weigh_last):
                    scores(h, j, needed)
                    if weigh_last:
                        transpose_probs(h - 1, j + 3)
                    if project_next:
                        project(0, at, bk, w, n_w, qin)
                    if weigh_last:
                        weigh_values(h - 1)
                    if project_next:
                        project(1, at, bk, w, n_w, qin)

                def turn(g, first, last):
                    step(G * g, 0, rope_at(g, "q1"), ring_at(g, "q1"), 0, w_q[0], 1, True, not first)
                    for n in range(2):
                        project(n, ring_at(g, "v"), 2, w_kv, 1, cin)
                    if not first:
                        project_out(2 * g - 1, 1, ring_at(g, "out23a"), range(BH), 0)
                    transpose_values(g)
                    pe.wait_ge(q_ready, 2 * g + 2)
                    pe.wait_ge(v_act, g + 1)
                    pe.wait_ge(v_dve, g + 1)
                    step(G * g + 1, 1, rope_at(g, "q1") + 2, ring_at(g, "q2"), 0, w_q[1], 0, True, True)
                    if not first:
                        project_out(2 * g - 1, 1, ring_at(g, "out23b"), range(BH, B), 2)
                    step(G * g + 2, 2, rope_at(g, "q2") + 2, ring_at(g, "q3"), 2, w_q[1], 1, True, True)
                    project_out(2 * g, 0, ring_at(g, "out01a"), range(BH), 0)
                    if not last:
                        pe.wait_ge(q_ready, 2 * g + 3)
                    step(G * g + 3, 3, rope_at(g, "q3") + 2, ring_at(g, "q0"), 0, w_q[0], 0, not last, True)
                    if not last:
                        pe.wait_ge(kv_ready, g + 2)
                        project_both(ring_at(g, "k"), 2, w_kv, 0, cin)
                    project_out(2 * g, 0, ring_at(g, "out01b") - (4 if last else 0), range(BH, B), 0)

                turns(turn, pe)
                transpose_probs(G * N - 1, 3)
                weigh_values(G * N - 1)
                project_out(2 * N - 1, 1, OUT_LAST + 4, range(B), 0)

            @block.scalar
            def _(act):
                def exps(h, j):
                    act.wait_ge(top_ready, h + 1)
                    wait(act, inv_done, h)
                    for b in range(B):
                        act.activation(probs[j % 2][:, b, :], probs[j % 2][:, b, :], ACT.Exp, bias=top[:, b:b + 1],
                                       accum_out=row_sum[:, b:b + 1]).then_inc(exp_done, 1)

                def split_high(n, raw, w, loaded, per, hi, free):
                    act.wait_ge(loaded, per * (n + 1))
                    wait(act, ring_full, free)
                    sl = tuple(slice(None) for _ in raw.shape)
                    act.activation(w[0][sl], raw[sl], ACT.Copy).then_inc(hi, 1)

                def copy_probs(h):
                    act.wait_ge(t_full, 2 * h + 1)
                    act.activation(probs_t[:, 0:BH, :], bank[6][:, :].rearrange("p (b n) -> p b n", b=BH), ACT.Copy
                                   ).then_inc(t_act, 1)

                def heads_high(h, j):
                    for half in range(2):
                        act.wait_ge(h_full, 2 * h + half + 1)
                        act.activation(heads[j // 2][0][:, j % 2, half * HALF:(half + 1) * HALF], bank[6 + half][:, :],
                                       ACT.Copy).then_inc(h_hi, 1)

                split_high(1, raw_q, w_q[1], q_loaded, 32, q_hi, 0)

                def turn(g, first, last):
                    h = G * g
                    if not first:
                        copy_probs(h - 1)
                    exps(h, 0)
                    if not first:
                        wait(act, ring_full, ring_at(g - 1, "out01b") + 4)
                        heads_high(h - 1, 3)
                    if not last:
                        split_high(g + 1, raw_kv, w_kv, kv_loaded, 16, kv_hi, ring_at(g, "v") + 2)
                        split_high(2 * g + 2, raw_q, w_q[0], q_loaded, 32, q_hi, ring_at(g, "q1") + 2)
                    act.wait_ge(v_full, 2 * g + 1)
                    act.activation(v[:, 0:BH, :], bank[6][:, :].rearrange("p (b n) -> p b n", b=BH), ACT.Copy
                                   ).then_inc(v_act, 1)
                    copy_probs(h)
                    exps(h + 1, 1)
                    heads_high(h, 0)
                    split_high(2 * g, raw_o, w_o, o_loaded, 16, o_hi, 0 if first else ring_at(g, "out23b") + 4)
                    copy_probs(h + 1)
                    exps(h + 2, 2)
                    heads_high(h + 1, 1)
                    copy_probs(h + 2)
                    exps(h + 3, 3)
                    heads_high(h + 2, 2)
                    if not last:
                        split_high(2 * g + 3, raw_q, w_q[1], q_loaded, 32, q_hi, ring_at(g, "q3") + 2)
                    split_high(2 * g + 1, raw_o, w_o, o_loaded, 16, o_hi,
                               ring_at(g, "out01b") + 4 - (4 if last else 0))

                turns(turn, act)
                copy_probs(G * N - 1)
                heads_high(G * N - 1, 3)

            @block.vector
            def _(dve):
                def mask_scores(h, j):
                    wait(dve, t_full, 2 * (h - 1))
                    for half in range(2):
                        part = slice(half * BH, (half + 1) * BH)
                        dve.wait_ge(scores_full, 2 * h + half + 1)
                        dve.scalar_tensor_tensor(probs[j % 2][:, part, :],
                                                 bank[4 + half][:, :].rearrange("p (b n) -> p b n", b=BH), SCALE,
                                                 mask[:, part, :], ALU.mult, ALU.add).then_inc(scores_read, 1)
                    dve.wait_ge(scores_read, 2 * h + 2)
                    wait(dve, exp_done, B * h)
                    dve.tensor_reduce(top[:, :], probs[j % 2][:, :, :], AX.X, ALU.max).then_inc(top_raw, 1)
                    dve.wait_ge(top_raw, h + 1)
                    dve.tensor_scalar(top[:, :], top[:, :], -1.0, None, ALU.mult).then_inc(top_ready, 1)

                def normalise(h, j):
                    dve.wait_ge(exp_done, B * (h + 1))
                    dve.reciprocal(inv_sum[:, :], row_sum[:, :]).then_inc(inv_done, 1)
                    dve.wait_ge(inv_done, h + 1)
                    dve.tensor_tensor(probs[j % 2][:, :, :], probs[j % 2][:, :, :],
                                      inv_sum[:, :].rearrange("p (b o) -> p b o", o=1).to_broadcast([P, B, P]),
                                      ALU.mult).then_inc(probs_ready, 1)

                def rotate(n, ring, at, bk):
                    table = lambda part, n: rope[part, n:n + 1, :].to_broadcast([part.stop - part.start, BH, P])
                    low, high, whole = slice(0, HP), slice(HP, P), slice(0, P)
                    src = bank[bk + n][:, :].rearrange("p (b t) -> p b t", b=BH)
                    cos, sine = (t[n][:, :].rearrange("p (b t) -> p b t", b=BH) for t in (cosine, cross))
                    dve.wait_ge(ring_full, ring + n + 1)
                    wait(dve, rotated, at + n - 1)
                    dve.tensor_tensor(cos, src, table(whole, 0), ALU.mult)
                    dve.tensor_tensor(sine[high, :, :], src[low, :, :], table(low, 1), ALU.mult)
                    dve.tensor_tensor(sine[low, :, :], src[high, :, :], table(high, 1), ALU.mult
                                      ).then_inc(ring_drained, 1)

                def copy_probs(h):
                    dve.wait_ge(t_full, 2 * h + 2)
                    dve.tensor_copy(probs_t[:, BH:B, :], bank[7][:, :].rearrange("p (b n) -> p b n", b=BH)
                                    ).then_inc(t_dve, 1)

                def heads_low(h, j):
                    for half in range(2):
                        part = slice(half * HALF, (half + 1) * HALF)
                        hi, lo = heads[j // 2]
                        dve.wait_ge(h_hi, 2 * h + half + 1)
                        dve.tensor_tensor(lo[:, j % 2, part], bank[6 + half][:, :], as_f32(hi[:, j % 2, part]),
                                          ALU.subtract).then_inc(h_drained, 1)

                def add_out(at, batches, first_bank, final=False):
                    for n, b in enumerate(batches):
                        dve.wait_ge(ring_full, at + n + 1)
                        dve.tensor_tensor(x[:, b, :], x[:, b, :], bank[(first_bank + n) % 4][:, :], ALU.add
                                          ).then_inc(ring_drained, 1)
                        if final:
                            dve.wait_ge(ring_drained, at + n + 1)
                            core.statistics(dve, b)

                dve.wait_ge(rope_loaded, 16)
                for n in range(2):
                    rotate(n, 0, 0, 0)
                for n in range(2):
                    rotate(n, 2, 2, 2)
                dve.wait_ge(mask_loaded, 16)

                def step(h, j, ring, at, bk, rotate_next, weigh_last):
                    mask_scores(h, j)
                    if weigh_last:
                        copy_probs(h - 1)
                    if rotate_next:
                        rotate(0, ring, at, bk)
                    if weigh_last:
                        heads_low(h - 1, (j + 3) % 4)
                    if rotate_next:
                        rotate(1, ring, at, bk)
                    normalise(h, j)

                def turn(g, first, last):
                    step(G * g, 0, ring_at(g, "q1"), rope_at(g, "q1"), 0, True, not first)
                    for n in range(2):
                        dve.wait_ge(ring_full, ring_at(g, "v") + n + 1)
                        dve.tensor_copy(vt[:, n * HALF:(n + 1) * HALF], bank[2 + n][:, :]).then_inc(ring_drained, 1)
                    if not first:
                        add_out(ring_at(g, "out23a"), range(BH), 0)
                    dve.wait_ge(v_full, 2 * g + 2)
                    dve.tensor_copy(v[:, BH:B, :], bank[7][:, :].rearrange("p (b n) -> p b n", b=BH)
                                    ).then_inc(v_dve, 1)
                    step(G * g + 1, 1, ring_at(g, "q2"), rope_at(g, "q2"), 0, True, True)
                    if not first:
                        add_out(ring_at(g, "out23b"), range(BH, B), 2)
                    step(G * g + 2, 2, ring_at(g, "q3"), rope_at(g, "q3"), 2, True, True)
                    add_out(ring_at(g, "out01a"), range(BH), 0)
                    step(G * g + 3, 3, ring_at(g, "q0"), rope_at(g, "q0"), 0, not last, True)
                    if not last:
                        for n in range(2):
                            rotate(n, ring_at(g, "k"), rope_at(g, "k"), 2)
                    add_out(ring_at(g, "out01b") - (4 if last else 0), range(BH, B), 0)

                turns(turn, dve)
                copy_probs(G * N - 1)
                heads_low(G * N - 1, 3)
                add_out(OUT_LAST + 4, range(B), 0, True)


def build(nc, dram, out):
    ctx = ExitStack()
    with ctx:
        core = Core(nc, ctx)
        with ExitStack() as early:
            core.hold_first(early)
            l0_attention(core, dram)
            core.hold_kv(early)
            l0_ffn(core, dram)
            l1_attention(core, dram)
        l1_ffn(core, dram)
        core.free_semaphores()
        l2_attention(core, dram)
        with ExitStack() as late:
            core.hold_second(late)
            l2_ffn(core, dram)
            l3_attention(core, dram)
        l3_ffn(core, dram, out)


def laid_out(inputs):
    a = {name: np.asarray(value) for name, value in inputs.items()}
    chunks = lambda w: w.reshape(DC, P, -1).transpose(1, 0, 2)
    got = {"x": a["x"]}
    got["ctx_t"] = chunks(a["ctx_4096"].reshape(T, D).T)
    got["mask_b_q"] = a["mask_BxSxS2_bk0"].transpose(1, 0, 2)
    got["L0_xattn_position_bias"] = a["L0_xattn_position_bias"]
    got["L0_xattn_ln_weight"] = a["L0_xattn_ln_weight"].reshape(DC, P).T
    qk = np.stack([a["L0_xattn_w_q"], a["L0_xattn_w_k"]]).reshape(2, 16, 2, P, DC, P)
    got["L0_qk"] = qk.transpose(1, 2, 5, 0, 4, 3)
    got["L0_v"] = a["L0_xattn_w_v"].reshape(16, 2 * P, DC, P).transpose(0, 3, 2, 1)
    got["L0_o"] = a["L0_xattn_w_out"].T.reshape(16, 2, P, D).transpose(0, 2, 1, 3)
    got["L0f_wq"] = chunks(a["L0_ffn_Wq"].T)
    got["L0f_keys"] = a["L0_ffn_lora_keys"].T
    got["L0f_down"] = chunks(a["L0_ffn_lora_down"].transpose(1, 0, 2).reshape(D, -1))
    got["L0f_org"] = chunks(a["L0_ffn_W_org"].T)
    got["L0f_up"] = chunks(a["L0_ffn_lora_up"].reshape(-1, D))
    got["L1x_wq"] = chunks(a["L1_xattn_Wq"].reshape(D, 8, 4, 16).transpose(0, 2, 1, 3).reshape(D, D))
    got["L1x_wkv"] = chunks(np.concatenate([a["L1_xattn_Wk"], a["L1_xattn_Wv"]], axis=1))
    got["L1x_wo"] = chunks(a["L1_xattn_Wo"].reshape(8, 4, 16, D).transpose(1, 0, 2, 3).reshape(D, D))
    got["L1f_wq"] = chunks(a["L1_ffn_Wq"].T)
    got["L1f_wr"] = a["L1_ffn_Wr"].T
    got["L1f_keys"] = a["L1_ffn_aux_keys"].T
    got["L1f_values"] = chunks(a["L1_ffn_aux_values"].T)
    got["L1f_wvd"] = chunks(a["L1_ffn_Wvd"].T)
    got["L1f_wvu"] = a["L1_ffn_Wvu"].T
    got["L1f_wu1"] = chunks(a["L1_ffn_Wu1"].T)
    got["L1f_wu2"] = a["L1_ffn_Wu2"].T
    on_all = [np.broadcast_to(a[n].reshape(1), (P,)) for n in ("L1_ffn_bu2", "L1_ffn_gate_w1", "L1_ffn_gate_bias")]
    got["L1f_consts"] = np.stack([a["L1_ffn_bu1"]] + on_all, axis=1)
    got["L1f_log_rel"] = np.broadcast_to(a["L1_ffn_log_rel"], (P, 1, P))
    got["l2f_a"] = chunks(np.concatenate([a["L2_ffn_lora_A"].reshape(P, D), a["L2_ffn_W_router"]]).T)
    got["l2f_b"] = a["L2_ffn_lora_B"].transpose(0, 2, 1).reshape(P, D)
    got["l2f_base"] = chunks(a["L2_ffn_W_base"].T)
    got["l2f_bias"] = np.broadcast_to(a["L2_ffn_b_base"], (P, D))
    got["l3f_a"] = chunks(np.concatenate([a["L3_ffn_A"].reshape(P, D), a["L3_ffn_route_w"]]).T)
    got["l3f_b"] = a["L3_ffn_Bw"].transpose(0, 2, 1).reshape(P, D)
    rank = a["ctx_4096"][:, ::-1, :].reshape(B, P, DC, P).transpose(2, 0, 3, 1).reshape(L0_PAIRS, TPT, P, P)
    got["ctx_rank"] = rank.transpose(0, 2, 1, 3)
    got["L2x_taps"] = np.repeat(a["L2_xattn_conv_w"][0], 16, axis=0)
    got["L2x_affine"] = np.broadcast_to(np.concatenate([a["L2_xattn_bn_gamma"], a["L2_xattn_bn_beta"]]), (16, 2))
    got["L3_q"] = a["L3_xattn_wq"].reshape(DC, P, 32, P).transpose(2, 1, 0, 3)
    got["L3_kv"] = np.stack([a["L3_xattn_wk"], a["L3_xattn_wv"]]).reshape(2, DC, P, 8, P).transpose(3, 2, 0, 1, 4)
    got["L3_o"] = a["L3_xattn_wo"].reshape(16, 2, P, D).transpose(0, 2, 1, 3)
    got["L3_mask"] = a["mask_BxSxS2_ff0"].transpose(1, 0, 2)
    angle = np.arange(P)[None, :] * (1.0 / 10000.0 ** (np.arange(0, P, 2) / P))[:, None]
    got["L3_rope"] = np.stack([np.tile(np.cos(angle), (2, 1)), np.concatenate([np.sin(angle), -np.sin(angle)])],
                              axis=1).astype(np.float32)
    return {name: np.ascontiguousarray(value) for name, value in got.items()}


def kernel(**inputs):
    import concourse.bacc as bacc
    from concourse.bass_utils import run_bass_kernel_spmd

    nc = bacc.Bacc("TRN2", target_bir_lowering=False, num_devices=1)
    arrays = laid_out(inputs)
    dram = {name: nc.dram_tensor(name + "_dram", a.shape, mybir.dt.from_np(a.dtype), kind="ExternalInput").ap()
            for name, a in arrays.items()}
    out = nc.dram_tensor("out_dram", (B, P, D), F32, kind="ExternalOutput").ap()
    build(nc, dram, out)
    result = run_bass_kernel_spmd(nc, [{name + "_dram": a for name, a in arrays.items()}], core_ids=[0])
    return result.results[0]["out_dram"]
```
